# Optimizing a Trainium2 kernel written in Bass

```python
import numpy as np
import jax
import jax.numpy as jnp

def _softmax(x, axis=-1):
    return jax.nn.softmax(x, axis=axis)

def _gelu(x):
    return jax.nn.gelu(x, approximate=True)

def _silu(x):
    return jax.nn.silu(x)

def _sigmoid(x):
    return jax.nn.sigmoid(x)

def _layernorm(x, axis=-1, eps=1e-05):
    m = jnp.mean(x, axis=axis, keepdims=True)
    v = jnp.var(x, axis=axis, keepdims=True)
    return (x - m) / jnp.sqrt(v + eps)

def _scatter_add(tgt, idx, src, axis=0):
    return tgt.at[idx].add(src)

def _segment_sum(src, seg, n):
    return jax.ops.segment_sum(src, seg, n)
kernel_name = 'mk_adaln_d2_jaxref_r8_91f52a'

def setup_inputs(seed: int=0):
    np.random.seed(seed)
    _w = jnp.asarray

    def _L0_attn_setup():
        import jax, jax.numpy as jnp
        import numpy as np
        from jax import lax
        HID = 128
        NH = 16
        NKV = 4
        HD = 64
        SPLIT = 64
        KS = 3

        def _dynamic_conv(x, w_kgen, b_kgen, w_conv, b_conv):
            context = x.mean(axis=1)
            dyn = context @ w_kgen.T + b_kgen
            gate = jax.nn.sigmoid(dyn).mean(axis=1)
            x_t = x.transpose(0, 2, 1)
            y = lax.conv_general_dilated(x_t, w_conv, window_strides=(1,), padding=[(KS // 2, KS // 2)], feature_group_count=HID, dimension_numbers=('NCH', 'OIH', 'NCH'))
            y = (y + b_conv[None, :, None]) * gate[:, None, None]
            return y.transpose(0, 2, 1)

        def _fixed_split_attention(x, w_q, w_k, w_v, w_o):
            B, S, _ = x.shape
            q = (x @ w_q.T).reshape(B, S, NH, HD).transpose(0, 2, 1, 3)
            k = (x @ w_k.T).reshape(B, S, NKV, HD).transpose(0, 2, 1, 3)
            v = (x @ w_v.T).reshape(B, S, NKV, HD).transpose(0, 2, 1, 3)
            n_rep = NH // NKV
            k = jnp.repeat(k, n_rep, axis=1)
            v = jnp.repeat(v, n_rep, axis=1)
            C = S // SPLIT
            kc = k.reshape(B, NH, C, SPLIT, HD)
            vc = v.reshape(B, NH, C, SPLIT, HD)
            scale = HD ** (-0.5)
            scores = jnp.einsum('bhqd,bhckd->bhcqk', q, kc) * scale
            w = jax.nn.softmax(scores.astype(jnp.float32), axis=-1).astype(q.dtype)
            chunk_out = jnp.einsum('bhcqk,bhckd->bhcqd', w, vc)
            sum_w = w.sum(axis=-1, keepdims=True)
            combined = (chunk_out * sum_w).sum(axis=2)
            total = sum_w.sum(axis=2)
            out = combined / (total + 1e-09)
            out = out.transpose(0, 2, 1, 3).reshape(B, S, NH * HD)
            return out @ w_o.T
        key = jax.random.key(seed)
        ks = jax.random.split(key, 9)
        s = 0.02
        return {'hidden_states': jax.random.normal(ks[0], (2, 256, HID), jnp.float32), 'w_q': jax.random.normal(ks[1], (NH * HD, HID), jnp.float32) * s, 'w_k': jax.random.normal(ks[2], (NKV * HD, HID), jnp.float32) * s, 'w_v': jax.random.normal(ks[3], (NKV * HD, HID), jnp.float32) * s, 'w_o': jax.random.normal(ks[4], (HID, NH * HD), jnp.float32) * s, 'w_kgen': jax.random.normal(ks[5], (KS, HID), jnp.float32) * s, 'b_kgen': jnp.zeros((KS,), jnp.float32), 'w_conv': jax.random.normal(ks[6], (HID, 1, KS), jnp.float32) * s, 'b_conv': jnp.zeros((HID,), jnp.float32)}
    _L0_attn_in = _L0_attn_setup()

    def _L0_ffn_setup():
        import jax, jax.numpy as jnp
        import numpy as np
        B, N, D = (4, 512, 128)
        E, S, F = (16, 64, 256)
        DO = 128
        EPS = 1e-05

        def _layernorm(x, g, b):
            mu = jnp.mean(x, axis=-1, keepdims=True)
            var = jnp.mean(jnp.square(x - mu), axis=-1, keepdims=True)
            return (x - mu) * jax.lax.rsqrt(var + EPS) * g + b
        key = jax.random.key(seed)
        ks = jax.random.split(key, 8)
        d = {'x': jax.random.normal(ks[0], (B, N, D), dtype=jnp.float32), 'norm_g': jnp.ones((D,), jnp.float32), 'norm_b': jnp.zeros((D,), jnp.float32), 'slot_g': jnp.ones((D,), jnp.float32), 'slot_b': jnp.zeros((D,), jnp.float32), 'scale': jnp.ones((1,), jnp.float32), 'slot_embeds': jax.random.normal(ks[1], (E, S, D), jnp.float32) / np.sqrt(D), 'Wg': jax.random.normal(ks[2], (E, D, F), jnp.float32) * np.sqrt(2.0 / (D + F)), 'bg': jnp.zeros((E, F), jnp.float32), 'Wu': jax.random.normal(ks[3], (E, D, F), jnp.float32) * np.sqrt(2.0 / (D + F)), 'bu': jnp.zeros((E, F), jnp.float32), 'Wd': jax.random.normal(ks[4], (E, F, DO), jnp.float32) * np.sqrt(2.0 / (F + DO)), 'bd': jnp.zeros((E, DO), jnp.float32)}
        return d
    _L0_ffn_in = _L0_ffn_setup()
    _L0_c = _w((lambda *s: np.random.randn(*s).astype(np.float32) * 0.05)(2, 128))
    _L0_wmod = _w((lambda *s: np.random.randn(*s).astype(np.float32) * 0.05)(128, 6 * 128) * 128 ** (-0.5))

    def _L1_attn_setup():
        import jax, jax.numpy as jnp
        import numpy as np
        EPS = 1e-10

        def scores_dtype(x):
            return x.dtype
        key = jax.random.key(seed)
        ks = jax.random.split(key, 5)
        B, S, D, N, H = (2, 256, 128, 16, 64)
        init_range = 0.02
        residual = jax.random.normal(ks[0], (B, S, D), dtype=jnp.float32)
        W_key = jax.random.normal(ks[1], (N, D, H), dtype=jnp.float32) * init_range
        W_query = jax.random.normal(ks[2], (N, D, H), dtype=jnp.float32) * init_range
        W_values = jax.random.normal(ks[3], (N, D, H), dtype=jnp.float32) * init_range
        W_output = jax.random.normal(ks[4], (N, H, D), dtype=jnp.float32) * init_range
        return {'residual': residual, 'W_key': W_key, 'W_query': W_query, 'W_values': W_values, 'W_output': W_output, 'Bias_key': jnp.zeros((N, H), jnp.float32), 'Bias_query': jnp.zeros((N, H), jnp.float32), 'Bias_values': jnp.zeros((N, H), jnp.float32), 'Bias_output': jnp.zeros((D,), jnp.float32)}
    _L1_attn_in = _L1_attn_setup()

    def _L1_ffn_setup():
        import jax, jax.numpy as jnp
        import numpy as np
        B, S, H = (2, 256, 128)
        N, F, SF, K = (16, 128, 512, 1)
        key = jax.random.key(seed)
        ks = jax.random.split(key, 7)
        std = 0.02
        return {'hidden_states': jax.random.normal(ks[0], (B, S, H), dtype=jnp.float32), 'router_w': jax.random.normal(ks[1], (N, H), dtype=jnp.float32) * std, 'gate_up_proj': jax.random.normal(ks[2], (N, H, 2 * F), dtype=jnp.float32) * std, 'down_proj': jax.random.normal(ks[3], (N, F, H), dtype=jnp.float32) * std, 'shared_gate_w': jax.random.normal(ks[4], (SF, H), dtype=jnp.float32) * std, 'shared_up_w': jax.random.normal(ks[5], (SF, H), dtype=jnp.float32) * std, 'shared_down_w': jax.random.normal(ks[6], (H, SF), dtype=jnp.float32) * std}
    _L1_ffn_in = _L1_ffn_setup()
    _L1_c = _w((lambda *s: np.random.randn(*s).astype(np.float32) * 0.05)(2, 128))
    _L1_wmod = _w((lambda *s: np.random.randn(*s).astype(np.float32) * 0.05)(128, 6 * 128) * 128 ** (-0.5))
    _d = {'L0_attn_hidden_states': _L0_attn_in['hidden_states'], 'L0_attn_w_q': _L0_attn_in['w_q'], 'L0_attn_w_k': _L0_attn_in['w_k'], 'L0_attn_w_v': _L0_attn_in['w_v'], 'L0_attn_w_o': _L0_attn_in['w_o'], 'L0_attn_w_kgen': _L0_attn_in['w_kgen'], 'L0_attn_b_kgen': _L0_attn_in['b_kgen'], 'L0_attn_w_conv': _L0_attn_in['w_conv'], 'L0_attn_b_conv': _L0_attn_in['b_conv'], 'L0_ffn_norm_g': _L0_ffn_in['norm_g'], 'L0_ffn_norm_b': _L0_ffn_in['norm_b'], 'L0_ffn_slot_g': _L0_ffn_in['slot_g'], 'L0_ffn_slot_b': _L0_ffn_in['slot_b'], 'L0_ffn_scale': _L0_ffn_in['scale'], 'L0_ffn_slot_embeds': _L0_ffn_in['slot_embeds'], 'L0_ffn_Wg': _L0_ffn_in['Wg'], 'L0_ffn_bg': _L0_ffn_in['bg'], 'L0_ffn_Wu': _L0_ffn_in['Wu'], 'L0_ffn_bu': _L0_ffn_in['bu'], 'L0_ffn_Wd': _L0_ffn_in['Wd'], 'L0_ffn_bd': _L0_ffn_in['bd'], 'L0_c': _L0_c, 'L0_wmod': _L0_wmod, 'L1_attn_W_key': _L1_attn_in['W_key'], 'L1_attn_W_query': _L1_attn_in['W_query'], 'L1_attn_W_values': _L1_attn_in['W_values'], 'L1_attn_W_output': _L1_attn_in['W_output'], 'L1_attn_Bias_key': _L1_attn_in['Bias_key'], 'L1_attn_Bias_query': _L1_attn_in['Bias_query'], 'L1_attn_Bias_values': _L1_attn_in['Bias_values'], 'L1_attn_Bias_output': _L1_attn_in['Bias_output'], 'L1_ffn_router_w': _L1_ffn_in['router_w'], 'L1_ffn_gate_up_proj': _L1_ffn_in['gate_up_proj'], 'L1_ffn_down_proj': _L1_ffn_in['down_proj'], 'L1_ffn_shared_gate_w': _L1_ffn_in['shared_gate_w'], 'L1_ffn_shared_up_w': _L1_ffn_in['shared_up_w'], 'L1_ffn_shared_down_w': _L1_ffn_in['shared_down_w'], 'L1_c': _L1_c, 'L1_wmod': _L1_wmod}
    _x0 = _d['L0_attn_hidden_states']
    _d['L0_attn_hidden_states'] = jax.random.normal(jax.random.fold_in(jax.random.key(seed), 1), (2, 1024, 128), dtype=_x0.dtype)
    del _x0
    return _d

def reference(L0_attn_hidden_states, L0_attn_w_q, L0_attn_w_k, L0_attn_w_v, L0_attn_w_o, L0_attn_w_kgen, L0_attn_b_kgen, L0_attn_w_conv, L0_attn_b_conv, L0_ffn_norm_g, L0_ffn_norm_b, L0_ffn_slot_g, L0_ffn_slot_b, L0_ffn_scale, L0_ffn_slot_embeds, L0_ffn_Wg, L0_ffn_bg, L0_ffn_Wu, L0_ffn_bu, L0_ffn_Wd, L0_ffn_bd, L0_c, L0_wmod, L1_attn_W_key, L1_attn_W_query, L1_attn_W_values, L1_attn_W_output, L1_attn_Bias_key, L1_attn_Bias_query, L1_attn_Bias_values, L1_attn_Bias_output, L1_ffn_router_w, L1_ffn_gate_up_proj, L1_ffn_down_proj, L1_ffn_shared_gate_w, L1_ffn_shared_up_w, L1_ffn_shared_down_w, L1_c, L1_wmod):

    def _L0_attn_ref(hidden_states, w_q, w_k, w_v, w_o, w_kgen, b_kgen, w_conv, b_conv):
        import jax, jax.numpy as jnp
        import numpy as np
        from jax import lax
        HID = 128
        NH = 16
        NKV = 4
        HD = 64
        SPLIT = 64
        KS = 3

        def _dynamic_conv(x, w_kgen, b_kgen, w_conv, b_conv):
            context = x.mean(axis=1)
            dyn = context @ w_kgen.T + b_kgen
            gate = jax.nn.sigmoid(dyn).mean(axis=1)
            x_t = x.transpose(0, 2, 1)
            y = lax.conv_general_dilated(x_t, w_conv, window_strides=(1,), padding=[(KS // 2, KS // 2)], feature_group_count=HID, dimension_numbers=('NCH', 'OIH', 'NCH'))
            y = (y + b_conv[None, :, None]) * gate[:, None, None]
            return y.transpose(0, 2, 1)

        def _fixed_split_attention(x, w_q, w_k, w_v, w_o):
            B, S, _ = x.shape
            q = (x @ w_q.T).reshape(B, S, NH, HD).transpose(0, 2, 1, 3)
            k = (x @ w_k.T).reshape(B, S, NKV, HD).transpose(0, 2, 1, 3)
            v = (x @ w_v.T).reshape(B, S, NKV, HD).transpose(0, 2, 1, 3)
            n_rep = NH // NKV
            k = jnp.repeat(k, n_rep, axis=1)
            v = jnp.repeat(v, n_rep, axis=1)
            C = S // SPLIT
            kc = k.reshape(B, NH, C, SPLIT, HD)
            vc = v.reshape(B, NH, C, SPLIT, HD)
            scale = HD ** (-0.5)
            scores = jnp.einsum('bhqd,bhckd->bhcqk', q, kc) * scale
            w = jax.nn.softmax(scores.astype(jnp.float32), axis=-1).astype(q.dtype)
            chunk_out = jnp.einsum('bhcqk,bhckd->bhcqd', w, vc)
            sum_w = w.sum(axis=-1, keepdims=True)
            combined = (chunk_out * sum_w).sum(axis=2)
            total = sum_w.sum(axis=2)
            out = combined / (total + 1e-09)
            out = out.transpose(0, 2, 1, 3).reshape(B, S, NH * HD)
            return out @ w_o.T
        h = _dynamic_conv(hidden_states, w_kgen, b_kgen, w_conv, b_conv)
        return _fixed_split_attention(h, w_q, w_k, w_v, w_o)

    def _L0_ffn_ref(x, norm_g, norm_b, slot_g, slot_b, scale, slot_embeds, Wg, bg, Wu, bu, Wd, bd):
        import jax, jax.numpy as jnp
        import numpy as np
        B, N, D = (4, 512, 128)
        E, S, F = (16, 64, 256)
        DO = 128
        EPS = 1e-05

        def _layernorm(x, g, b):
            mu = jnp.mean(x, axis=-1, keepdims=True)
            var = jnp.mean(jnp.square(x - mu), axis=-1, keepdims=True)
            return (x - mu) * jax.lax.rsqrt(var + EPS) * g + b
        x = _layernorm(x, norm_g, norm_b)
        se = _layernorm(slot_embeds, slot_g, slot_b) * scale
        logits = jnp.einsum('bnd,esd->bnes', x, se)
        dispatch = jax.nn.softmax(logits, axis=1)
        combine = jax.nn.softmax(logits.reshape(x.shape[0], x.shape[1], -1), axis=-1)
        slots = jnp.einsum('bnd,bnes->besd', x, dispatch)
        gate = jax.nn.gelu(jnp.einsum('besd,edf->besf', slots, Wg) + bg[None, :, None, :], approximate=False)
        up = jnp.einsum('besd,edf->besf', slots, Wu) + bu[None, :, None, :]
        eout = jnp.einsum('besf,efo->beso', gate * up, Wd) + bd[None, :, None, :]
        eout = eout.reshape(eout.shape[0], -1, eout.shape[-1])
        return jnp.einsum('bns,bso->bno', combine, eout)

    def _L1_attn_ref(residual, W_key, W_query, W_values, W_output, Bias_key, Bias_query, Bias_values, Bias_output):
        import jax, jax.numpy as jnp
        import numpy as np
        EPS = 1e-10

        def scores_dtype(x):
            return x.dtype
        B, S, D = residual.shape
        N, _, H = W_key.shape
        keys = jnp.einsum('bse,neh->bsnh', residual, W_key) + Bias_key
        queries = jnp.einsum('bse,neh->bsnh', residual, W_query) + Bias_query
        values = jnp.einsum('bse,neh->bsnh', residual, W_values) + Bias_values
        scores = jnp.einsum('bknh,bqnh->bnqk', keys, queries) / jnp.sqrt(jnp.asarray(H, scores_dtype(residual)))
        q_idx = jnp.arange(S)[:, None]
        k_idx = jnp.arange(S)[None, :]
        causal_mask = q_idx < k_idx
        scores = jnp.where(causal_mask[None, None, :, :], jnp.asarray(EPS, scores.dtype), scores)
        probs = jax.nn.softmax(scores, axis=3)
        weighted = jnp.einsum('bnqk,bknh->bqnh', probs, values)
        out = jnp.einsum('bqnh,nhe->bqe', weighted, W_output) + Bias_output
        return out

    def _L1_ffn_ref(hidden_states, router_w, gate_up_proj, down_proj, shared_gate_w, shared_up_w, shared_down_w):
        import jax, jax.numpy as jnp
        import numpy as np
        B, S, H = (2, 256, 128)
        N, F, SF, K = (16, 128, 512, 1)
        b, s, h = hidden_states.shape
        hidden = hidden_states.reshape(-1, h)
        t = hidden.shape[0]
        logits = hidden @ router_w.T
        top_vals, top_idx = jax.lax.top_k(logits, K)
        scores = jnp.full_like(logits, -jnp.inf)
        scores = scores.at[jnp.arange(t)[:, None], top_idx].set(top_vals)
        scores = jax.nn.sigmoid(scores.astype(jnp.float32)).astype(hidden.dtype)
        routed_in = hidden[None, :, :] * scores.T[:, :, None]
        gate_up = jnp.einsum('nth,nhf->ntf', routed_in, gate_up_proj)
        gate, up = jnp.split(gate_up, 2, axis=-1)
        routed_out = jnp.einsum('ntf,nfh->nth', up * jax.nn.silu(gate), down_proj)
        expert_sum = routed_out.sum(axis=0)
        shared = jax.nn.silu(hidden @ shared_gate_w.T) * (hidden @ shared_up_w.T) @ shared_down_w.T
        return (shared + expert_sum).reshape(b, s, h)
    x = L0_attn_hidden_states
    mod = (_silu(L0_c) @ L0_wmod).reshape(L0_c.shape[0], 6, 1, -1)
    sa, ca, ga, sb, cb, gb = (mod[:, 0], mod[:, 1], mod[:, 2], mod[:, 3], mod[:, 4], mod[:, 5])
    ga = (2 * (ga >= 0) - 1) * jnp.maximum(jnp.abs(ga), 0.25)
    gb = (2 * (gb >= 0) - 1) * jnp.maximum(jnp.abs(gb), 0.25)
    h = _layernorm(x, axis=-1) * (1 + ca) + sa
    x = x + ga * _L0_attn_ref(h, L0_attn_w_q, L0_attn_w_k, L0_attn_w_v, L0_attn_w_o, L0_attn_w_kgen, L0_attn_b_kgen, L0_attn_w_conv, L0_attn_b_conv)
    h = _layernorm(x, axis=-1) * (1 + cb) + sb
    x = x + gb * _L0_ffn_ref(h, L0_ffn_norm_g, L0_ffn_norm_b, L0_ffn_slot_g, L0_ffn_slot_b, L0_ffn_scale, L0_ffn_slot_embeds, L0_ffn_Wg, L0_ffn_bg, L0_ffn_Wu, L0_ffn_bu, L0_ffn_Wd, L0_ffn_bd)
    mod = (_silu(L1_c) @ L1_wmod).reshape(L1_c.shape[0], 6, 1, -1)
    sa, ca, ga, sb, cb, gb = (mod[:, 0], mod[:, 1], mod[:, 2], mod[:, 3], mod[:, 4], mod[:, 5])
    ga = (2 * (ga >= 0) - 1) * jnp.maximum(jnp.abs(ga), 0.25)
    gb = (2 * (gb >= 0) - 1) * jnp.maximum(jnp.abs(gb), 0.25)
    h = _layernorm(x, axis=-1) * (1 + ca) + sa
    x = x + ga * _L1_attn_ref(h, L1_attn_W_key, L1_attn_W_query, L1_attn_W_values, L1_attn_W_output, L1_attn_Bias_key, L1_attn_Bias_query, L1_attn_Bias_values, L1_attn_Bias_output)
    h = _layernorm(x, axis=-1) * (1 + cb) + sb
    x = x + gb * _L1_ffn_ref(h, L1_ffn_router_w, L1_ffn_gate_up_proj, L1_ffn_down_proj, L1_ffn_shared_gate_w, L1_ffn_shared_up_w, L1_ffn_shared_down_w)
    return x

_drawn_inputs = setup_inputs


def setup_inputs(seed=0):
    import zlib

    import numpy as np

    out = dict(_drawn_inputs(seed))
    spreads = {'L0_attn_b_kgen': (0.0, 0.8),
     'L0_attn_b_conv': (0.0, 0.8),
     'L0_ffn_norm_g': (1.0, 0.2),
     'L0_ffn_norm_b': (0.0, 0.287),
     'L0_ffn_slot_g': (1.0, 0.2),
     'L0_ffn_slot_b': (0.0, 0.442),
     'L0_ffn_bg': (0.0, 0.576),
     'L0_ffn_bu': (0.0, 0.595),
     'L0_ffn_bd': (0.0, 0.35),
     'L1_attn_Bias_key': (0.0, 0.8),
     'L1_attn_Bias_query': (0.0, 0.8),
     'L1_attn_Bias_values': (0.0, 0.519),
     'L1_attn_Bias_output': (0.0, 0.319)}
    factors = {'L0_attn_w_q': 8.0,
     'L0_attn_w_k': 8.0,
     'L0_attn_w_v': 8.0,
     'L0_attn_w_o': 8.0,
     'L0_attn_w_kgen': 8.0,
     'L0_attn_w_conv': 8.0,
     'L1_attn_W_key': 8.0,
     'L1_attn_W_query': 8.0,
     'L1_attn_W_values': 8.0,
     'L1_attn_W_output': 3.379,
     'L1_ffn_router_w': 8.0,
     'L1_ffn_gate_up_proj': 8.0,
     'L1_ffn_down_proj': 8.0,
     'L1_ffn_shared_gate_w': 8.0,
     'L1_ffn_shared_up_w': 8.0,
     'L1_ffn_shared_down_w': 8.0}
    for name, (base, spread) in spreads.items():
        noise = np.random.default_rng([zlib.crc32(name.encode()), seed]).standard_normal(out[name].shape)
        drawn = base * np.exp(spread * noise) if base else spread * noise
        out[name] = jnp.asarray(drawn.astype(out[name].dtype))
    for name, factor in factors.items():
        out[name] = (out[name] * factor).astype(out[name].dtype)
    return out
```

```python
from contextlib import ExitStack

import concourse.bass as bass
from concourse import mybir
from concourse.alu_op_type import AluOpType as ALU

F32 = mybir.dt.float32
FR = mybir.dt.float32r
BF16 = mybir.dt.bfloat16
I32 = mybir.dt.int32
ACT = mybir.ActivationFunctionType
AX = mybir.AxisListType.X
ds = bass.ds

P = 128
NB = 2
T = 1024
NT = T // P
BANK = 512
HALF = T // BANK
HD = 64
HEADS = 16
PAIRS = HEADS // 2
GROUPS = PAIRS // 2
CHUNK = 64
NC = T // CHUNK
E0, F0, SLOTS = 16, 256, 64
E1, F1, SF = 16, 128, 512
QSCALE = HD ** -0.5
EPS_LN = 1e-5
EPS_MASK = 1e-10
EPS_TOTAL = 1e-9

CONST_COLS = {"ident": 128, "neg": 128, "mask": 128, "quad": 128, "minus_lo": 1, "first": 16,
              "eps_row": NT, "chunk": NT * 32, "spread": T}
CONST_AT = {}
_at = 0
for _name, _cols in CONST_COLS.items():
    CONST_AT[_name] = _at
    _at += _cols
CONST_TOTAL = _at

UNITS1 = E1 + SF // F1

LN_STEPS = 4
MOD_STEPS = 9
CONV_STEPS = 7
NORM_STEPS = 5
ROUTE_STEPS = 5


def layer_program(nc, A, out):
    ctx = ExitStack()
    with ctx:
        def sb(name, shape, dt=F32):
            return ctx.enter_context(nc.sbuf_tensor(name, shape, dt))

        def sem(name):
            return ctx.enter_context(nc.semaphore(name))

        consts = sb("consts", [P, CONST_TOTAL])

        def const(name, lo=0, hi=None):
            at = CONST_AT[name]
            return consts[:, at + lo:at + (CONST_COLS[name] if hi is None else hi)]

        ident = const("ident")
        ident_b = sb("ident_b", [P, P], BF16)
        neg_b = sb("neg_b", [P, P], BF16)
        chunk_sum = const("chunk").rearrange("p (t c) -> p t c", t=NT)
        ones_row = sb("ones_row", [1, BANK])
        eps_col = sb("eps_col", [P, 2])

        x = sb("x", [P, NT, P])
        xn = sb("xn", [P, NT, P])
        hT = sb("hT", [P, T + 2])
        att_in = sb("att_in", [P, T])
        stats = sb("stats", [P, NT, 6])
        mv = sb("mv", [P, NT, 2])
        std = sb("std", [P, NT])
        rstd = sb("rstd", [P, NT])
        ccol = sb("ccol", [P, 2])
        scol = sb("scol", [P, 2])
        sc_b = sb("sc_b", [P, 2, P])
        mod = sb("mod", [P, 2, 6 * P])

        conv_w = sb("conv_w", [P, 3])
        conv_b = sb("conv_b", [P, 1])
        kgen_w = sb("kgen_w", [P, 3])
        kgen_b = sb("kgen_b", [P, 3])
        ctx_sum = sb("ctx_sum", [P, 1])
        ctx_b = sb("ctx_b", [P, P])
        dyn = sb("dyn", [P, 3])
        dsig = sb("dsig", [P, 3])
        dsum = sb("dsum", [P, 1])
        gate = sb("gate", [P, 1])

        wq_s = sb("wq_s", [P, 4, P])
        wk_s = sb("wk_s", [P, 4, P])
        wv_s = sb("wv_s", [P, 256])
        bq_s = sb("bq_s", [1, 4, P])
        bk_s = sb("bk_s", [1, 4, P])
        bv_s = sb("bv_s", [1, 256])
        wo = sb("wo", [P, PAIRS, P])
        bo1 = sb("bo1", [1, P])
        QA = [sb(f"QA{h}", [P, T], FR) for h in range(2)]
        QB = [sb(f"QB{h}", [P, T], FR) for h in range(2)]
        KA = [sb(f"KA{h}", [P, T], FR) for h in range(2)]
        KB = [sb(f"KB{h}", [P, T], FR) for h in range(2)]
        V0 = sb("V0", [P, NT, HD])
        V1 = sb("V1", [P, NT, 2, P])
        Vlater = sb("Vlater", [P, NT - 2, 2, P])
        E = sb("E", [P, 2, NT, T])
        U = sb("U", [P, PAIRS, T])
        mx = sb("mx", [P, 2, NT, NC])
        mrow1 = sb("mrow1", [P, 2, NT])
        mx1 = sb("mx1", [P, 2, NT])
        rs, sw, r3 = (Vlater[:, 2 * i:2 * i + 2, :, :].rearrange("p t h d -> p (t h d)") for i in range(3))
        r_hi, r_parts = KA[1][:, 0:BANK], KA[1][:, BANK:T]
        spread = KB[1]
        gsign = E[:, 1, 4, 0:4 * P].rearrange("p (l h d) -> p l h d", l=2, h=2)
        gabs = E[:, 1, 4, 4 * P:8 * P].rearrange("p (l h d) -> p l h d", l=2, h=2)
        F = [att_in, xn[:, :, :].rearrange("p t d -> p (t d)")]

        seT = sb("seT", [P, T])
        slot_aff = sb("slot_aff", [P, 3, P])
        norm_aff = sb("norm_aff", [P, 2, P])
        scale_b = sb("scale_b", [P, 1])
        xfT = U[:, 0, :]
        slT = U[:, 1, :]
        slot_tok = U[:, 2, :].rearrange("p (t d) -> p t d", t=NT)
        neg_rows = U[0:1, 1:3, :]
        Uf = U[:, :, :].rearrange("p n t -> p (n t)")
        u_at = [3 * T]

        def in_u(cols, rows=P):
            at = u_at[0]
            u_at[0] += cols
            assert u_at[0] <= PAIRS * T
            return Uf[0:rows, at:at + cols]

        xfa = in_u(NT * (P + 1)).rearrange("p (t d) -> p t d", t=NT)
        eo = in_u(NT * (P + 1)).rearrange("p (t d) -> p t d", t=NT)
        mxs = sb("mxs", [P, 2, NT])
        rsl = sb("rsl", [P, NT])
        wg_s = [in_u(F0) for _ in range(2)]
        wu_s = [in_u(F0) for _ in range(2)]
        wd_s = [in_u(F0).rearrange("p (h d) -> p h d", h=2) for _ in range(2)]
        bgu_s = [sb(f"bgu_s{i}", [P, 2, 2]) for i in range(2)]
        bd_s = [sb(f"bd_s{i}", [1, P]) for i in range(2)]
        gel = [sb(f"gel{i}", [P, 2, SLOTS]) for i in range(2)]
        act0 = [sb(f"act0{i}", [P, 2, SLOTS]) for i in range(2)]

        router = sb("router", [P, E1])
        lg = sb("lg", [P, NT, E1])
        top = sb("top", [P, NT])
        eq = sb("eq", [P, NT, E1])
        best = sb("best", [P, NT])
        sig = sb("sig", [P, NT])
        sc_tok = sb("sc_tok", [P, NT, E1])
        scT = E[0:E1, 1, 4, :]
        wgu1 = [E[:, 1, 5, i * 4 * P:i * 4 * P + 2 * P] for i in range(2)]
        wd1 = [E[:, 1, 5, i * 4 * P + 2 * P:i * 4 * P + 3 * P] for i in range(2)]
        sel1 = [E[0:E1, 1, 5, i * 4 * P + 3 * P:(i + 1) * 4 * P] for i in range(2)]
        zero_row = E[0:1, 1, 6, 0:BANK]
        xs1 = [E[:, 0, i, :] for i in range(2)]
        sg1 = [E[:, 0, 2 + i, :] for i in range(2)]
        ac1 = [E[:, 0, 4 + i, :] for i in range(2)]
        wmod = E[:, 1, 2:4, :].rearrange("p a b -> p (a b)")[:, 0:12 * P].rearrange("p (l n) -> p l n", l=2)
        wsh = E[:, 1, 0:2, :].rearrange("p a b -> p (a b)")[:, 0:3 * SF]
        tmp = E[:, 1, 7, :].rearrange("p (t d) -> p t d", t=NT)

        PS = ctx.enter_context(nc.psum_tensor("PS", [P, 8 * BANK], F32))

        def banks(first, cols=T, lo=0, rows=P):
            return PS[0:rows, first * BANK + lo:first * BANK + lo + cols]

        s_const = sem("s_const")
        s_prep = sem("s_prep")
        s_x = sem("s_x")
        s_c = sem("s_c")
        s_out = sem("s_out")
        s_held = sem("s_held")
        s_silu = sem("s_silu")
        s_scb = sem("s_scb")
        s_mod_ps = sem("s_mod_ps")
        s_mod = sem("s_mod")
        ln_var = sem("ln_var")
        ln_std = sem("ln_std")
        ln_link = sem("ln_link")
        ln_out = sem("ln_out")
        s_rows = sem("s_rows")
        tr_ps = sem("tr_ps")
        tr_out = sem("tr_out")
        cv_link = sem("cv_link")
        cv_ctx = sem("cv_ctx")
        cv_dyn = sem("cv_dyn")
        cv_pre = sem("cv_pre")
        cv_sig = sem("cv_sig")
        cv_out = sem("cv_out")

        def layer_sems(names):
            return [{n: sem(f"{n}_{L}") for n in ("wo_in " + names).split()} for L in range(2)]

        S = layer_sems("w_in proj_q q_hi q_lo proj_k k_hi k_lo proj_v v_out p1_full p1_max "
                       "m_top mt_ps m_rows p2_full p2_exp u_full u_out o_full")
        s_full = sem("s_full")
        nr_link = sem("nr_link")
        s_sw = sem("s_sw")
        t_full = sem("t_full")
        s_rr = sem("s_rr")
        p3_full = sem("p3_full")
        p3_mul = sem("p3_mul")
        later = sem("later")
        f_exp = sem("f_exp")
        diag = sem("diag")
        u_link = sem("u_link")
        res_link = sem("res_link")

        lg_full = sem("lg_full")
        lg_max = sem("lg_max")
        nm_ps = sem("nm_ps")
        nm_out = sem("nm_out")
        ex_full = sem("ex_full")
        ex_out = sem("ex_out")
        sl_full = sem("sl_full")
        sl_link = sem("sl_link")
        sl_out = sem("sl_out")
        xw = [sem(f"xw{i}") for i in range(2)]
        xf_full = sem("xf_full")
        xf_gel = sem("xf_gel")
        xf_act = sem("xf_act")
        xd_full = sem("xd_full")
        xd_out = sem("xd_out")
        cb_full = sem("cb_full")
        xw_ones = sem("xw_ones")

        rt_full = sem("rt_full")
        rt_link = sem("rt_link")
        rt_sig_in = sem("rt_sig_in")
        rt_sig = sem("rt_sig")
        rt_out = sem("rt_out")
        rt_ps = sem("rt_ps")
        rt_T = sem("rt_T")
        yw = [sem(f"yw{i}") for i in range(2)]
        shw = sem("shw")
        y_sc = sem("y_sc")
        y_xs = sem("y_xs")
        y_gate = sem("y_gate")
        y_up = sem("y_up")
        y_silu = sem("y_silu")
        y_act = sem("y_act")
        y_dn = sem("y_dn")

        start_at_one = [s_out, xd_full, y_dn, p3_mul, f_exp, xf_act, xd_out, y_silu, y_act, y_xs, later]
        start_at_one += [S[L][name] for L in range(2) for name in ("proj_v", "proj_q", "o_full", "u_out", "u_full")]

        class Chain:

            def __init__(self, eng, semaphore, base):
                self.eng, self.semaphore, self.base, self.n = eng, semaphore, base, 0

            def done(self, ins):
                ins.then_inc(self.semaphore, 1)
                self.n += 1
                self.eng.wait_ge(self.semaphore, self.base + self.n)

        block = ctx.enter_context(nc.Block())

        LN_CALLS = 5
        TR_CALLS = 5

        @block.sync
        def _(sp):
            for dst, src in [(consts[:, :], A["consts"]), (conv_w[:, :], A["conv_w"]), (conv_b[:, :], A["conv_b"]),
                             (kgen_w[:, :], A["kgen_w"]), (kgen_b[:, :], A["kgen_b"].partition_broadcast(P)),
                             (bo1[:, :], A["bo1"]),
                             (slot_aff[:, 0, :], A["slot_g"].partition_broadcast(P)),
                             (slot_aff[:, 1, :], A["slot_b"].partition_broadcast(P)),
                             (scale_b[:, :], A["scale"].partition_broadcast(P)),
                             (norm_aff[:, 0, :], A["norm_g"].partition_broadcast(P)),
                             (norm_aff[:, 1, :], A["norm_b"].partition_broadcast(P)),
                             (router[:, :], A["router"]),
                             (x[:, :, :], A["slots"])]:
                sp.dma_start(dst, src).then_inc(s_const, 16)
            for q in start_at_one:
                sp.sem_inc(q, 1)
            sp.wait_ge(ln_out, 1)
            with sp.Fori(0, NB) as b:
                sp.wait_ge(s_out, 1 + b * 16)
                sp.dma_start(x[:, :, :], A["hidden"][ds(b, 1)].squeeze(0).rearrange("(t p) d -> p t d", p=P)).then_inc(s_x, 16)
                sp.dma_start(ccol[:, :], A["c"][ds(b, 1)].squeeze(0)).then_inc(s_c, 16)
                sp.dma_start(wmod[:, :, :], A["wmod"]).then_inc(s_c, 16)
                for L in range(2):
                    v_used = sp.snap(1 + (b + L) * (GROUPS * (2 if L == 0 else 1)))
                    q_used = sp.snap(1 + (b + L) * (GROUPS * 4))
                    wo_used = sp.snap(1 + b + L)
                    sp.wait_ge(S[1 - L]["proj_v"], v_used)
                    sp.sem_inc(s_held, 1)
                    sp.wait_ge(S[1 - L]["proj_q"], q_used)
                    sp.sem_inc(s_held, 1)
                    sp.wait_ge(S[1 - L]["o_full"], wo_used)
                    sp.sem_inc(s_held, 1)
                    sp.dma_start(wo[:, :, :], A[f"wo{L}"]).then_inc(S[L]["wo_in"], 16)
                    with sp.Fori(0, GROUPS) as g:
                        v_used = sp.snap(1 + (b * GROUPS + g) * (1 if L == 0 else 2))
                        q_used = sp.snap(1 + (b * GROUPS + g) * 4)
                        sp.wait_ge(S[L]["proj_v"], v_used)
                        sp.wait_ge(S[L]["proj_q"], q_used)
                        sp.sem_inc(s_held, 1)
                        w_in = S[L]["w_in"]
                        for half in range(2):
                            cols = slice(half * HD, half * HD + HD)
                            sp.dma_start(wq_s[:, :, cols], A[f"wq{L}"][:, ds(g * 4, 4), :]).then_inc(w_in, 16)
                            if L == 0:
                                sp.dma_start(wk_s[:, 0, cols], A["wk0"][:, ds(g, 1), :].squeeze(1)).then_inc(w_in, 16)
                            else:
                                sp.dma_start(wk_s[:, :, cols], A["wk1"][:, ds(g * 4, 4), :]).then_inc(w_in, 16)
                                sp.dma_start(bq_s[:, :, cols], A["bq1"][:, ds(g * 4, 4), :]).then_inc(w_in, 16)
                                sp.dma_start(bk_s[:, :, cols], A["bk1"][:, ds(g * 4, 4), :]).then_inc(w_in, 16)
                        if L == 0:
                            sp.dma_start(wv_s[:, 0:HD], A["wv0"][:, ds(g * HD, HD)]).then_inc(w_in, 16)
                        else:
                            sp.dma_start(wv_s[:, :], A["wv1"][:, ds(g * 256, 256)]).then_inc(w_in, 16)
                            sp.dma_start(bv_s[:, :], A["bv1"][:, ds(g * 256, 256)]).then_inc(w_in, 16)
                    if L == 0:
                        with sp.Fori(0, E0 // 2) as j:
                            for i in range(2):
                                sp.wait_ge(S[0]["o_full"], 1 + b + 1)
                                sp.sem_inc(s_held, 1)
                                sp.wait_ge(xd_full, 1 + b * (E0 // 2) + j)
                                e = j * 2 + i
                                sp.dma_start(wg_s[i], A["Wg"][ds(e, 1)].squeeze(0)).then_inc(xw[i], 16)
                                sp.dma_start(wu_s[i], A["Wu"][ds(e, 1)].squeeze(0)).then_inc(xw[i], 16)
                                sp.dma_start(wd_s[i], A["Wd"][ds(e, 1)].squeeze(0).rearrange("(h p) d -> p h d", p=P)).then_inc(xw[i], 16)
                                sp.dma_start(bgu_s[i][:, :, :], A["bgu"][ds(e, 1)].squeeze(0)).then_inc(xw[i], 16)
                                sp.dma_start(bd_s[i][:, :], A["bd"][ds(e, 1)]).then_inc(xw[i], 16)
                    else:
                        sp.wait_ge(S[1]["o_full"], 1 + b + 1)
                        sp.dma_start(wsh, A["wsh"]).then_inc(shw, 16)
                        with sp.Fori(0, E1 // 2) as j:
                            for i in range(2):
                                sp.wait_ge(y_dn, 1 + b * UNITS1 + j * 2)
                                e = j * 2 + i
                                sp.dma_start(wgu1[i], A["gate_up"][ds(e, 1)].squeeze(0)).then_inc(yw[i], 16)
                                sp.dma_start(wd1[i], A["down"][ds(e, 1)].squeeze(0)).then_inc(yw[i], 16)
                                sp.dma_start(sel1[i], A["sel"][ds(e, 1)].squeeze(0)).then_inc(yw[i], 16)
                sp.wait_ge(res_link, (b + 1) * 8)
                sp.dma_start(out[ds(b, 1)].squeeze(0).rearrange("(t p) d -> p t d", p=P), x[:, :, :]).then_inc(s_out, 16)
            sp.wait_ge(s_out, 1 + NB * 16)

        @block.tensor
        def _(pe):
            def transposed(src, m):
                for t in range(NT):
                    mm = pe.transpose(banks(0, P, t * P), src(t), ident)
                mm.then_inc(tr_ps, 1)

            def attention(L, b):
                s = S[L]
                x_in = att_in if L == 0 else hT[:, 1:T + 1]
                m_rows_n = NC if L == 0 else 1
                krows = HD + m_rows_n
                ring = 2 * NT if L == 0 else 2 * NT + 2
                per_out = 1 if L == 0 else 2
                with pe.Fori(0, GROUPS) as g:
                    for u in range(2):
                        n = b * PAIRS + g * 2 + u
                        if u == 0:
                            if L == 0:
                                pe.wait_ge(cv_out, b + 1)
                            else:
                                pe.wait_ge(tr_out, 1 + b * TR_CALLS + 4)
                            pe.wait_ge(s["w_in"], (b * GROUPS + g + 1) * (80 if L == 0 else 160))
                        if L == 0:
                            pe.wait_ge(p3_mul, 1 + n * 2 * NT)
                        else:
                            pe.wait_ge(f_exp, 1 + n * 2)
                        for h in range(2):
                            for half in range(2):
                                mm = pe.matmul(banks(2 * h + half, BANK), wq_s[:, 2 * u + h, :],
                                               x_in[:, half * BANK:(half + 1) * BANK], start=True, stop=(L == 0))
                                if L == 1:
                                    mm = pe.matmul(banks(2 * h + half, BANK), bq_s[:, 2 * u + h, :], ones_row[:, :],
                                                   start=False, stop=True)
                            mm.then_inc(s["proj_q"], 1)
                        pe.wait_ge(s["u_out"], 1 + n * per_out)
                        if L == 0 and u == 0:
                            for half in range(2):
                                mm = pe.matmul(banks(4 + half, BANK), wk_s[:, 0, :],
                                               x_in[:, half * BANK:(half + 1) * BANK], start=True, stop=True)
                            mm.then_inc(s["proj_k"], 1)
                            for t in range(NT):
                                mm = pe.matmul(banks(6, HD, t * HD), x_in[:, t * P:(t + 1) * P], wv_s[:, 0:HD],
                                               start=True, stop=True)
                            mm.then_inc(s["proj_v"], 1)
                        if L == 1:
                            for h in range(2):
                                for half in range(2):
                                    pe.matmul(banks(4 + 2 * h + half, BANK), wk_s[:, 2 * u + h, :],
                                              x_in[:, half * BANK:(half + 1) * BANK], start=True, stop=False)
                                    mm = pe.matmul(banks(4 + 2 * h + half, BANK), bk_s[:, 2 * u + h, :],
                                                   ones_row[:, :], start=False, stop=True)
                                mm.then_inc(s["proj_k"], 1)
                            pe.wait_ge(s["q_hi"], 2 * n + 1)
                            pe.wait_ge(s["q_lo"], 2 * n + 1)
                            for t in range(NT):
                                pe.matmul(banks(0, P, t * P), x_in[:, t * P:(t + 1) * P],
                                          wv_s[:, u * P:(u + 1) * P], start=True, stop=False)
                                mm = pe.matmul(banks(0, P, t * P), ones_row[:, 0:P], bv_s[:, u * P:(u + 1) * P],
                                               start=False, stop=True)
                            mm.then_inc(s["proj_v"], 1)
                        n_k = b * GROUPS + g + 1 if L == 0 else 2 * n + 2
                        pe.wait_ge(s["q_hi"], 2 * n + 2)
                        pe.wait_ge(s["q_lo"], 2 * n + 2)
                        pe.wait_ge(s["k_hi"], n_k)
                        pe.wait_ge(s["k_lo"], n_k)
                        pe.wait_ge(s["v_out"], b * GROUPS + g + 1 if L == 0 else n + 1)
                        for i in range(2 * NT):
                            h, t = divmod(i, NT)
                            k = KA[0 if L == 0 else h]
                            first = 2 * (i % 2)
                            if i >= 2:
                                pe.wait_ge(s["p1_max"], n * 2 * NT + i - 1)
                            width = T if L == 0 else (t + 1) * P
                            for lo in range(0, width, BANK):
                                hi = min(lo + BANK, width)
                                own = L == 1 and hi == width
                                mm = pe.matmul(banks(first, hi - lo, lo), QB[h][0:HD, t * P:(t + 1) * P],
                                               k[0:HD, lo:hi], start=True, stop=not own)
                                if own:
                                    mm = pe.matmul(banks(first, P, width - P), ident_b[:, :], neg_b[:, :],
                                                   start=False, stop=True)
                            mm.then_inc(s["p1_full"], 1)
                        if L == 0:
                            pe.wait_ge(s["p1_max"], (n + 1) * 2 * NT)
                        else:
                            pe.wait_ge(s["m_top"], n + 1)
                        for h in range(2):
                            for t in range(NT):
                                src = mx[:, h, t, :] if L == 0 else mx1[:, h, t:t + 1]
                                mm = pe.transpose(banks(4 + 2 * h, P, t * P, rows=m_rows_n), src, ident)
                            mm.then_inc(s["mt_ps"], 1)
                        pe.wait_ge(s["m_rows"], 2 * n + 2)

                        def chunk_sums(t):
                            pe.wait_ge(s["p2_exp"], n * 2 * NT + 2 * t + 2)
                            for h in range(2):
                                for half in range(2):
                                    j = 2 * h + half
                                    mm = pe.matmul(PS[32 * j:32 * j + 32, 4 * BANK:5 * BANK], chunk_sum[:, t, :],
                                                   E[:, h, t, half * BANK:(half + 1) * BANK],
                                                   start=(t == 0), stop=(t == NT - 1))
                            return mm

                        for i in range(2 * NT):
                            t, h = divmod(i, 2)
                            kk = 0 if L == 0 else h
                            first = 2 * (i % 2)
                            if i >= 2:
                                pe.wait_ge(s["p2_exp"], n * 2 * NT + i - 1)
                            spans = []
                            for half in range(2):
                                lo, hi = max(half * BANK, 0 if L == 0 else t * P), (half + 1) * BANK
                                if lo < hi:
                                    spans.append((lo, hi))
                            for lo, hi in spans:
                                pe.matmul(banks(first, hi - lo, lo), KA[kk][:, t * P:(t + 1) * P], QA[h][:, lo:hi],
                                          start=True, stop=False)
                            for lo, hi in spans:
                                mm = pe.matmul(banks(first, hi - lo, lo), KB[kk][0:krows, t * P:(t + 1) * P],
                                               QB[h][0:krows, lo:hi], start=False, stop=True)
                            mm.then_inc(s["p2_full"], 1)
                            if L == 0 and h == 1 and t >= 1:
                                chunk_sums(t - 1)
                        if L == 0:
                            chunk_sums(NT - 1).then_inc(s_full, 1)
                            pe.wait_ge(s_sw, n + 1)
                            pe.matmul(banks(5, BANK), const("quad"), sw[:, :], start=True, stop=True).then_inc(t_full, 1)
                            pe.wait_ge(s_rr, n + 1)

                            def values(t):
                                pe.wait_ge(p3_mul, 1 + n * 2 * NT + 2 * t + 2)
                                for half in range(2):
                                    for h in range(2):
                                        mm = pe.matmul(PS[HD * h:HD * h + HD, (6 + half) * BANK:(7 + half) * BANK],
                                                       V0[:, t, :], E[:, h, t, half * BANK:(half + 1) * BANK],
                                                       start=(t == 0), stop=(t == NT - 1))
                                return mm

                            for i in range(2 * NT):
                                t, h = divmod(i, 2)
                                first = 2 * (i % 2)
                                if i >= 2:
                                    pe.wait_ge(p3_mul, 1 + n * 2 * NT + i - 1)
                                for half in range(2):
                                    q = 32 * (2 * h + half)
                                    mm = pe.matmul(banks(first + half, BANK), spread[q:q + 32, t * P:(t + 1) * P],
                                                   r_parts[q:q + 32, :], start=True, stop=True,
                                                   tile_position=(q, 0))
                                mm.then_inc(p3_full, 1)
                                if h == 1 and t >= 1:
                                    values(t - 1)
                            values(NT - 1).then_inc(s["u_full"], 1)
                        else:
                            for h in range(2):
                                pe.wait_ge(s["p2_exp"], n * 2 * NT + 2 * NT - 1 + h)
                                for half in range(2):
                                    mm = pe.matmul(banks(2 * h + half, BANK), KB[h][HD:HD + 1, 0:P],
                                                   QB[h][HD:HD + 1, half * BANK:(half + 1) * BANK],
                                                   start=True, stop=True)
                                mm.then_inc(s["p2_full"], 1)
                            pe.wait_ge(later, 1 + n + 1)
                            for h in range(2):
                                pe.wait_ge(diag, 2 * n + h + 1)
                                for t in range(NT):
                                    for half in range(2):
                                        lo, hi = max(half * BANK, t * P), (half + 1) * BANK
                                        if lo < hi:
                                            pe.matmul(banks(4 + 2 * h, hi - lo, lo), V1[:, t, h, :], E[:, h, t, lo:hi],
                                                      start=(t == 0), stop=False, skip_group_check=True)
                                for t in range(NT - 1):
                                    v = V1[:, t + 1, h, :] if t == NT - 2 else Vlater[:, t, h, :]
                                    mm = pe.matmul(banks(4 + 2 * h, P, t * P), v,
                                                   F[h][:, t * P:(t + 1) * P], start=False, stop=(t in (3, NT - 2)),
                                                   skip_group_check=True)
                                mm.then_inc(s["u_full"], 1)
                pe.wait_ge(s["u_out"], 1 + (b + 1) * PAIRS * per_out)
                pe.wait_ge(s["wo_in"], (b + 1) * 16)
                for t in range(NT):
                    for p in range(PAIRS):
                        mm = pe.matmul(banks(0, P, t * P), U[:, p, t * P:(t + 1) * P], wo[:, p, :],
                                       start=(p == 0), stop=(p == PAIRS - 1 and L == 0))
                    if L == 1:
                        mm = pe.matmul(banks(0, P, t * P), ones_row[:, 0:P], bo1[:, :], start=False, stop=True)
                mm.then_inc(s["o_full"], 1)

            def mixture(b):
                pe.wait_ge(tr_out, 1 + b * TR_CALLS + 2)
                for i in range(2 * NT):
                    kind, t = divmod(i, NT)
                    a, c = (xfT, seT) if kind == 0 else (seT, xfT)
                    first = 2 * (i % 2)
                    if i >= 2:
                        pe.wait_ge(lg_max, b * 2 * NT + i - 1)
                    for half in range(2):
                        mm = pe.matmul(banks(first + half, BANK), a[:, t * P:(t + 1) * P],
                                       c[:, half * BANK:(half + 1) * BANK], start=True, stop=True)
                    mm.then_inc(lg_full, 1)
                pe.wait_ge(lg_max, (b + 1) * 2 * NT)
                for kind in range(2):
                    for t in range(NT):
                        mm = pe.transpose(banks(4 + 2 * kind, P, t * P, rows=1), mxs[:, kind, t:t + 1], ident)
                mm.then_inc(nm_ps, 1)
                pe.wait_ge(nm_out, b + 1)
                for i in range(2 * NT):
                    kind, t = divmod(i, NT)
                    a, c = (xfT, seT) if kind == 0 else (seT, xfT)
                    first = 2 * (i % 2)
                    if i >= 2:
                        pe.wait_ge(ex_out, b * 2 * NT + i - 1)
                    for half in range(2):
                        cols = slice(half * BANK, (half + 1) * BANK)
                        pe.matmul(banks(first + half, BANK), a[:, t * P:(t + 1) * P], c[:, cols],
                                  start=True, stop=False)
                        mm = pe.matmul(banks(first + half, BANK), ones_row[:, 0:P], neg_rows[:, 1 - kind, cols],
                                       start=False, stop=True)
                    mm.then_inc(ex_full, 1)
                pe.wait_ge(ex_out, b * 2 * NT + NT)
                for st in range(NT):
                    for t in range(NT):
                        mm = pe.matmul(banks(4, P + 1, st * 256), E[:, 0, t, st * P:(st + 1) * P], xfa[:, t, :],
                                       start=(t == 0), stop=(t == NT - 1))
                mm.then_inc(sl_full, 1)
                pe.wait_ge(sl_out, b + 1)
                pe.wait_ge(ex_out, (b + 1) * 2 * NT)
                transposed(lambda t: slot_tok[:, t, :], None)
                with pe.Fori(0, E0 // 2) as j:
                    pe.wait_ge(tr_out, 1 + b * TR_CALLS + 3)
                    for i in range(2):
                        ex = (b * (E0 // 2) + j) * 2 + i
                        pe.wait_ge(xw[i], (b * (E0 // 2) + j + 1) * 80)
                        pe.wait_ge(xf_act, 1 + ex - i)
                        rhs = slT[:, ds((j * 2 + i) * SLOTS, SLOTS)]
                        for k in range(4):
                            w = (wg_s if k < 2 else wu_s)[i]
                            mm = pe.matmul(banks(i, SLOTS, k * SLOTS), w[:, (k % 2) * P:(k % 2 + 1) * P], rhs,
                                           start=True, stop=True)
                        mm.then_inc(xf_full, 1)
                    pe.wait_ge(xd_out, 1 + b * (E0 // 2) + j)
                    for i in range(2):
                        pe.wait_ge(xf_act, 1 + (b * (E0 // 2) + j) * 2 + i + 1)
                        o = PS[HD * i:HD * i + HD, 2 * BANK:2 * BANK + P]
                        pe.matmul(o, act0[i][:, 0, :], wd_s[i][:, 0, :], start=True, stop=False)
                        pe.matmul(o, act0[i][:, 1, :], wd_s[i][:, 1, :], start=False, stop=False)
                        mm = pe.matmul(o, ones_row[:, 0:SLOTS], bd_s[i][:, :], start=False, stop=True)
                    mm.then_inc(xd_full, 1)
                pe.wait_ge(xd_out, 1 + (b + 1) * (E0 // 2))
                for t in range(NT):
                    for st in range(NT):
                        mm = pe.matmul(banks(4, P + 1, t * 256), E[:, 1, st, t * P:(t + 1) * P], eo[:, st, :],
                                       start=(st == 0), stop=(st == NT - 1))
                mm.then_inc(cb_full, 1)

            def experts(b):
                pe.wait_ge(tr_out, 1 + b * TR_CALLS + 5)
                for t in range(NT):
                    mm = pe.matmul(banks(2, E1, t * E1), hT[:, 1 + t * P:1 + (t + 1) * P], router[:, :],
                                   start=True, stop=True)
                mm.then_inc(rt_full, 1)
                pe.wait_ge(rt_out, b + 1)
                for t in range(NT):
                    mm = pe.transpose(banks(4, P, t * P, rows=E1), sc_tok[:, t, :], ident)
                mm.then_inc(rt_ps, 1)
                pe.wait_ge(rt_T, b + 1)
                for half in range(2):
                    pe.matmul(banks(6 + half, BANK), ones_row[:, 0:P], zero_row, start=True, stop=False,
                              skip_group_check=True)

                def gate_up(y, wg, wu, src, from_acc):
                    pe.wait_ge(y_silu, 1 + y)
                    for half in range(2):
                        mm = pe.matmul(banks(2 + half, BANK), wg, src[:, half * BANK:(half + 1) * BANK],
                                       start=True, stop=True)
                    mm.then_inc(y_gate, 1)
                    pe.wait_ge(y_act, 1 + y)
                    for half in range(2):
                        mm = pe.matmul(banks(4 + half, BANK), wu, src[:, half * BANK:(half + 1) * BANK],
                                       start=True, stop=True)
                    mm.then_inc(y_up, 1)

                def down(y, a, w):
                    pe.wait_ge(y_act, 1 + y + 1)
                    for t in range(NT):
                        mm = pe.matmul(banks(6, P, t * P), a[:, t * P:(t + 1) * P], w, start=False, stop=False,
                                       skip_group_check=True)
                    mm.then_inc(y_dn, 1)

                with pe.Fori(0, E1 // 2) as j:
                    for i in range(2):
                        e = b * E1 + j * 2 + i
                        y = b * UNITS1 + j * 2 + i
                        pe.wait_ge(yw[i], (b * (E1 // 2) + j + 1) * 48)
                        pe.wait_ge(y_xs, 1 + e)
                        for half in range(2):
                            mm = pe.matmul(banks(half, BANK), sel1[i], scT[:, half * BANK:(half + 1) * BANK],
                                           start=True, stop=True)
                        mm.then_inc(y_sc, 1)
                        pe.wait_ge(y_xs, 1 + e + 1)
                        gate_up(y, wgu1[i][:, 0:F1], wgu1[i][:, F1:2 * F1], xs1[i], True)
                    for i in range(2):
                        down(b * UNITS1 + j * 2 + i, ac1[i], wd1[i])
                pe.wait_ge(shw, (b + 1) * 16)
                for k in range(SF // F1):
                    y = b * UNITS1 + E1 + k
                    gate_up(y, wsh[:, k * P:(k + 1) * P], wsh[:, SF + k * P:SF + (k + 1) * P], hT[:, 1:T + 1], False)
                    down(y, ac1[k % 2], wsh[:, 2 * SF + k * P:2 * SF + (k + 1) * P])

            pe.wait_ge(s_const, 13 * 16)
            pe.wait_ge(s_prep, 3)
            pe.wait_ge(ln_out, 1)
            transposed(lambda t: xn[:, t, :], 0)
            with pe.Fori(0, NB) as b:
                pe.wait_ge(s_c, (b + 1) * 32)
                pe.wait_ge(s_scb, b + 1)
                for L in range(2):
                    for half in range(2):
                        mm = pe.matmul(banks(2 * L + half, 3 * P), sc_b[:, L, :],
                                       wmod[:, L, half * 3 * P:(half + 1) * 3 * P], start=True, stop=True)
                mm.then_inc(s_mod_ps, 1)
                pe.wait_ge(ln_out, 1 + b * LN_CALLS + 1)
                transposed(lambda t: xn[:, t, :], 0)
                pe.wait_ge(cv_ctx, b + 1)
                pe.matmul(banks(2, 3), ctx_b[:, :], kgen_w[:, :], start=True, stop=True).then_inc(cv_dyn, 1)
                attention(0, b)
                pe.wait_ge(ln_out, 1 + b * LN_CALLS + 3)
                transposed(lambda t: xfa[:, t, 0:P], 1)
                mixture(b)
                pe.wait_ge(ln_out, 1 + b * LN_CALLS + 4)
                transposed(lambda t: xn[:, t, :], 3)
                attention(1, b)
                pe.wait_ge(ln_out, 1 + b * LN_CALLS + 5)
                transposed(lambda t: xn[:, t, :], 4)
                experts(b)

        @block.scalar
        def _(act):
            def std_of(m):
                act.wait_ge(ln_var, m + 1)
                act.activation(std[:, :], mv[:, :, 1], ACT.Sqrt, bias=eps_col[:, 0:1]).then_inc(ln_std, 1)

            def attention(L, b):
                s = S[L]
                with act.Fori(0, GROUPS) as g:
                    for u in range(2):
                        n = b * PAIRS + g * 2 + u
                        for h in range(2):
                            act.wait_ge(s["proj_q"], 1 + 2 * n + h + 1)
                            act.activation(QA[h][:, :], banks(2 * h), ACT.Copy, scale=QSCALE)
                            act.activation(QB[h][0:HD, :], banks(2 * h, rows=HD), ACT.Copy,
                                           scale=QSCALE).then_inc(s["q_hi"], 1)
                        if L == 0 and u == 0:
                            act.wait_ge(s["proj_k"], b * GROUPS + g + 1)
                            act.activation(KA[0][:, :], banks(4), ACT.Copy).then_inc(s["k_hi"], 1)
                            act.wait_ge(s["proj_v"], 1 + b * GROUPS + g + 1)
                            act.activation(V0[:, :, :].rearrange("p t d -> p (t d)"), banks(6, BANK),
                                           ACT.Copy).then_inc(s["v_out"], 1)
                        if L == 1:
                            for h in range(2):
                                act.wait_ge(s["proj_k"], 2 * n + h + 1)
                                act.activation(KA[h][:, :], banks(4 + 2 * h), ACT.Copy).then_inc(s["k_hi"], 1)
                            act.wait_ge(s["proj_v"], 1 + n + 1)
                            act.wait_ge(later, 1 + n)
                            act.activation(V1[:, :, :, 0:HD],
                                           banks(0).rearrange("p (t h d) -> p t h d", t=NT, h=2),
                                           ACT.Copy).then_inc(s["v_out"], 1)
                        for i in range(2 * NT):
                            t, h = divmod(i, 2)
                            lo = 0 if L == 0 else t * P
                            act.wait_ge(s["p2_full"], (n * 2 * NT if L == 0 else n * (2 * NT + 2)) + i + 1)
                            act.activation(E[:, h, t, lo:T], banks(2 * (i % 2), T - lo, lo),
                                           ACT.Exp).then_inc(s["p2_exp"], 1)
                        if L == 0:
                            act.wait_ge(s["u_full"], 1 + n + 1)
                            act.activation(U[:, ds(g * 2 + u, 1), :].squeeze(1), banks(6), ACT.Copy).then_inc(s["u_out"], 1)
                        else:
                            for h in range(2):
                                act.wait_ge(s["p2_full"], n * (2 * NT + 2) + 2 * NT + h + 1)
                                act.activation(F[h][:, :], banks(2 * h), ACT.Exp,
                                               bias=eps_col[:, 1:2]).then_inc(f_exp, 1)

            act.wait_ge(s_prep, 3)
            std_of(0)
            with act.Fori(0, NB) as b:
                m = 1 + b * LN_CALLS
                act.wait_ge(s_c, (b + 1) * 32)
                act.activation(scol[:, :], ccol[:, :], ACT.Silu).then_inc(s_silu, 1)
                std_of(m)
                act.wait_ge(cv_pre, b + 1)
                act.activation(dsig[:, :], dyn[:, :], ACT.Sigmoid).then_inc(cv_sig, 1)
                attention(0, b)
                std_of(m + 1)
                std_of(m + 2)
                for i in range(2 * NT):
                    kind, t = divmod(i, NT)
                    act.wait_ge(ex_full, b * 2 * NT + i + 1)
                    act.activation(E[:, kind, t, :], banks(2 * (i % 2)), ACT.Exp).then_inc(ex_out, 1)
                with act.Fori(0, E0 // 2) as j:
                    for i in range(2):
                        act.wait_ge(xf_full, (b * (E0 // 2) + j) * 2 + i + 1)
                        act.activation(gel[i][:, 0, :], banks(i, SLOTS), ACT.Gelu, bias=bgu_s[i][:, 0, 0:1])
                        act.activation(gel[i][:, 1, :], banks(i, SLOTS, SLOTS), ACT.Gelu,
                                       bias=bgu_s[i][:, 0, 1:2]).then_inc(xf_gel, 1)
                    act.wait_ge(xd_full, 1 + b * (E0 // 2) + j + 1)
                    act.activation(eo[:, ds(j, 1), 0:P].squeeze(1), banks(2, P), ACT.Copy).then_inc(xd_out, 1)
                std_of(m + 3)
                attention(1, b)
                std_of(m + 4)
                act.wait_ge(rt_sig_in, b + 1)
                act.activation(sig[:, :], top[:, :], ACT.Sigmoid).then_inc(rt_sig, 1)

                def silu(y, i):
                    act.wait_ge(y_gate, y + 1)
                    act.activation(sg1[i], banks(2), ACT.Silu).then_inc(y_silu, 1)

                with act.Fori(0, E1 // 2) as j:
                    for i in range(2):
                        silu(b * UNITS1 + j * 2 + i, i)
                for k in range(SF // F1):
                    silu(b * UNITS1 + E1 + k, k % 2)

        @block.vector
        def _(dve):
            def layernorm(src, dst, scale, shift, m):
                step = Chain(dve, ln_link, m * LN_STEPS)
                for t in range(NT):
                    ins = dve.bn_stats(stats[:, t, :], src[:, t, :])
                step.done(ins)
                dve.sem_inc(s_held, 1)
                for t in range(NT):
                    ins = dve.bn_aggr(mv[:, t, :], stats[:, t, :])
                ins.then_inc(ln_var, 1)
                dve.wait_ge(ln_std, m + 1)
                step.done(dve.reciprocal(rstd[:, :], std[:, :]))
                for t in range(NT):
                    ins = dve.tensor_scalar(xn[:, t, :], src[:, t, :], mv[:, t, 0:1], rstd[:, t:t + 1],
                                            ALU.subtract, ALU.mult)
                step.done(ins)
                step.done(dve.tensor_tensor(xn[:, :, :], xn[:, :, :],
                                            scale.unsqueeze(1).to_broadcast([P, NT, P]), ALU.mult))
                dve.tensor_tensor(dst, xn[:, :, :], shift.unsqueeze(1).to_broadcast([P, NT, P]),
                                  ALU.add).then_inc(ln_out, 1)
                dve.wait_ge(ln_out, m + 1)
                assert step.n == LN_STEPS

            def evacuate(dst, m):
                dve.wait_ge(tr_ps, m + 1)
                dve.tensor_copy(dst, banks(0)).then_inc(tr_out, 1)

            def residual(b, k, y, g):
                step = Chain(dve, res_link, b * 8 + 2 * k)
                step.done(dve.tensor_tensor(xn[:, :, :], y, g.unsqueeze(1).to_broadcast([P, NT, P]), ALU.mult))
                step.done(dve.tensor_tensor(x[:, :, :], x[:, :, :], xn[:, :, :], ALU.add))

            def tiles(ap):
                return ap.rearrange("p (t d) -> p t d", t=NT)

            def modulation(b):
                dve.wait_ge(s_silu, b + 1)
                dve.tensor_copy(sc_b[:, :, :], scol[:, :].unsqueeze(2).to_broadcast([P, 2, P])).then_inc(s_scb, 1)
                step = Chain(dve, s_mod, b * MOD_STEPS)
                dve.wait_ge(s_mod_ps, b + 1)
                for L in range(2):
                    for half in range(2):
                        ins = dve.tensor_copy(mod[:, L, half * 3 * P:(half + 1) * 3 * P], banks(2 * L + half, 3 * P))
                step.done(ins)
                parts = mod[:, :, :].rearrange("p l (h k d) -> p l h k d", h=2, k=3)
                step.done(dve.tensor_scalar(parts[:, 0, :, 1, :], parts[:, 0, :, 1, :], 1.0, None, ALU.add))
                step.done(dve.tensor_scalar(parts[:, 1, :, 1, :], parts[:, 1, :, 1, :], 1.0, None, ALU.add))
                for L in range(2):
                    dve.tensor_scalar(gsign[:, L, :, :], parts[:, L, :, 2, :], 0.0, 2.0, ALU.is_ge, ALU.mult)
                    step.done(dve.scalar_tensor_tensor(out=gabs[:, L, :, :], in0=parts[:, L, :, 2, :], scalar=-1.0,
                                                       in1=parts[:, L, :, 2, :], op0=ALU.mult, op1=ALU.max))
                step.done(dve.tensor_scalar(gabs, gabs, 0.25, None, ALU.max))
                for L in range(2):
                    ins = dve.scalar_tensor_tensor(out=parts[:, L, :, 2, :], in0=gsign[:, L, :, :], scalar=-1.0,
                                                   in1=gabs[:, L, :, :], op0=ALU.add, op1=ALU.mult)
                step.done(ins)
                dve.tensor_copy(KB[0][HD:HD + NC, :], const("spread")[HD:HD + NC, :])
                dve.tensor_copy(spread[:, :], const("spread"))
                step.done(dve.memset(hT[:, 0:1], 0.0))
                step.done(dve.memset(hT[:, T + 1:T + 2], 0.0))
                assert step.n == MOD_STEPS, step.n

            def convolution(b):
                step = Chain(dve, cv_link, b * CONV_STEPS)
                dve.wait_ge(tr_out, 1 + b * TR_CALLS + 1)
                step.done(dve.tensor_reduce(ctx_sum[:, :], hT[:, 1:T + 1], AX, ALU.add))
                step.done(dve.tensor_scalar(ctx_sum[:, :], ctx_sum[:, :], 1.0 / T, None, ALU.mult))
                dve.tensor_copy(ctx_b[:, :], ctx_sum[:, :].to_broadcast([P, P])).then_inc(cv_ctx, 1)
                step.done(dve.tensor_scalar(att_in[:, :], hT[:, 0:T], conv_w[:, 0:1], None, ALU.mult))
                for k in range(1, 3):
                    step.done(dve.scalar_tensor_tensor(out=att_in[:, :], in0=hT[:, k:k + T], scalar=conv_w[:, k:k + 1],
                                                       in1=att_in[:, :], op0=ALU.mult, op1=ALU.add))
                dve.wait_ge(cv_dyn, b + 1)
                dve.tensor_tensor(dyn[:, :], banks(2, 3), kgen_b[:, :], ALU.add).then_inc(cv_pre, 1)
                dve.wait_ge(cv_sig, b + 1)
                step.done(dve.tensor_reduce(dsum[:, :], dsig[:, :], AX, ALU.add))
                step.done(dve.tensor_scalar(gate[:, :], dsum[:, :], 1.0 / 3.0, None, ALU.mult))
                dve.tensor_scalar(att_in[:, :], att_in[:, :], conv_b[:, 0:1], gate[:, 0:1],
                                  ALU.add, ALU.mult).then_inc(cv_out, 1)
                assert step.n == CONV_STEPS, step.n

            def attention(L, b):
                s = S[L]
                with dve.Fori(0, GROUPS) as g:
                    for u in range(2):
                        n = b * PAIRS + g * 2 + u
                        for h in range(2):
                            dve.wait_ge(s["q_hi"], 2 * n + h + 1)
                            dve.scalar_tensor_tensor(out=QA[h][HD:P, :], in0=PS[HD:P, 2 * h * BANK:2 * h * BANK + T],
                                                     scalar=QSCALE, in1=QA[h][HD:P, :], op0=ALU.mult,
                                                     op1=ALU.subtract).then_inc(s["q_lo"], 1)
                        if L == 1 or u == 0:
                            for h in range(1 + L):
                                dve.wait_ge(s["k_hi"], b * GROUPS + g + 1 if L == 0 else 2 * n + h + 1)
                                dve.tensor_tensor(KB[h][0:HD, :], banks(4 + 2 * h, rows=HD), KA[h][0:HD, :],
                                                  ALU.subtract).then_inc(s["k_lo"], 1)
                        for i in range(2 * NT):
                            h, t = divmod(i, NT)
                            dve.wait_ge(s["p1_full"], n * 2 * NT + i + 1)
                            if L == 0:
                                dve.tensor_reduce(mx[:, h, t, :], banks(2 * (i % 2)).rearrange("p (c k) -> p c k", c=NC),
                                                  AX, ALU.max).then_inc(s["p1_max"], 1)
                            else:
                                dve.tensor_reduce(mrow1[:, h, t:t + 1], banks(2 * (i % 2), (t + 1) * P),
                                                  AX, ALU.max).then_inc(s["p1_max"], 1)
                        if L == 1:
                            dve.wait_ge(s["p1_max"], (n + 1) * 2 * NT)
                            dve.tensor_tensor(mx1[:, :, :], mrow1[:, :, :],
                                              const("eps_row").unsqueeze(1).to_broadcast([P, 2, NT]),
                                              ALU.max).then_inc(s["m_top"], 1)
                        rows = NC if L == 0 else 1
                        for h in range(2):
                            dve.wait_ge(s["mt_ps"], 2 * n + h + 1)
                            dve.tensor_scalar(QB[h][HD:HD + rows, :], banks(4 + 2 * h, rows=rows), -1.0, None,
                                              ALU.mult).then_inc(s["m_rows"], 1)
                        if L == 0:
                            step = Chain(dve, nr_link, n * NORM_STEPS)
                            dve.wait_ge(s_full, n + 1)
                            step.done(dve.reciprocal(rs[:, :], banks(4, BANK)))
                            dve.tensor_tensor(sw[:, :], banks(4, BANK), rs[:, :], ALU.mult).then_inc(s_sw, 1)
                            dve.wait_ge(s_sw, n + 1)
                            step.done(dve.tensor_tensor(rs[:, :], rs[:, :], sw[:, :], ALU.mult))
                            dve.wait_ge(t_full, n + 1)
                            step.done(dve.tensor_scalar(r3[:, :], banks(5, BANK), EPS_TOTAL, None, ALU.add))
                            step.done(dve.reciprocal(r3[:, :], r3[:, :]))
                            step.done(dve.tensor_tensor(rs[:, :], rs[:, :], r3[:, :], ALU.mult))
                            dve.tensor_copy(r_hi[:, :], rs[:, :]).then_inc(s_rows, 1)
                            dve.wait_ge(s_rows, n + 1)
                            dve.scalar_tensor_tensor(out=r_parts[:, :], in0=r_hi[:, :], scalar=const("minus_lo"),
                                                     in1=rs[:, :], op0=ALU.mult, op1=ALU.add).then_inc(s_rr, 1)
                            assert step.n == NORM_STEPS
                            for i in range(2 * NT):
                                t, h = divmod(i, 2)
                                dve.wait_ge(p3_full, n * 2 * NT + i + 1)
                                dve.tensor_tensor(E[:, h, t, :], E[:, h, t, :], banks(2 * (i % 2)),
                                                  ALU.mult).then_inc(p3_mul, 1)
                        else:
                            for h in range(2):
                                dve.wait_ge(f_exp, 1 + 2 * n + h + 1)
                                dve.sem_inc(s_held, 1)
                                Eh = E[:, h, :, :].rearrange("p t q -> p (t q)")
                                for t in range(NT):
                                    at = t * (T + P)
                                    ins = dve.copy_predicated(Eh[:, at:at + P], const("mask").bitcast(I32),
                                                              F[h][:, t * P:(t + 1) * P])
                                ins.then_inc(diag, 1)
                            for h in range(2):
                                dve.wait_ge(s["u_full"], 1 + 2 * n + h + 1)
                                at = (4 + 2 * h) * BANK
                                inv = F[h]
                                dve.reciprocal(inv[0:HD, :], PS[HD:P, at:at + T]).then_inc(u_link, 1)
                                dve.wait_ge(u_link, 2 * n + h + 1)
                                dve.tensor_tensor(U[HD * h:HD * h + HD, ds(g * 2 + u, 1), :].squeeze(1),
                                                  PS[0:HD, at:at + T], inv[0:HD, :], ALU.mult).then_inc(s["u_out"], 1)
                dve.wait_ge(s["o_full"], 1 + b + 1)
                residual(b, 2 * L, tiles(banks(0)), mod[:, L, 2 * P:3 * P])

            def mixture(b):
                for i in range(2 * NT):
                    kind, t = divmod(i, NT)
                    dve.wait_ge(lg_full, b * 2 * NT + i + 1)
                    dve.tensor_reduce(mxs[:, kind, t:t + 1], banks(2 * (i % 2)), AX, ALU.max).then_inc(lg_max, 1)
                dve.wait_ge(nm_ps, b + 1)
                dve.tensor_scalar(neg_rows[:, 0, :], banks(4, rows=1), -1.0, None, ALU.mult)
                dve.tensor_scalar(neg_rows[:, 1, :], banks(6, rows=1), -1.0, None, ALU.mult).then_inc(nm_out, 1)
                dve.wait_ge(sl_full, b + 1)
                wide = banks(4, 4 * BANK).rearrange("p (t d) -> p t d", t=NT)
                dve.reciprocal(rsl[:, :], wide[:, :, P]).then_inc(sl_link, 1)
                dve.wait_ge(sl_link, b * 3 + 1)
                dve.tensor_tensor(slot_tok[:, :, :], wide[:, :, 0:P], rsl[:, :].unsqueeze(2).to_broadcast([P, NT, P]),
                                  ALU.mult).then_inc(sl_out, 1)
                evacuate(slT, 1 + b * TR_CALLS + 2)
                with dve.Fori(0, E0 // 2) as j:
                    for i in range(2):
                        dve.wait_ge(xf_gel, (b * (E0 // 2) + j) * 2 + i + 1)
                        for f in range(2):
                            ins = dve.scalar_tensor_tensor(out=act0[i][:, f, :], in0=banks(i, SLOTS, (2 + f) * SLOTS),
                                                           scalar=bgu_s[i][:, 1, f:f + 1], in1=gel[i][:, f, :],
                                                           op0=ALU.add, op1=ALU.mult)
                        ins.then_inc(xf_act, 1)
                dve.wait_ge(cb_full, b + 1)
                dve.reciprocal(rsl[:, :], wide[:, :, P]).then_inc(sl_link, 1)
                dve.wait_ge(sl_link, b * 3 + 2)
                dve.tensor_tensor(xn[:, :, :], wide[:, :, 0:P], rsl[:, :].unsqueeze(2).to_broadcast([P, NT, P]),
                                  ALU.mult).then_inc(sl_link, 1)
                dve.wait_ge(sl_link, b * 3 + 3)
                residual(b, 1, xn[:, :, :], mod[:, 0, 5 * P:6 * P])

            def experts(b):
                step = Chain(dve, rt_link, b * ROUTE_STEPS)
                wide = [P, NT, E1]
                dve.wait_ge(rt_full, b + 1)
                step.done(dve.tensor_copy(lg[:, :, :], banks(2, NT * E1).rearrange("p (t e) -> p t e", t=NT)))
                dve.tensor_reduce(top[:, :], lg[:, :, :], AX, ALU.max).then_inc(rt_sig_in, 1)
                dve.wait_ge(rt_sig_in, b + 1)
                step.done(dve.tensor_tensor(eq[:, :, :], lg[:, :, :], top[:, :].unsqueeze(2).to_broadcast(wide),
                                            ALU.is_equal))
                step.done(dve.tensor_tensor(eq[:, :, :], eq[:, :, :],
                                            const("first").unsqueeze(1).to_broadcast(wide), ALU.mult))
                step.done(dve.tensor_reduce(best[:, :], eq[:, :, :], AX, ALU.max))
                step.done(dve.tensor_tensor(eq[:, :, :], eq[:, :, :], best[:, :].unsqueeze(2).to_broadcast(wide),
                                            ALU.is_equal))
                assert step.n == ROUTE_STEPS
                dve.wait_ge(rt_sig, b + 1)
                dve.tensor_tensor(sc_tok[:, :, :], eq[:, :, :], sig[:, :].unsqueeze(2).to_broadcast(wide),
                                  ALU.mult).then_inc(rt_out, 1)
                dve.wait_ge(rt_ps, b + 1)
                dve.memset(zero_row, 0.0)
                dve.tensor_copy(scT[:, :], banks(4, rows=E1)).then_inc(rt_T, 1)

                def product(y, i):
                    dve.wait_ge(y_up, y + 1)
                    dve.wait_ge(y_silu, 1 + y + 1)
                    dve.tensor_tensor(ac1[i], banks(4), sg1[i], ALU.mult).then_inc(y_act, 1)

                with dve.Fori(0, E1 // 2) as j:
                    for i in range(2):
                        dve.wait_ge(y_sc, b * E1 + j * 2 + i + 1)
                        dve.tensor_tensor(xs1[i], hT[:, 1:T + 1], banks(0), ALU.mult).then_inc(y_xs, 1)
                        product(b * UNITS1 + j * 2 + i, i)
                for k in range(SF // F1):
                    product(b * UNITS1 + E1 + k, k % 2)
                dve.wait_ge(y_dn, 1 + (b + 1) * UNITS1)
                residual(b, 3, tiles(banks(6)), mod[:, 1, 5 * P:6 * P])

            dve.memset(ones_row[:, :], 1.0)
            dve.memset(eps_col[:, 0:1], EPS_LN)
            dve.memset(eps_col[:, 1:2], EPS_MASK)
            dve.memset(V1[:, :, :, HD:P], 1.0).then_inc(s_prep, 1)
            dve.wait_ge(s_const, 13 * 16)
            dve.tensor_copy(ident_b[:, :], ident)
            dve.tensor_copy(neg_b[:, :], const("neg")).then_inc(s_prep, 1)
            dve.tensor_scalar(slot_aff[:, 0:2, :], slot_aff[:, 0:2, :], scale_b[:, 0:1], None,
                              ALU.mult).then_inc(s_prep, 1)
            dve.wait_ge(s_prep, 3)
            layernorm(x, xn[:, :, :], slot_aff[:, 0, :], slot_aff[:, 1, :], 0)
            evacuate(seT[:, :], 0)
            with dve.Fori(0, NB) as b:
                m = 1 + b * LN_CALLS
                r = 1 + b * TR_CALLS
                modulation(b)
                dve.wait_ge(s_x, (b + 1) * 16)
                layernorm(x, xn[:, :, :], mod[:, 0, P:2 * P], mod[:, 0, 0:P], m)
                evacuate(hT[:, 1:T + 1], r)
                convolution(b)
                attention(0, b)
                layernorm(x, xn[:, :, :], mod[:, 0, 4 * P:5 * P], mod[:, 0, 3 * P:4 * P], m + 1)
                dve.memset(xfa[:, :, P:P + 1], 1.0)
                dve.memset(eo[:, :, P:P + 1], 1.0)
                layernorm(xn, xfa[:, :, 0:P], norm_aff[:, 0, :], norm_aff[:, 1, :], m + 2)
                evacuate(xfT, r + 1)
                mixture(b)
                for h in range(2):
                    dve.tensor_scalar(KB[h][HD:HD + 1, :], const("spread")[HD:HD + 1, :], 0.0, 1.0,
                                      ALU.mult, ALU.add)
                layernorm(x, xn[:, :, :], mod[:, 1, P:2 * P], mod[:, 1, 0:P], m + 3)
                evacuate(hT[:, 1:T + 1], r + 3)
                attention(1, b)
                layernorm(x, xn[:, :, :], mod[:, 1, 4 * P:5 * P], mod[:, 1, 3 * P:4 * P], m + 4)
                evacuate(hT[:, 1:T + 1], r + 4)
                experts(b)

        @block.gpsimd
        def _(pool):
            with pool.Fori(0, NB) as b:
                with pool.Fori(0, PAIRS) as p:
                    n = b * PAIRS + p
                    pool.wait_ge(S[1]["v_out"], n + 1)
                    pool.wait_ge(S[1]["u_full"], 1 + 2 * n)
                    for t in reversed(range(NT - 2)):
                        after = V1[:, t + 2, :, :] if t == NT - 3 else Vlater[:, t + 1, :, :]
                        ins = pool.tensor_tensor(Vlater[:, t, :, :], after, V1[:, t + 1, :, :], ALU.add)
                        if t:
                            ins.then_inc(xw_ones, 1)
                            pool.wait_ge(xw_ones, n * (NT - 3) + NT - 2 - t)
                    ins.then_inc(later, 1)


def const_array():
    import numpy as np
    c = np.zeros((P, CONST_TOTAL), np.float32)

    def put(name, a):
        c[:, CONST_AT[name]:CONST_AT[name] + CONST_COLS[name]] = a

    p = np.arange(P)[:, None]
    q = np.arange(P)[None, :]
    put("ident", p == q)
    put("neg", np.where(q > p, -1e30, 0.0))
    put("mask", p > q)
    put("quad", (p // 32 == q // 32) & (p % 32 < NC))
    put("minus_lo", -1.0 * (p % 32 >= NC))
    put("first", np.broadcast_to(E1 - np.arange(E1)[None, :], (P, E1)))
    rows = np.full((P, NT), EPS_MASK)
    rows[P - 1, NT - 1] = -3e38
    put("eps_row", rows)
    t = np.arange(NT)[None, :, None]
    col = np.arange(32)[None, None, :]
    put("chunk", ((col % NC) == 2 * t + (np.arange(P) // CHUNK)[:, None, None]).reshape(P, NT * 32))
    k = np.arange(T)[None, :]
    put("spread", (p % NC) == k // CHUNK)
    sel = np.zeros((E1, E1, P), np.float32)
    for e in range(E1):
        sel[e, e, :] = 1.0
    return c, sel


def host_arrays(inp):
    import numpy as np
    g = lambda n: np.asarray(inp[n])
    c, sel = const_array()
    a = {"consts": c, "sel": sel, "hidden": g("L0_attn_hidden_states")}
    a["c"] = np.stack([g("L0_c"), g("L1_c")], -1)
    a["wmod"] = np.stack([g("L0_wmod"), g("L1_wmod")], 1)
    a["wq0"] = g("L0_attn_w_q").T.reshape(P, HEADS, HD)
    a["wk0"] = g("L0_attn_w_k").T.reshape(P, GROUPS, HD)
    a["wv0"] = g("L0_attn_w_v").T
    a["wo0"] = g("L0_attn_w_o").T.reshape(PAIRS, P, P).transpose(1, 0, 2)
    a["kgen_w"] = g("L0_attn_w_kgen").T
    a["kgen_b"] = g("L0_attn_b_kgen")
    a["conv_w"] = g("L0_attn_w_conv")[:, 0, :]
    a["conv_b"] = g("L0_attn_b_conv")[:, None]
    for n in ("norm_g", "norm_b", "slot_g", "slot_b", "scale"):
        a[n] = g(f"L0_ffn_{n}")
    a["slots"] = g("L0_ffn_slot_embeds").reshape(NT, P, P).transpose(1, 0, 2)
    for n in ("Wg", "Wu", "Wd", "bd"):
        a[n] = g(f"L0_ffn_{n}")
    a["bgu"] = np.stack([g("L0_ffn_bg").reshape(E0, 2, P), g("L0_ffn_bu").reshape(E0, 2, P)], 1).transpose(0, 3, 1, 2)
    a["wq1"] = g("L1_attn_W_query").transpose(1, 0, 2)
    a["wk1"] = g("L1_attn_W_key").transpose(1, 0, 2)
    a["wv1"] = g("L1_attn_W_values").transpose(1, 0, 2).reshape(P, HEADS * HD)
    a["wo1"] = g("L1_attn_W_output").reshape(PAIRS, P, P).transpose(1, 0, 2)
    a["bq1"] = g("L1_attn_Bias_query")[None]
    a["bk1"] = g("L1_attn_Bias_key")[None]
    a["bv1"] = g("L1_attn_Bias_values").reshape(1, HEADS * HD)
    a["bo1"] = g("L1_attn_Bias_output")[None]
    a["router"] = g("L1_ffn_router_w").T
    a["gate_up"] = g("L1_ffn_gate_up_proj")
    a["down"] = g("L1_ffn_down_proj")
    a["wsh"] = np.concatenate([g("L1_ffn_shared_gate_w").T, g("L1_ffn_shared_up_w").T,
                               g("L1_ffn_shared_down_w").T.reshape(SF // P, P, P).transpose(1, 0, 2).reshape(P, SF)], 1)
    return {n: np.ascontiguousarray(v) for n, v in a.items()}


def kernel(**inputs):
    import concourse.bacc as _bacc
    from concourse.bass_utils import run_bass_kernel_spmd as _run

    nc = _bacc.Bacc("TRN2", target_bir_lowering=False, num_devices=1)
    arrays = {f"in_{n}": a for n, a in host_arrays(inputs).items()}
    A = {n[3:]: nc.dram_tensor(n, a.shape, mybir.dt.from_np(a.dtype), kind="ExternalInput").ap()
         for n, a in arrays.items()}
    out = nc.dram_tensor("out_0", (NB, T, P), F32, kind="ExternalOutput").ap()
    layer_program(nc, A, out)
    r = _run(nc, [arrays], core_ids=[0])
    return r.results[0]["out_0"]
```

```python
from contextlib import ExitStack

import concourse.bass as bass
from concourse import mybir
from concourse.alu_op_type import AluOpType as ALU

F32 = mybir.dt.float32
FR = mybir.dt.float32r
BF16 = mybir.dt.bfloat16
I32 = mybir.dt.int32
ACT = mybir.ActivationFunctionType
AX = mybir.AxisListType.X
ds = bass.ds

P = 128
NB = 2
T = 1024
NT = T // P
BANK = 512
HALF = T // BANK
HD = 64
HEADS = 16
PAIRS = HEADS // 2
GH = 4
GROUPS = HEADS // GH
CHUNK = 64
NC = T // CHUNK
E0, F0, SLOTS = 16, 256, 64
E1, F1, SF = 16, 128, 512
QSCALE = HD ** -0.5
EPS_LN = 1e-5
EPS_MASK = 1e-10
EPS_TOTAL = 1e-9
CQ = NC // 2

CONST_COLS = {"ident": 128, "neg": 128, "mask": 128, "first": 16,
              "eps_row": NT, "chunk": 4 * 32, "spread": T, "own_chunk": T}
CONST_AT = {}
_at = 0
for _name, _cols in CONST_COLS.items():
    CONST_AT[_name] = _at
    _at += _cols
CONST_TOTAL = _at

UNITS1 = E1 + SF // F1

LN_STEPS = 4
MOD_STEPS = 9
CONV_STEPS = 7
NORM_STEPS = 8
ROUTE_STEPS = 5


def layer_program(nc, A, out):
    ctx = ExitStack()
    with ctx:
        def sb(name, shape, dt=F32):
            return ctx.enter_context(nc.sbuf_tensor(name, shape, dt))

        def sem(name):
            return ctx.enter_context(nc.semaphore(name))

        consts = sb("consts", [P, CONST_TOTAL])

        def const(name, lo=0, hi=None):
            at = CONST_AT[name]
            return consts[:, at + lo:at + (CONST_COLS[name] if hi is None else hi)]

        ident = const("ident")
        ident_b = sb("ident_b", [P, P], BF16)
        neg_b = sb("neg_b", [P, P], BF16)
        chunk_sum = const("chunk").rearrange("p (a c) -> p a c", a=4)
        ones_row = sb("ones_row", [1, BANK])
        eps_col = sb("eps_col", [P, 2])

        x = sb("x", [P, NT, P])
        xn = sb("xn", [P, NT, P])
        hT = sb("hT", [P, T + 2])
        att_in = sb("att_in", [P, T])
        stats = sb("stats", [P, NT, 6])
        mv = sb("mv", [P, NT, 2])
        std = sb("std", [P, NT])
        rstd = sb("rstd", [P, NT])
        ccol = sb("ccol", [P, 2])
        scol = sb("scol", [P, 2])
        sc_b = sb("sc_b", [P, 2, P])
        mod = sb("mod", [P, 2, 6 * P])

        conv_w = sb("conv_w", [P, 3])
        conv_b = sb("conv_b", [P, 1])
        kgen_w = sb("kgen_w", [P, 3])
        kgen_b = sb("kgen_b", [P, 3])
        ctx_sum = sb("ctx_sum", [P, 1])
        ctx_b = sb("ctx_b", [P, P])
        dyn = sb("dyn", [P, 3])
        dsig = sb("dsig", [P, 3])
        dsum = sb("dsum", [P, 1])
        gate = sb("gate", [P, 1])

        wq_s = sb("wq_s", [P, 4, P])
        wk_s = sb("wk_s", [P, 4, P])
        wv_s = sb("wv_s", [P, 256])
        bq = sb("bq", [P, HEADS])
        bk = sb("bk", [P, HEADS])
        bv_s = sb("bv_s", [1, 256])
        wo = sb("wo", [P, PAIRS, P])
        bo1 = sb("bo1", [1, P])
        QA = [sb(f"QA{i}", [P, T], FR) for i in range(2)]
        QB = [sb(f"QB{i}", [P, T], FR) for i in range(2)]
        KA = [sb(f"KA{i}", [P, T], FR) for i in range(2)]
        KB = [sb(f"KB{i}", [P, T], FR) for i in range(2)]
        V0 = [sb(f"V0{i}", [P, NT, HD]) for i in range(2)]
        V1 = [sb(f"V1{i}", [P, NT, 2, P]) for i in range(2)]
        Vlater = sb("Vlater", [P, NT - 2, 2, P])
        E = sb("E", [P, NT, T])
        U = sb("U", [P, PAIRS, T])
        mx = sb("mx", [P, NT, NC])
        mrow1 = sb("mrow1", [P, NT, 2])
        mtop1 = sb("mtop1", [P, NT])
        mx1 = sb("mx1", [P, NT])
        spread = sb("spread", [P, T], FR)
        S_sb = sb("S_sb", [P, BANK])
        r0 = sb("r0", [P, 4, 4, CQ])
        sw = sb("sw", [P, 4, 4, CQ])
        r1 = sb("r1", [P, 4, 4, CQ])
        tot = sb("tot", [P, 4, 2])
        rhi = sb("rhi", [P, 4, 4, CQ], FR)
        rp = sb("rp", [P, 4, 4, 32])
        r_parts = sb("r_parts", [P, BANK], FR)
        F = att_in
        lnd = xn[:, :, :].rearrange("p t d -> p (t d)")
        gsign = U[:, 3, 0:4 * P].rearrange("p (l h d) -> p l h d", l=2, h=2)
        gabs = U[:, 3, 4 * P:8 * P].rearrange("p (l h d) -> p l h d", l=2, h=2)

        seT = sb("seT", [P, T])
        slot_aff = sb("slot_aff", [P, 2, P])
        norm_aff = sb("norm_aff", [P, 2, P])
        scale_b = sb("scale_b", [P, 1])
        xfT = U[:, 0, :]
        slT = U[:, 1, :]
        slot_tok = U[:, 2, :].rearrange("p (t d) -> p t d", t=NT)
        neg_rows = [att_in[0:1, :], Vlater[0:1, :, :, :].rearrange("p t h d -> p (t h d)")[:, 0:T]]
        Uf = U[:, :, :].rearrange("p n t -> p (n t)")
        u_at = [3 * T]

        def in_u(cols, rows=P):
            at = u_at[0]
            u_at[0] += cols
            assert u_at[0] <= PAIRS * T
            return Uf[0:rows, at:at + cols]

        xfa = in_u(NT * (P + 1)).rearrange("p (t d) -> p t d", t=NT)
        eo = in_u(NT * (P + 1)).rearrange("p (t d) -> p t d", t=NT)
        mxs = sb("mxs", [P, 2, NT])
        rsl = sb("rsl", [P, NT])
        wg_s = [in_u(F0) for _ in range(2)]
        wu_s = [in_u(F0) for _ in range(2)]
        wd_s = [in_u(F0).rearrange("p (h d) -> p h d", h=2) for _ in range(2)]
        bgu_s = [sb(f"bgu_s{i}", [P, 2, 2]) for i in range(2)]
        bd_s = [sb(f"bd_s{i}", [1, P]) for i in range(2)]
        gel = [sb(f"gel{i}", [P, 2, SLOTS]) for i in range(2)]
        act0 = [sb(f"act0{i}", [P, 2, SLOTS]) for i in range(2)]

        router = sb("router", [P, E1])
        lg = sb("lg", [P, NT, E1])
        top = sb("top", [P, NT])
        eq = sb("eq", [P, NT, E1])
        best = sb("best", [P, NT])
        sig = sb("sig", [P, NT])
        sc_tok = sb("sc_tok", [P, NT, E1])
        scT = U[0:E1, 0, :]
        wgu1 = [U[:, 1, i * 4 * P:i * 4 * P + 2 * P] for i in range(2)]
        wd1 = [U[:, 1, i * 4 * P + 2 * P:i * 4 * P + 3 * P] for i in range(2)]
        sel1 = [U[0:E1, 1, i * 4 * P + 3 * P:(i + 1) * 4 * P] for i in range(2)]
        zero_row = U[0:1, 2, 0:BANK]
        xs1 = [E[:, i, :] for i in range(2)]
        sg1 = [E[:, 2 + i, :] for i in range(2)]
        ac1 = [E[:, 4 + i, :] for i in range(2)]
        wmod = U[:, 4:6, :].rearrange("p a b -> p (a b)")[:, 0:12 * P].rearrange("p (l n) -> p l n", l=2)
        wsh = E[:, 6:8, :].rearrange("p a b -> p (a b)")[:, 0:3 * SF]

        PS = ctx.enter_context(nc.psum_tensor("PS", [P, 8 * BANK], F32))

        def banks(first, cols=T, lo=0, rows=P):
            return PS[0:rows, first * BANK + lo:first * BANK + lo + cols]

        s_const = sem("s_const")
        s_prep = sem("s_prep")
        s_x = sem("s_x")
        s_c = sem("s_c")
        s_out = sem("s_out")
        s_held = sem("s_held")
        s_silu = sem("s_silu")
        s_scb = sem("s_scb")
        s_mod_ps = sem("s_mod_ps")
        s_mod = sem("s_mod")
        ln_var = sem("ln_var")
        ln_std = sem("ln_std")
        ln_link = sem("ln_link")
        ln_out = sem("ln_out")
        tr_ps = sem("tr_ps")
        tr_out = sem("tr_out")
        cv_link = sem("cv_link")
        cv_ctx = sem("cv_ctx")
        cv_dyn = sem("cv_dyn")
        cv_pre = sem("cv_pre")
        cv_sig = sem("cv_sig")
        cv_out = sem("cv_out")

        def layer_sems(names):
            return [{n: sem(f"{n}_{L}") for n in ("wo_in " + names).split()} for L in range(2)]

        S = layer_sems("w_in proj_q q_hi q_lo proj_k k_hi k_lo proj_v v_out p1_full p1_max "
                       "m_both m_top mt_ps m_rows p2_full p2_f p2_exp u_full u_out o_full")
        s_full = sem("s_full")
        nr_link = sem("nr_link")
        s_copy = sem("s_copy")
        st_ps = sem("st_ps")
        rp_out = sem("rp_out")
        rb_ps = sem("rb_ps")
        s_rr = sem("s_rr")
        p3_full = sem("p3_full")
        p3_mul = sem("p3_mul")
        k_copy = sem("k_copy")
        v_copy = sem("v_copy")
        later = sem("later")
        f_exp = sem("f_exp")
        diag = sem("diag")
        u_ln = sem("u_ln")
        u_inv = sem("u_inv")
        res_link = sem("res_link")

        lg_full = sem("lg_full")
        lg_max = sem("lg_max")
        nm_ps = sem("nm_ps")
        nm_out = sem("nm_out")
        ex_full = sem("ex_full")
        ex_out = sem("ex_out")
        sl_full = sem("sl_full")
        sl_link = sem("sl_link")
        sl_out = sem("sl_out")
        xw = [sem(f"xw{i}") for i in range(2)]
        xf_full = sem("xf_full")
        xf_gel = sem("xf_gel")
        xf_act = sem("xf_act")
        xd_full = sem("xd_full")
        xd_out = sem("xd_out")
        cb_full = sem("cb_full")
        xw_ones = sem("xw_ones")

        rt_full = sem("rt_full")
        rt_link = sem("rt_link")
        rt_sig_in = sem("rt_sig_in")
        rt_sig = sem("rt_sig")
        rt_out = sem("rt_out")
        rt_ps = sem("rt_ps")
        rt_T = sem("rt_T")
        yw = [sem(f"yw{i}") for i in range(2)]
        shw = sem("shw")
        y_sc = sem("y_sc")
        y_xs = sem("y_xs")
        y_gate = sem("y_gate")
        y_up = sem("y_up")
        y_silu = sem("y_silu")
        y_act = sem("y_act")
        y_dn = sem("y_dn")

        start_at_one = [s_out, s_full, xd_full, y_dn, p3_mul, f_exp, k_copy, v_copy, xf_act, xd_out, y_gate,
                        y_silu, y_act, y_xs, later]
        start_at_one += [S[L][name] for L in range(2) for name in ("proj_v", "proj_q", "proj_k", "q_hi", "q_lo", "k_hi", "k_lo", "v_out", "p1_max",
                                                               "p2_exp", "o_full", "u_out", "u_full")]

        class Chain:

            def __init__(self, eng, semaphore, base):
                self.eng, self.semaphore, self.base, self.n = eng, semaphore, base, 0

            def done(self, ins):
                ins.then_inc(self.semaphore, 1)
                self.n += 1
                self.eng.wait_ge(self.semaphore, self.base + self.n)

        block = ctx.enter_context(nc.Block())

        LN_CALLS = 5
        TR_CALLS = 5

        @block.sync
        def _(sp):
            for dst, src in [(consts[:, :], A["consts"]), (conv_w[:, :], A["conv_w"]), (conv_b[:, :], A["conv_b"]),
                             (kgen_w[:, :], A["kgen_w"]), (kgen_b[:, :], A["kgen_b"].partition_broadcast(P)),
                             (bo1[:, :], A["bo1"]),
                             (bq[0:HD, :], A["bq1"]), (bq[HD:P, :], A["bq1"]), (bk[0:HD, :], A["bk1"]), (bk[HD:P, :], A["bk1"]),
                             (slot_aff[:, 0, :], A["slot_g"].partition_broadcast(P)),
                             (slot_aff[:, 1, :], A["slot_b"].partition_broadcast(P)),
                             (scale_b[:, :], A["scale"].partition_broadcast(P)),
                             (norm_aff[:, 0, :], A["norm_g"].partition_broadcast(P)),
                             (norm_aff[:, 1, :], A["norm_b"].partition_broadcast(P)),
                             (router[:, :], A["router"]),
                             (x[:, :, :], A["slots"])]:
                sp.dma_start(dst, src).then_inc(s_const, 16)
            for q in start_at_one:
                sp.sem_inc(q, 1)
            sp.wait_ge(ln_out, 1)
            with sp.Fori(0, NB) as b:
                sp.wait_ge(s_out, 1 + b * 16)
                sp.dma_start(x[:, :, :], A["hidden"][ds(b, 1)].squeeze(0).rearrange("(t p) d -> p t d", p=P)).then_inc(s_x, 16)
                sp.dma_start(ccol[:, :], A["c"][ds(b, 1)].squeeze(0)).then_inc(s_c, 16)
                sp.dma_start(wmod[:, :, :], A["wmod"]).then_inc(s_c, 16)
                for L in range(2):
                    v_used = sp.snap(1 + (b + L) * (GROUPS * (2 if L == 0 else 1)))
                    q_used = sp.snap(1 + (b + L) * (GROUPS * 4))
                    k_used = sp.snap(1 + (b + L) * (GROUPS * (4 if L == 0 else 1)))
                    wo_used = sp.snap(1 + b + L)
                    sp.wait_ge(S[1 - L]["proj_v"], v_used)
                    sp.sem_inc(s_held, 1)
                    sp.wait_ge(S[1 - L]["proj_q"], q_used)
                    sp.sem_inc(s_held, 1)
                    sp.wait_ge(S[1 - L]["proj_k"], k_used)
                    sp.sem_inc(s_held, 1)
                    sp.wait_ge(S[1 - L]["o_full"], wo_used)
                    sp.sem_inc(s_held, 1)
                    sp.dma_start(wo[:, :, :], A[f"wo{L}"]).then_inc(S[L]["wo_in"], 16)
                    with sp.Fori(0, GROUPS) as g:
                        v_used = sp.snap(1 + (b * GROUPS + g) * (1 if L == 0 else 4))
                        q_used = sp.snap(1 + (b * GROUPS + g) * 4)
                        sp.wait_ge(S[L]["proj_v" if L == 0 else "proj_k"], v_used)
                        sp.wait_ge(S[L]["proj_q"], q_used)
                        sp.sem_inc(s_held, 1)
                        w_in = S[L]["w_in"]
                        for half in range(2):
                            cols = slice(half * HD, half * HD + HD)
                            sp.dma_start(wq_s[:, :, cols], A[f"wq{L}"][:, ds(g * 4, 4), :]).then_inc(w_in, 16)
                            if L == 0:
                                sp.dma_start(wk_s[:, 0, cols], A["wk0"][:, ds(g, 1), :].squeeze(1)).then_inc(w_in, 16)
                            else:
                                sp.dma_start(wk_s[:, :, cols], A["wk1"][:, ds(g * 4, 4), :]).then_inc(w_in, 16)
                        if L == 0:
                            sp.dma_start(wv_s[:, 0:HD], A["wv0"][:, ds(g * HD, HD)]).then_inc(w_in, 16)
                        else:
                            sp.dma_start(wv_s[:, :], A["wv1"][:, ds(g * 256, 256)]).then_inc(w_in, 16)
                            sp.dma_start(bv_s[:, :], A["bv1"][:, ds(g * 256, 256)]).then_inc(w_in, 16)
                    if L == 0:
                        with sp.Fori(0, E0 // 2) as j:
                            for i in range(2):
                                sp.wait_ge(S[0]["o_full"], 1 + b + 1)
                                sp.sem_inc(s_held, 1)
                                sp.wait_ge(xd_full, 1 + b * (E0 // 2) + j)
                                e = j * 2 + i
                                sp.dma_start(wg_s[i], A["Wg"][ds(e, 1)].squeeze(0)).then_inc(xw[i], 16)
                                sp.dma_start(wu_s[i], A["Wu"][ds(e, 1)].squeeze(0)).then_inc(xw[i], 16)
                                sp.dma_start(wd_s[i], A["Wd"][ds(e, 1)].squeeze(0).rearrange("(h p) d -> p h d", p=P)).then_inc(xw[i], 16)
                                sp.dma_start(bgu_s[i][:, :, :], A["bgu"][ds(e, 1)].squeeze(0)).then_inc(xw[i], 16)
                                sp.dma_start(bd_s[i][:, :], A["bd"][ds(e, 1)]).then_inc(xw[i], 16)
                    else:
                        sp.wait_ge(S[1]["o_full"], 1 + b + 1)
                        sp.dma_start(wsh, A["wsh"]).then_inc(shw, 16)
                        with sp.Fori(0, E1 // 2) as j:
                            for i in range(2):
                                sp.wait_ge(y_gate, 1 + b * UNITS1 + j * 2 + i)
                                e = j * 2 + i
                                sp.dma_start(wgu1[i], A["gate_up"][ds(e, 1)].squeeze(0)).then_inc(yw[i], 16)
                                sp.dma_start(wd1[i], A["down"][ds(e, 1)].squeeze(0)).then_inc(yw[i], 16)
                                sp.dma_start(sel1[i], A["sel"][ds(e, 1)].squeeze(0)).then_inc(yw[i], 16)
                sp.wait_ge(res_link, (b + 1) * 8)
                sp.dma_start(out[ds(b, 1)].squeeze(0).rearrange("(t p) d -> p t d", p=P), x[:, :, :]).then_inc(s_out, 16)
            sp.wait_ge(s_out, 1 + NB * 16)

        @block.tensor
        def _(pe):
            def transposed(src, m):
                for t in range(NT):
                    mm = pe.transpose(banks(0, P, t * P), src(t), ident)
                mm.then_inc(tr_ps, 1)

            def attention(L, b):
                s = S[L]
                x_in = att_in if L == 0 else hT[:, 1:T + 1]
                m_rows_n = NC if L == 0 else 1
                krows = HD + m_rows_n
                b1 = (5, 6) if L == 0 else (4, 5)
                b_out = 7 if L == 0 else 6
                b1_units = 2 * NT if L == 0 else NT + NT // 2
                h0 = b * HEADS
                g0 = b * GROUPS

                def project(i, g, u):
                    n = h0 + i
                    if u == 0:
                        if L == 0:
                            pe.wait_ge(cv_out, b + 1)
                        else:
                            pe.wait_ge(tr_out, 1 + b * TR_CALLS + 4)
                        pe.wait_ge(s["w_in"], (g0 + g + 1) * (80 if L == 0 else 96))
                    for half in range(2):
                        mm = pe.matmul(banks(half, BANK), wq_s[:, u, :], x_in[:, half * BANK:(half + 1) * BANK],
                                       start=True, stop=True)
                    mm.then_inc(s["proj_q"], 1)
                    if L == 1 or u == 0:
                        if L == 0:
                            pe.wait_ge(k_copy, 1 + g0 + g)
                        for half in range(2):
                            mm = pe.matmul(banks(2 + half, BANK), wk_s[:, u * L, :],
                                           x_in[:, half * BANK:(half + 1) * BANK], start=True, stop=True)
                        mm.then_inc(s["proj_k"], 1)
                    if L == 0 and u == 0:
                        pe.wait_ge(v_copy, 1 + g0 + g)
                        pe.wait_ge(s["u_out"], 1 + u_before(i))
                        for t in range(NT):
                            mm = pe.matmul(banks(7, HD, t * HD), x_in[:, t * P:(t + 1) * P], wv_s[:, 0:HD],
                                           start=True, stop=True)
                        mm.then_inc(s["proj_v"], 1)
                    if L == 1 and u % 2 == 0:
                        if not isinstance(i, int) or i >= 2:
                            pe.wait_ge(s["m_rows"], n)
                        for t in range(NT):
                            pe.matmul(banks(4, P, t * P), x_in[:, t * P:(t + 1) * P],
                                      wv_s[:, u * HD:u * HD + P], start=True, stop=False)
                            mm = pe.matmul(banks(4, P, t * P), ones_row[:, 0:P], bv_s[:, u * HD:u * HD + P],
                                           start=False, stop=True)
                        mm.then_inc(s["proj_v"], 1)

                def u_before(i):
                    return h0 if isinstance(i, int) and i == 0 else h0 + i - 2

                def maxima(i, g, u, units):
                    n = h0 + i
                    q = QB[u % 2]
                    k = KA[1 if u == 0 else 0] if L == 0 else KA[u % 2]
                    for x in units:
                        if L == 0:
                            t, half = divmod(x, 2)
                        else:
                            t, half = (x, 0) if x < NT // 2 else divmod(x + NT // 2, 2)
                        lo, hi = half * BANK, (half + 1) * BANK
                        if L == 1:
                            hi = min(hi, (t + 1) * P)
                        if x >= 2:
                            pe.wait_ge(s["p1_max"], 1 + n * b1_units + x - 1)
                        own = L == 1 and hi == (t + 1) * P
                        mm = pe.matmul(banks(b1[x % 2], hi - lo), q[0:HD, t * P:(t + 1) * P], k[0:HD, lo:hi],
                                       start=True, stop=not own)
                        if own:
                            mm = pe.matmul(banks(b1[x % 2], P, hi - lo - P), ident_b[:, :], neg_b[:, :],
                                           start=False, stop=True)
                        mm.then_inc(s["p1_full"], 1)

                def maxima_ready(i, g, u):
                    n = h0 + i
                    n_k = g0 + g + 1 if L == 0 else n + 1
                    pe.wait_ge(s["q_hi"], 1 + n + 1)
                    pe.wait_ge(s["q_lo"], 1 + n + 1)
                    pe.wait_ge(s["k_hi"], 1 + n_k)
                    pe.wait_ge(s["k_lo"], 1 + n_k)

                def turn_maxima(i):
                    n = h0 + i
                    if L == 0:
                        pe.wait_ge(s["p1_max"], 1 + (n + 1) * b1_units)
                    else:
                        pe.wait_ge(s["m_top"], n + 1)
                    for t in range(NT):
                        src = mx[:, t, :] if L == 0 else mx1[:, t:t + 1]
                        mm = pe.transpose(banks(b1[0], P, t * P, rows=m_rows_n), src, ident)
                    mm.then_inc(s["mt_ps"], 1)

                def chunk_sums(i, a):
                    pe.wait_ge(s["p2_exp"], 1 + (h0 + i) * NT + 2 * a + 2)
                    for half in range(2):
                        for odd in range(2):
                            j = 2 * half + odd
                            mm = pe.matmul(PS[32 * j:32 * j + 32, 4 * BANK:5 * BANK], chunk_sum[:, a, :],
                                           E[:, 2 * a + odd, half * BANK:(half + 1) * BANK],
                                           start=(a == 0), stop=(a == 3))
                    return mm

                def values0(i, t):
                    pe.wait_ge(p3_mul, 1 + (h0 + i) * NT + t + 1)
                    for half in range(2):
                        mm = pe.matmul(PS[HD * half:HD * half + HD, 7 * BANK:8 * BANK], V0[0][:, t, :],
                                       E[:, t, half * BANK:(half + 1) * BANK],
                                       start=(t == 0), stop=(t == NT - 1))
                    return mm

                def head(i, g, u, has_next, has_second):
                    n = h0 + i
                    par = u % 2
                    kk = 0 if L == 0 else par
                    g1, u1 = (g, u + 1) if u < GH - 1 else (g + 1, 0)
                    g2, u2 = (g, u + 2) if u < GH - 2 else (g + 1, u - 2)
                    pe.wait_ge(s["m_rows"], n + 1)
                    if L == 0 and u == 0:
                        pe.wait_ge(k_copy, 1 + g0 + g + 1)
                    if has_next:
                        maxima_ready(i + 1, g1, u1)
                    per = b1_units // NT + (1 if L == 1 else 0)
                    done = 0
                    for t in range(NT):
                        first = 2 * (t % 2)
                        if t >= 2:
                            pe.wait_ge(s["p2_exp"], 1 + n * NT + t - 1)
                        spans = []
                        for half in range(2):
                            lo, hi = max(half * BANK, 0 if L == 0 else t * P), (half + 1) * BANK
                            if lo < hi:
                                spans.append((lo, hi))
                        for lo, hi in spans:
                            pe.matmul(banks(first, hi - lo, lo), KA[kk][:, t * P:(t + 1) * P], QA[par][:, lo:hi],
                                      start=True, stop=False)
                        for lo, hi in spans:
                            mm = pe.matmul(banks(first, hi - lo, lo), KB[kk][0:krows, t * P:(t + 1) * P],
                                           QB[par][0:krows, lo:hi], start=False, stop=True)
                        mm.then_inc(s["p2_full"], 1)
                        if has_next:
                            todo = range(done, min(b1_units, done + per))
                            maxima(i + 1, g1, u1, todo)
                            done += len(todo)
                        if L == 0 and t >= 2 and t % 2 == 0:
                            chunk_sums(i, t // 2 - 1)
                    if L == 0:
                        chunk_sums(i, 3).then_inc(s_full, 1)
                    else:
                        pe.wait_ge(s["p2_exp"], 1 + n * NT + NT - 1)
                        for half in range(2):
                            mm = pe.matmul(banks(half, BANK), KB[par][HD:HD + 1, 0:P],
                                           QB[par][HD:HD + 1, half * BANK:(half + 1) * BANK], start=True, stop=True)
                        mm.then_inc(s["p2_f"], 1)
                    if has_next:
                        turn_maxima(i + 1)
                    if has_second:
                        pe.wait_ge(s["p2_exp"], 1 + (n + 1) * NT)
                        if L == 1:
                            pe.wait_ge(f_exp, 1 + n + 1)
                        project(i + 2, g2, u2)
                    if L == 0:
                        pe.wait_ge(s_copy, n + 1)
                        if has_next:
                            pe.wait_ge(s["m_rows"], n + 2)
                        for k in range(4):
                            mm = pe.transpose(banks(5, P, k * P), S_sb[:, k * P:(k + 1) * P], ident)
                        mm.then_inc(st_ps, 1)
                        pe.wait_ge(rp_out, n + 1)
                        for k in range(4):
                            mm = pe.transpose(banks(6, P, k * P), rp[:, k, :, :].rearrange("p j c -> p (j c)"), ident)
                        mm.then_inc(rb_ps, 1)
                        pe.wait_ge(s_rr, n + 1)
                        if has_second and u2 == 0:
                            pe.wait_ge(s["k_hi"], 1 + g0 + g2 + 1)
                            pe.wait_ge(s["k_lo"], 1 + g0 + g2 + 1)
                            pe.wait_ge(s["v_out"], 1 + g0 + g2 + 1)
                        if u == 0:
                            pe.wait_ge(v_copy, 1 + g0 + g + 1)
                        pe.wait_ge(s["u_out"], 1 + n)
                        for t in range(NT):
                            first = 2 - 2 * (t % 2)
                            if t >= 2:
                                pe.wait_ge(p3_mul, 1 + n * NT + t - 1)
                            if t == 1 and has_second:
                                pe.wait_ge(s["q_hi"], 1 + n + 3)
                                pe.wait_ge(s["q_lo"], 1 + n + 3)
                            for half in range(2):
                                q = 32 * (2 * half + t % 2)
                                mm = pe.matmul(banks(first + half, BANK), spread[q:q + 2 * CQ, t * P:(t + 1) * P],
                                               r_parts[q:q + 2 * CQ, :], start=True, stop=True,
                                               tile_position=(q, 0))
                            mm.then_inc(p3_full, 1)
                            if t >= 1:
                                values0(i, t - 1)
                        values0(i, NT - 1).then_inc(s["u_full"], 1)
                    else:
                        pe.wait_ge(later, 1 + pairs_before(g, u) + 1)
                        pe.wait_ge(diag, n + 1)
                        pe.wait_ge(s["u_out"], 1 + n)
                        v1 = V1[u // 2]
                        for t in range(NT):
                            for half in range(2):
                                lo, hi = max(half * BANK, t * P), (half + 1) * BANK
                                if lo < hi:
                                    pe.matmul(banks(6, hi - lo, lo), v1[:, t, par, :], E[:, t, lo:hi],
                                              start=(t == 0), stop=False, skip_group_check=True)
                        for t in range(NT - 1):
                            v = v1[:, t + 1, par, :] if t == NT - 2 else Vlater[:, t, par, :]
                            mm = pe.matmul(banks(6, P, t * P), v, F[:, t * P:(t + 1) * P], start=False,
                                           stop=(t in (3, NT - 2)), skip_group_check=True)
                        mm.then_inc(s["u_full"], 1)
                        if has_second:
                            pe.wait_ge(s["q_lo"], 1 + n + 3)
                            pe.wait_ge(s["q_hi"], 1 + n + 3)
                            pe.wait_ge(s["k_lo"], 1 + n + 3)
                            pe.wait_ge(s["k_hi"], 1 + n + 3)
                            if u % 2 == 0:
                                pe.wait_ge(s["v_out"], 1 + pairs_before(g, u) + 2)

                def pairs_before(g, u):
                    return b * PAIRS + g * 2 + u // 2

                project(0, 0, 0)
                maxima_ready(0, 0, 0)
                if L == 0:
                    pe.wait_ge(s["v_out"], 1 + g0 + 1)
                else:
                    pe.wait_ge(s["v_out"], 1 + b * PAIRS + 1)
                project(1, 0, 1)
                maxima(0, 0, 0, range(b1_units))
                turn_maxima(0)
                pe.wait_ge(s["q_hi"], 1 + h0 + 2)
                pe.wait_ge(s["q_lo"], 1 + h0 + 2)
                if L == 1:
                    pe.wait_ge(s["k_hi"], 1 + h0 + 2)
                    pe.wait_ge(s["k_lo"], 1 + h0 + 2)
                pe.sem_inc(s_held, 1)
                with pe.Fori(0, GROUPS - 1) as g:
                    for u in range(GH):
                        head(g * GH + u, g, u, True, True)
                with pe.Fori(GROUPS - 1, GROUPS) as g:
                    for u in range(GH):
                        head(g * GH + u, g, u, u < GH - 1, u < GH - 2)
                pe.wait_ge(s["u_out"], 1 + (b + 1) * HEADS)
                pe.wait_ge(s["wo_in"], (b + 1) * 16)
                for t in range(NT):
                    for p in range(PAIRS):
                        mm = pe.matmul(banks(0, P, t * P), U[:, p, t * P:(t + 1) * P], wo[:, p, :],
                                       start=(p == 0), stop=(p == PAIRS - 1 and L == 0))
                    if L == 1:
                        mm = pe.matmul(banks(0, P, t * P), ones_row[:, 0:P], bo1[:, :], start=False, stop=True)
                mm.then_inc(s["o_full"], 1)

            def mixture(b):
                pe.wait_ge(tr_out, 1 + b * TR_CALLS + 2)
                for i in range(2 * NT):
                    kind, t = divmod(i, NT)
                    a, c = (xfT, seT) if kind == 0 else (seT, xfT)
                    first = 2 * (i % 2)
                    if i >= 2:
                        pe.wait_ge(lg_max, b * 2 * NT + i - 1)
                    for half in range(2):
                        mm = pe.matmul(banks(first + half, BANK), a[:, t * P:(t + 1) * P],
                                       c[:, half * BANK:(half + 1) * BANK], start=True, stop=True)
                    mm.then_inc(lg_full, 1)
                pe.wait_ge(lg_max, (b + 1) * 2 * NT)
                for kind in range(2):
                    for t in range(NT):
                        mm = pe.transpose(banks(4 + 2 * kind, P, t * P, rows=1), mxs[:, kind, t:t + 1], ident)
                mm.then_inc(nm_ps, 1)
                pe.wait_ge(nm_out, b + 1)

                def exponents(kind):
                    for t in range(NT):
                        i = kind * NT + t
                        a, c = (xfT, seT) if kind == 0 else (seT, xfT)
                        first = 2 * (i % 2)
                        if i >= 2:
                            pe.wait_ge(ex_out, b * 2 * NT + i - 1)
                        for half in range(2):
                            cols = slice(half * BANK, (half + 1) * BANK)
                            pe.matmul(banks(first + half, BANK), a[:, t * P:(t + 1) * P], c[:, cols],
                                      start=True, stop=False)
                            mm = pe.matmul(banks(first + half, BANK), ones_row[:, 0:P], neg_rows[1 - kind][:, cols],
                                           start=False, stop=True)
                        mm.then_inc(ex_full, 1)

                exponents(0)
                pe.wait_ge(ex_out, b * 2 * NT + NT)
                for st in range(NT):
                    for t in range(NT):
                        mm = pe.matmul(banks(4, P + 1, st * 256), E[:, t, st * P:(st + 1) * P], xfa[:, t, :],
                                       start=(t == 0), stop=(t == NT - 1))
                mm.then_inc(sl_full, 1)
                exponents(1)
                pe.wait_ge(sl_out, b + 1)
                pe.wait_ge(ex_out, (b + 1) * 2 * NT)
                transposed(lambda t: slot_tok[:, t, :], None)
                with pe.Fori(0, E0 // 2) as j:
                    pe.wait_ge(tr_out, 1 + b * TR_CALLS + 3)
                    for i in range(2):
                        ex = (b * (E0 // 2) + j) * 2 + i
                        pe.wait_ge(xw[i], (b * (E0 // 2) + j + 1) * 80)
                        pe.wait_ge(xf_act, 1 + ex - i)
                        rhs = slT[:, ds((j * 2 + i) * SLOTS, SLOTS)]
                        for k in range(4):
                            w = (wg_s if k < 2 else wu_s)[i]
                            mm = pe.matmul(banks(i, SLOTS, k * SLOTS), w[:, (k % 2) * P:(k % 2 + 1) * P], rhs,
                                           start=True, stop=True)
                        mm.then_inc(xf_full, 1)
                    pe.wait_ge(xd_out, 1 + b * (E0 // 2) + j)
                    for i in range(2):
                        pe.wait_ge(xf_act, 1 + (b * (E0 // 2) + j) * 2 + i + 1)
                        o = PS[HD * i:HD * i + HD, 2 * BANK:2 * BANK + P]
                        pe.matmul(o, act0[i][:, 0, :], wd_s[i][:, 0, :], start=True, stop=False)
                        pe.matmul(o, act0[i][:, 1, :], wd_s[i][:, 1, :], start=False, stop=False)
                        mm = pe.matmul(o, ones_row[:, 0:SLOTS], bd_s[i][:, :], start=False, stop=True)
                    mm.then_inc(xd_full, 1)
                pe.wait_ge(xd_out, 1 + (b + 1) * (E0 // 2))
                for t in range(NT):
                    for st in range(NT):
                        mm = pe.matmul(banks(4, P + 1, t * 256), E[:, st, t * P:(t + 1) * P], eo[:, st, :],
                                       start=(st == 0), stop=(st == NT - 1))
                mm.then_inc(cb_full, 1)

            def experts(b):
                pe.wait_ge(tr_out, 1 + b * TR_CALLS + 5)
                for t in range(NT):
                    mm = pe.matmul(banks(2, E1, t * E1), hT[:, 1 + t * P:1 + (t + 1) * P], router[:, :],
                                   start=True, stop=True)
                mm.then_inc(rt_full, 1)
                pe.wait_ge(rt_out, b + 1)
                for t in range(NT):
                    mm = pe.transpose(banks(4, P, t * P, rows=E1), sc_tok[:, t, :], ident)
                mm.then_inc(rt_ps, 1)
                pe.wait_ge(rt_T, b + 1)
                for half in range(2):
                    pe.matmul(banks(6 + half, BANK), ones_row[:, 0:P], zero_row, start=True, stop=False,
                              skip_group_check=True)

                def gate_up(y, wg, wu, src):
                    pe.wait_ge(y_silu, 1 + y)
                    for half in range(2):
                        mm = pe.matmul(banks(2 + half, BANK), wg, src[:, half * BANK:(half + 1) * BANK],
                                       start=True, stop=True)
                    mm.then_inc(y_gate, 1)
                    pe.wait_ge(y_act, 1 + y)
                    for half in range(2):
                        mm = pe.matmul(banks(4 + half, BANK), wu, src[:, half * BANK:(half + 1) * BANK],
                                       start=True, stop=True)
                    mm.then_inc(y_up, 1)

                def down(y, a, w):
                    pe.wait_ge(y_act, 1 + y + 1)
                    for t in range(NT):
                        mm = pe.matmul(banks(6, P, t * P), a[:, t * P:(t + 1) * P], w, start=False, stop=False,
                                       skip_group_check=True)
                    mm.then_inc(y_dn, 1)

                def routed(j, i):
                    e = b * E1 + j * 2 + i
                    y = b * UNITS1 + j * 2 + i
                    pe.wait_ge(yw[i], (b * (E1 // 2) + j + 1) * 48)
                    pe.wait_ge(y_xs, 1 + e)
                    for half in range(2):
                        mm = pe.matmul(banks(half, BANK), sel1[i], scT[:, half * BANK:(half + 1) * BANK],
                                       start=True, stop=True)
                    mm.then_inc(y_sc, 1)
                    if i == 1 or not isinstance(j, int):
                        down(y - 1, ac1[1 - i], wd1[1 - i])
                    pe.wait_ge(y_xs, 1 + e + 1)
                    gate_up(y, wgu1[i][:, 0:F1], wgu1[i][:, F1:2 * F1], xs1[i])

                for i in range(2):
                    routed(0, i)
                with pe.Fori(1, E1 // 2) as j:
                    for i in range(2):
                        routed(j, i)
                pe.wait_ge(shw, (b + 1) * 16)
                for k in range(SF // F1):
                    y = b * UNITS1 + E1 + k
                    gate_up(y, wsh[:, k * P:(k + 1) * P], wsh[:, SF + k * P:SF + (k + 1) * P], hT[:, 1:T + 1])
                    if k == 0:
                        down(y - 1, ac1[1], wd1[1])
                    else:
                        down(y - 1, ac1[(k - 1) % 2], wsh[:, 2 * SF + (k - 1) * P:2 * SF + k * P])
                k = SF // F1 - 1
                down(y, ac1[k % 2], wsh[:, 2 * SF + k * P:2 * SF + (k + 1) * P])

            pe.wait_ge(s_const, 17 * 16)
            pe.wait_ge(s_prep, 3)
            pe.wait_ge(ln_out, 1)
            transposed(lambda t: xn[:, t, :], 0)
            with pe.Fori(0, NB) as b:
                pe.wait_ge(s_c, (b + 1) * 32)
                pe.wait_ge(s_scb, b + 1)
                for L in range(2):
                    for half in range(2):
                        mm = pe.matmul(banks(2 * L + half, 3 * P), sc_b[:, L, :],
                                       wmod[:, L, half * 3 * P:(half + 1) * 3 * P], start=True, stop=True)
                mm.then_inc(s_mod_ps, 1)
                pe.wait_ge(ln_out, 1 + b * LN_CALLS + 1)
                transposed(lambda t: xn[:, t, :], 0)
                pe.wait_ge(cv_ctx, b + 1)
                pe.matmul(banks(2, 3), ctx_b[:, :], kgen_w[:, :], start=True, stop=True).then_inc(cv_dyn, 1)
                attention(0, b)
                pe.wait_ge(ln_out, 1 + b * LN_CALLS + 3)
                transposed(lambda t: xfa[:, t, 0:P], 1)
                mixture(b)
                pe.wait_ge(ln_out, 1 + b * LN_CALLS + 4)
                transposed(lambda t: xn[:, t, :], 3)
                attention(1, b)
                pe.wait_ge(ln_out, 1 + b * LN_CALLS + 5)
                transposed(lambda t: xn[:, t, :], 4)
                experts(b)

        @block.scalar
        def _(act):
            def std_of(m):
                act.wait_ge(ln_var, m + 1)
                act.activation(std[:, :], mv[:, :, 1], ACT.Sqrt, bias=eps_col[:, 0:1]).then_inc(ln_std, 1)

            def attention(L, b):
                s = S[L]
                h0 = b * HEADS
                g0 = b * GROUPS

                def high_parts(i, g, u):
                    n = h0 + i
                    act.wait_ge(s["proj_q"], 1 + n + 1)
                    if L == 0:
                        act.activation(QA[u % 2][:, :], banks(0), ACT.Copy)
                        act.activation(QB[u % 2][0:HD, :], banks(0, rows=HD), ACT.Copy).then_inc(s["q_hi"], 1)
                    else:
                        bias = bq[:, ds(i, 1)]
                        act.activation(QA[u % 2][:, :], banks(0), ACT.Identity, bias=bias)
                        act.activation(QB[u % 2][0:HD, :], banks(0, rows=HD), ACT.Identity,
                                       bias=bq[0:HD, ds(i, 1)]).then_inc(s["q_hi"], 1)
                    if L == 0 and u == 0:
                        act.wait_ge(s["proj_k"], 1 + g0 + g + 1)
                        act.activation(KA[1][:, :], banks(2), ACT.Copy).then_inc(s["k_hi"], 1)
                        act.wait_ge(s["proj_v"], 1 + g0 + g + 1)
                        act.activation(V0[1][:, :, :].rearrange("p t d -> p (t d)"), banks(7, BANK),
                                       ACT.Copy).then_inc(s["v_out"], 1)
                    if L == 1:
                        act.wait_ge(s["proj_k"], 1 + n + 1)
                        act.activation(KA[u % 2][:, :], banks(2), ACT.Identity, bias=bk[:, ds(i, 1)]).then_inc(s["k_hi"], 1)
                        if u % 2 == 0:
                            act.wait_ge(s["proj_v"], 1 + b * PAIRS + g * 2 + u // 2 + 1)
                            act.activation(V1[u // 2][:, :, :, 0:HD],
                                           banks(4).rearrange("p (t h d) -> p t h d", t=NT, h=2),
                                           ACT.Copy).then_inc(s["v_out"], 1)

                def head(i, g, u, has_next, has_second):
                    n = h0 + i
                    for t in range(NT):
                        lo = 0 if L == 0 else t * P
                        act.wait_ge(s["p2_full"], n * NT + t + 1)
                        act.activation(E[:, t, lo:T], banks(2 * (t % 2), T - lo, lo), ACT.Exp,
                                       scale=QSCALE).then_inc(s["p2_exp"], 1)
                    if L == 0:
                        act.wait_ge(s_full, 1 + n + 1)
                        act.activation(S_sb[:, :], banks(4, BANK), ACT.Copy).then_inc(s_copy, 1)
                    else:
                        act.wait_ge(s["p2_f"], n + 1)
                        act.activation(F[:, :], banks(0), ACT.Exp, bias=eps_col[:, 1:2], scale=QSCALE).then_inc(f_exp, 1)
                    if has_second:
                        g2, u2 = (g, u + 2) if u < GH - 2 else (g + 1, u - 2)
                        high_parts(i + 2, g2, u2)
                    rows = slice(HD * (u % 2), HD * (u % 2) + HD)
                    if L == 0:
                        act.wait_ge(rb_ps, n + 1)
                        act.activation(r_parts[:, :], banks(6, BANK), ACT.Copy).then_inc(s_rr, 1)
                        act.wait_ge(s["u_full"], 1 + n + 1)
                        for half in range(2):
                            ins = act.activation(U[rows, ds(g * 2 + u // 2, 1), half * BANK:(half + 1) * BANK].squeeze(1),
                                                 PS[HD * half:HD * half + HD, 7 * BANK:8 * BANK], ACT.Copy)
                        ins.then_inc(s["u_out"], 1)
                    else:
                        act.wait_ge(s["u_full"], 1 + n + 1)
                        act.activation(lnd[0:HD, :], PS[HD:P, 6 * BANK:8 * BANK], ACT.Ln).then_inc(u_ln, 1)
                        act.wait_ge(u_ln, n + 1)
                        act.activation(lnd[HD:P, :], lnd[0:HD, :], ACT.Exp, scale=-1.0).then_inc(u_inv, 1)

                high_parts(0, 0, 0)
                high_parts(1, 0, 1)
                with act.Fori(0, GROUPS - 1) as g:
                    for u in range(GH):
                        head(g * GH + u, g, u, True, True)
                with act.Fori(GROUPS - 1, GROUPS) as g:
                    for u in range(GH):
                        head(g * GH + u, g, u, u < GH - 1, u < GH - 2)

            act.wait_ge(s_prep, 3)
            std_of(0)
            with act.Fori(0, NB) as b:
                m = 1 + b * LN_CALLS
                act.wait_ge(s_c, (b + 1) * 32)
                act.activation(scol[:, :], ccol[:, :], ACT.Silu).then_inc(s_silu, 1)
                std_of(m)
                act.wait_ge(cv_pre, b + 1)
                act.activation(dsig[:, :], dyn[:, :], ACT.Sigmoid).then_inc(cv_sig, 1)
                attention(0, b)
                std_of(m + 1)
                std_of(m + 2)
                for i in range(2 * NT):
                    kind, t = divmod(i, NT)
                    act.wait_ge(ex_full, b * 2 * NT + i + 1)
                    act.activation(E[:, t, :], banks(2 * (i % 2)), ACT.Exp).then_inc(ex_out, 1)
                with act.Fori(0, E0 // 2) as j:
                    for i in range(2):
                        act.wait_ge(xf_full, (b * (E0 // 2) + j) * 2 + i + 1)
                        act.activation(gel[i][:, 0, :], banks(i, SLOTS), ACT.Gelu, bias=bgu_s[i][:, 0, 0:1])
                        act.activation(gel[i][:, 1, :], banks(i, SLOTS, SLOTS), ACT.Gelu,
                                       bias=bgu_s[i][:, 0, 1:2]).then_inc(xf_gel, 1)
                    act.wait_ge(xd_full, 1 + b * (E0 // 2) + j + 1)
                    act.activation(eo[:, ds(j, 1), 0:P].squeeze(1), banks(2, P), ACT.Copy).then_inc(xd_out, 1)
                std_of(m + 3)
                attention(1, b)
                std_of(m + 4)
                act.wait_ge(rt_sig_in, b + 1)
                act.activation(sig[:, :], top[:, :], ACT.Sigmoid).then_inc(rt_sig, 1)

                def silu(y, i):
                    act.wait_ge(y_gate, 1 + y + 1)
                    act.activation(sg1[i], banks(2), ACT.Silu).then_inc(y_silu, 1)

                with act.Fori(0, E1 // 2) as j:
                    for i in range(2):
                        silu(b * UNITS1 + j * 2 + i, i)
                for k in range(SF // F1):
                    silu(b * UNITS1 + E1 + k, k % 2)

        @block.vector
        def _(dve):
            def layernorm(src, dst, scale, shift, m):
                step = Chain(dve, ln_link, m * LN_STEPS)
                for t in range(NT):
                    ins = dve.bn_stats(stats[:, t, :], src[:, t, :])
                step.done(ins)
                dve.sem_inc(s_held, 1)
                for t in range(NT):
                    ins = dve.bn_aggr(mv[:, t, :], stats[:, t, :])
                ins.then_inc(ln_var, 1)
                dve.wait_ge(ln_std, m + 1)
                step.done(dve.reciprocal(rstd[:, :], std[:, :]))
                for t in range(NT):
                    ins = dve.tensor_scalar(xn[:, t, :], src[:, t, :], mv[:, t, 0:1], rstd[:, t:t + 1],
                                            ALU.subtract, ALU.mult)
                step.done(ins)
                step.done(dve.tensor_tensor(xn[:, :, :], xn[:, :, :],
                                            scale.unsqueeze(1).to_broadcast([P, NT, P]), ALU.mult))
                dve.tensor_tensor(dst, xn[:, :, :], shift.unsqueeze(1).to_broadcast([P, NT, P]),
                                  ALU.add).then_inc(ln_out, 1)
                dve.wait_ge(ln_out, m + 1)
                assert step.n == LN_STEPS

            def evacuate(dst, m):
                dve.wait_ge(tr_ps, m + 1)
                dve.tensor_copy(dst, banks(0)).then_inc(tr_out, 1)

            def residual(b, k, y, g):
                step = Chain(dve, res_link, b * 8 + 2 * k)
                step.done(dve.tensor_tensor(xn[:, :, :], y, g.unsqueeze(1).to_broadcast([P, NT, P]), ALU.mult))
                step.done(dve.tensor_tensor(x[:, :, :], x[:, :, :], xn[:, :, :], ALU.add))

            def tiles(ap):
                return ap.rearrange("p (t d) -> p t d", t=NT)

            def modulation(b):
                dve.wait_ge(s_silu, b + 1)
                dve.tensor_copy(sc_b[:, :, :], scol[:, :].unsqueeze(2).to_broadcast([P, 2, P])).then_inc(s_scb, 1)
                step = Chain(dve, s_mod, b * MOD_STEPS)
                dve.wait_ge(s_mod_ps, b + 1)
                for L in range(2):
                    for half in range(2):
                        ins = dve.tensor_copy(mod[:, L, half * 3 * P:(half + 1) * 3 * P], banks(2 * L + half, 3 * P))
                step.done(ins)
                parts = mod[:, :, :].rearrange("p l (h k d) -> p l h k d", h=2, k=3)
                step.done(dve.tensor_scalar(parts[:, 0, :, 1, :], parts[:, 0, :, 1, :], 1.0, None, ALU.add))
                step.done(dve.tensor_scalar(parts[:, 1, :, 1, :], parts[:, 1, :, 1, :], 1.0, None, ALU.add))
                for L in range(2):
                    dve.tensor_scalar(gsign[:, L, :, :], parts[:, L, :, 2, :], 0.0, 2.0, ALU.is_ge, ALU.mult)
                    step.done(dve.scalar_tensor_tensor(out=gabs[:, L, :, :], in0=parts[:, L, :, 2, :], scalar=-1.0,
                                                       in1=parts[:, L, :, 2, :], op0=ALU.mult, op1=ALU.max))
                step.done(dve.tensor_scalar(gabs, gabs, 0.25, None, ALU.max))
                for L in range(2):
                    ins = dve.scalar_tensor_tensor(out=parts[:, L, :, 2, :], in0=gsign[:, L, :, :], scalar=-1.0,
                                                   in1=gabs[:, L, :, :], op0=ALU.add, op1=ALU.mult)
                step.done(ins)
                dve.tensor_copy(KB[0][HD:HD + NC, :], const("own_chunk")[HD:HD + NC, :])
                dve.tensor_copy(KB[1][HD:HD + NC, :], const("own_chunk")[HD:HD + NC, :])
                step.done(dve.memset(hT[:, 0:1], 0.0))
                step.done(dve.memset(hT[:, T + 1:T + 2], 0.0))
                assert step.n == MOD_STEPS, step.n

            def convolution(b):
                step = Chain(dve, cv_link, b * CONV_STEPS)
                dve.wait_ge(tr_out, 1 + b * TR_CALLS + 1)
                step.done(dve.tensor_reduce(ctx_sum[:, :], hT[:, 1:T + 1], AX, ALU.add))
                step.done(dve.tensor_scalar(ctx_sum[:, :], ctx_sum[:, :], 1.0 / T, None, ALU.mult))
                dve.tensor_copy(ctx_b[:, :], ctx_sum[:, :].to_broadcast([P, P])).then_inc(cv_ctx, 1)
                step.done(dve.tensor_scalar(att_in[:, :], hT[:, 0:T], conv_w[:, 0:1], None, ALU.mult))
                for k in range(1, 3):
                    step.done(dve.scalar_tensor_tensor(out=att_in[:, :], in0=hT[:, k:k + T], scalar=conv_w[:, k:k + 1],
                                                       in1=att_in[:, :], op0=ALU.mult, op1=ALU.add))
                dve.wait_ge(cv_dyn, b + 1)
                dve.tensor_tensor(dyn[:, :], banks(2, 3), kgen_b[:, :], ALU.add).then_inc(cv_pre, 1)
                dve.wait_ge(cv_sig, b + 1)
                step.done(dve.tensor_reduce(dsum[:, :], dsig[:, :], AX, ALU.add))
                step.done(dve.tensor_scalar(gate[:, :], dsum[:, :], 1.0 / 3.0, None, ALU.mult))
                dve.tensor_scalar(att_in[:, :], att_in[:, :], conv_b[:, 0:1], gate[:, 0:1],
                                  ALU.add, ALU.mult).then_inc(cv_out, 1)
                assert step.n == CONV_STEPS, step.n

            def attention(L, b):
                s = S[L]
                h0 = b * HEADS
                g0 = b * GROUPS
                b1 = (5, 6) if L == 0 else (4, 5)
                b1_units = 2 * NT if L == 0 else NT + NT // 2

                def low_parts(i, g, u):
                    n = h0 + i
                    dve.wait_ge(s["q_hi"], 1 + n + 1)
                    if L == 0:
                        dve.tensor_tensor(QA[u % 2][HD:P, :], PS[HD:P, 0:T], QA[u % 2][HD:P, :],
                                          ALU.subtract).then_inc(s["q_lo"], 1)
                    else:
                        dve.scalar_tensor_tensor(out=QA[u % 2][HD:P, :], in0=PS[HD:P, 0:T], scalar=bq[HD:P, ds(i, 1)],
                                                 in1=QA[u % 2][HD:P, :], op0=ALU.add,
                                                 op1=ALU.subtract).then_inc(s["q_lo"], 1)
                    if L == 0 and u == 0:
                        dve.wait_ge(s["k_hi"], 1 + g0 + g + 1)
                        dve.tensor_tensor(KB[1][0:HD, :], banks(2, rows=HD), KA[1][0:HD, :],
                                          ALU.subtract).then_inc(s["k_lo"], 1)
                    if L == 1:
                        dve.wait_ge(s["k_hi"], 1 + n + 1)
                        dve.scalar_tensor_tensor(out=KB[u % 2][0:HD, :], in0=banks(2, rows=HD), scalar=bk[0:HD, ds(i, 1)],
                                                 in1=KA[u % 2][0:HD, :], op0=ALU.add,
                                                 op1=ALU.subtract).then_inc(s["k_lo"], 1)

                def maxima(i):
                    n = h0 + i
                    for x in range(b1_units):
                        dve.wait_ge(s["p1_full"], n * b1_units + x + 1)
                        if L == 0:
                            t, half = divmod(x, 2)
                            dve.tensor_reduce(mx[:, t, half * 8:half * 8 + 8],
                                              banks(b1[x % 2], BANK).rearrange("p (c k) -> p c k", c=8),
                                              AX, ALU.max).then_inc(s["p1_max"], 1)
                        else:
                            t, half = (x, 0) if x < NT // 2 else divmod(x + NT // 2, 2)
                            width = min(BANK, (t + 1) * P - half * BANK)
                            dve.tensor_reduce(mrow1[:, t, half:half + 1], banks(b1[x % 2], width),
                                              AX, ALU.max).then_inc(s["p1_max"], 1)

                def maxima_rows(i, u):
                    n = h0 + i
                    if L == 1:
                        dve.wait_ge(s["p1_max"], 1 + (n + 1) * b1_units)
                        dve.tensor_reduce(mtop1[:, :], mrow1[:, :, :], AX, ALU.max).then_inc(s["m_both"], 1)
                        dve.wait_ge(s["m_both"], n + 1)
                        dve.tensor_tensor(mx1[:, :], mtop1[:, :], const("eps_row"), ALU.max).then_inc(s["m_top"], 1)
                    rows = NC if L == 0 else 1
                    dve.wait_ge(s["mt_ps"], n + 1)
                    dve.tensor_scalar(QB[u % 2][HD:HD + rows, :], banks(b1[0], rows=rows), -1.0, None,
                                      ALU.mult).then_inc(s["m_rows"], 1)

                def normaliser(n):
                    step = Chain(dve, nr_link, n * NORM_STEPS)
                    sums = banks(5, BANK).rearrange("p (k j c) -> p k j c", k=4, j=4)[:, :, :, 0:CQ]
                    dve.wait_ge(st_ps, n + 1)
                    step.done(dve.reciprocal(r0[:, :, :, :], sums))
                    step.done(dve.tensor_tensor(sw[:, :, :, :], sums, r0[:, :, :, :], ALU.mult))
                    dve.tensor_reduce(tot[:, :, :], sw[:, :, :, :].rearrange("p k (h o) c -> p k h (o c)", h=2), AX, ALU.add)
                    step.done(dve.tensor_tensor(r1[:, :, :, :], sw[:, :, :, :], r0[:, :, :, :], ALU.mult))
                    step.done(dve.tensor_scalar(tot[:, :, :], tot[:, :, :], EPS_TOTAL, None, ALU.add))
                    step.done(dve.reciprocal(tot[:, :, :], tot[:, :, :]))
                    flat = r1[:, :, :, :].rearrange("p k (h o) c -> p (k h) (o c)", h=2)
                    step.done(dve.tensor_tensor(flat, flat, tot[:, :, :].rearrange("p k h -> p (k h)").unsqueeze(2).to_broadcast([P, 8, 2 * CQ]),
                                                ALU.mult))
                    step.done(dve.tensor_copy(rhi[:, :, :, :], r1[:, :, :, :]))
                    step.done(dve.tensor_copy(rp[:, :, :, 0:CQ], rhi[:, :, :, :]))
                    dve.tensor_tensor(rp[:, :, :, CQ:2 * CQ], r1[:, :, :, :], rhi[:, :, :, :],
                                      ALU.subtract).then_inc(rp_out, 1)
                    assert step.n == NORM_STEPS, step.n

                def head(i, g, u, has_next, has_second):
                    n = h0 + i
                    if has_next:
                        maxima(i + 1)
                        maxima_rows(i + 1, u + 1)
                    g2, u2 = (g, u + 2) if u < GH - 2 else (g + 1, u - 2)
                    if L == 0:
                        normaliser(n)
                        if has_second:
                            low_parts(i + 2, g2, u2)
                        for t in range(NT):
                            dve.wait_ge(p3_full, n * NT + t + 1)
                            dve.tensor_tensor(E[:, t, :], E[:, t, :], banks(2 - 2 * (t % 2)),
                                              ALU.mult).then_inc(p3_mul, 1)
                    else:
                        dve.wait_ge(f_exp, 1 + n + 1)
                        dve.sem_inc(s_held, 1)
                        flat = E[:, :, :].rearrange("p t q -> p (t q)")
                        for t in range(NT):
                            at = t * (T + P)
                            ins = dve.copy_predicated(flat[:, at:at + P], const("mask").bitcast(I32),
                                                      F[:, t * P:(t + 1) * P])
                        ins.then_inc(diag, 1)
                        if has_second:
                            low_parts(i + 2, g2, u2)
                        dve.wait_ge(u_inv, n + 1)
                        rows = slice(HD * (u % 2), HD * (u % 2) + HD)
                        dve.tensor_tensor(U[rows, ds(g * 2 + u // 2, 1), :].squeeze(1), PS[0:HD, 6 * BANK:8 * BANK],
                                          lnd[HD:P, :], ALU.mult).then_inc(s["u_out"], 1)

                low_parts(0, 0, 0)
                low_parts(1, 0, 1)
                maxima(0)
                maxima_rows(0, 0)
                with dve.Fori(0, GROUPS - 1) as g:
                    for u in range(GH):
                        head(g * GH + u, g, u, True, True)
                with dve.Fori(GROUPS - 1, GROUPS) as g:
                    for u in range(GH):
                        head(g * GH + u, g, u, u < GH - 1, u < GH - 2)
                dve.wait_ge(s["o_full"], 1 + b + 1)
                residual(b, 2 * L, tiles(banks(0)), mod[:, L, 2 * P:3 * P])

            def mixture(b):
                for i in range(2 * NT):
                    kind, t = divmod(i, NT)
                    dve.wait_ge(lg_full, b * 2 * NT + i + 1)
                    dve.tensor_reduce(mxs[:, kind, t:t + 1], banks(2 * (i % 2)), AX, ALU.max).then_inc(lg_max, 1)
                dve.wait_ge(nm_ps, b + 1)
                dve.tensor_scalar(neg_rows[0], banks(4, rows=1), -1.0, None, ALU.mult)
                dve.tensor_scalar(neg_rows[1], banks(6, rows=1), -1.0, None, ALU.mult).then_inc(nm_out, 1)
                dve.wait_ge(sl_full, b + 1)
                wide = banks(4, 4 * BANK).rearrange("p (t d) -> p t d", t=NT)
                dve.reciprocal(rsl[:, :], wide[:, :, P]).then_inc(sl_link, 1)
                dve.wait_ge(sl_link, b * 3 + 1)
                dve.tensor_tensor(slot_tok[:, :, :], wide[:, :, 0:P], rsl[:, :].unsqueeze(2).to_broadcast([P, NT, P]),
                                  ALU.mult).then_inc(sl_out, 1)
                evacuate(slT, 1 + b * TR_CALLS + 2)
                with dve.Fori(0, E0 // 2) as j:
                    for i in range(2):
                        dve.wait_ge(xf_gel, (b * (E0 // 2) + j) * 2 + i + 1)
                        for f in range(2):
                            ins = dve.scalar_tensor_tensor(out=act0[i][:, f, :], in0=banks(i, SLOTS, (2 + f) * SLOTS),
                                                           scalar=bgu_s[i][:, 1, f:f + 1], in1=gel[i][:, f, :],
                                                           op0=ALU.add, op1=ALU.mult)
                        ins.then_inc(xf_act, 1)
                dve.wait_ge(cb_full, b + 1)
                dve.reciprocal(rsl[:, :], wide[:, :, P]).then_inc(sl_link, 1)
                dve.wait_ge(sl_link, b * 3 + 2)
                dve.tensor_tensor(xn[:, :, :], wide[:, :, 0:P], rsl[:, :].unsqueeze(2).to_broadcast([P, NT, P]),
                                  ALU.mult).then_inc(sl_link, 1)
                dve.wait_ge(sl_link, b * 3 + 3)
                residual(b, 1, xn[:, :, :], mod[:, 0, 5 * P:6 * P])

            def experts(b):
                step = Chain(dve, rt_link, b * ROUTE_STEPS)
                wide = [P, NT, E1]
                dve.wait_ge(rt_full, b + 1)
                step.done(dve.tensor_copy(lg[:, :, :], banks(2, NT * E1).rearrange("p (t e) -> p t e", t=NT)))
                dve.tensor_reduce(top[:, :], lg[:, :, :], AX, ALU.max).then_inc(rt_sig_in, 1)
                dve.wait_ge(rt_sig_in, b + 1)
                step.done(dve.tensor_tensor(eq[:, :, :], lg[:, :, :], top[:, :].unsqueeze(2).to_broadcast(wide),
                                            ALU.is_equal))
                step.done(dve.tensor_tensor(eq[:, :, :], eq[:, :, :],
                                            const("first").unsqueeze(1).to_broadcast(wide), ALU.mult))
                step.done(dve.tensor_reduce(best[:, :], eq[:, :, :], AX, ALU.max))
                step.done(dve.tensor_tensor(eq[:, :, :], eq[:, :, :], best[:, :].unsqueeze(2).to_broadcast(wide),
                                            ALU.is_equal))
                assert step.n == ROUTE_STEPS
                dve.wait_ge(rt_sig, b + 1)
                dve.tensor_tensor(sc_tok[:, :, :], eq[:, :, :], sig[:, :].unsqueeze(2).to_broadcast(wide),
                                  ALU.mult).then_inc(rt_out, 1)
                dve.wait_ge(rt_ps, b + 1)
                dve.memset(zero_row, 0.0)
                dve.tensor_copy(scT[:, :], banks(4, rows=E1)).then_inc(rt_T, 1)

                def product(y, i):
                    dve.wait_ge(y_up, y + 1)
                    dve.wait_ge(y_silu, 1 + y + 1)
                    dve.tensor_tensor(ac1[i], banks(4), sg1[i], ALU.mult).then_inc(y_act, 1)

                with dve.Fori(0, E1 // 2) as j:
                    for i in range(2):
                        dve.wait_ge(y_sc, b * E1 + j * 2 + i + 1)
                        dve.tensor_tensor(xs1[i], hT[:, 1:T + 1], banks(0), ALU.mult).then_inc(y_xs, 1)
                        product(b * UNITS1 + j * 2 + i, i)
                for k in range(SF // F1):
                    product(b * UNITS1 + E1 + k, k % 2)
                dve.wait_ge(y_dn, 1 + (b + 1) * UNITS1)
                residual(b, 3, tiles(banks(6)), mod[:, 1, 5 * P:6 * P])

            dve.memset(ones_row[:, :], 1.0)
            dve.memset(eps_col[:, 0:1], EPS_LN)
            dve.memset(eps_col[:, 1:2], EPS_MASK)
            dve.memset(V1[0][:, :, :, HD:P], 1.0)
            dve.memset(V1[1][:, :, :, HD:P], 1.0)
            dve.memset(rp[:, :, :, :], 0.0)
            dve.memset(mrow1[:, :, :], -3e38).then_inc(s_prep, 1)
            dve.wait_ge(s_const, 17 * 16)
            dve.tensor_copy(ident_b[:, :], ident)
            dve.tensor_copy(spread[:, :], const("spread"))
            dve.tensor_copy(neg_b[:, :], const("neg")).then_inc(s_prep, 1)
            dve.tensor_scalar(slot_aff[:, 0:2, :], slot_aff[:, 0:2, :], scale_b[:, 0:1], None,
                              ALU.mult).then_inc(s_prep, 1)
            dve.wait_ge(s_prep, 3)
            layernorm(x, xn[:, :, :], slot_aff[:, 0, :], slot_aff[:, 1, :], 0)
            evacuate(seT[:, :], 0)
            with dve.Fori(0, NB) as b:
                m = 1 + b * LN_CALLS
                r = 1 + b * TR_CALLS
                modulation(b)
                dve.wait_ge(s_x, (b + 1) * 16)
                layernorm(x, xn[:, :, :], mod[:, 0, P:2 * P], mod[:, 0, 0:P], m)
                evacuate(hT[:, 1:T + 1], r)
                convolution(b)
                attention(0, b)
                layernorm(x, xn[:, :, :], mod[:, 0, 4 * P:5 * P], mod[:, 0, 3 * P:4 * P], m + 1)
                dve.memset(xfa[:, :, P:P + 1], 1.0)
                dve.memset(eo[:, :, P:P + 1], 1.0)
                layernorm(xn, xfa[:, :, 0:P], norm_aff[:, 0, :], norm_aff[:, 1, :], m + 2)
                evacuate(xfT, r + 1)
                mixture(b)
                for h in range(2):
                    dve.tensor_scalar(KB[h][HD:HD + 1, :], const("own_chunk")[HD:HD + 1, :], 0.0, 1.0,
                                      ALU.mult, ALU.add)
                layernorm(x, xn[:, :, :], mod[:, 1, P:2 * P], mod[:, 1, 0:P], m + 3)
                evacuate(hT[:, 1:T + 1], r + 3)
                attention(1, b)
                layernorm(x, xn[:, :, :], mod[:, 1, 4 * P:5 * P], mod[:, 1, 3 * P:4 * P], m + 4)
                evacuate(hT[:, 1:T + 1], r + 4)
                experts(b)

        @block.gpsimd
        def _(pool):
            with pool.Fori(0, NB) as b:
                with pool.Fori(0, GROUPS) as g:
                    n = b * GROUPS + g
                    s = S[0]
                    pool.wait_ge(s["k_hi"], 1 + n + 1)
                    pool.wait_ge(s["k_lo"], 1 + n + 1)
                    pool.wait_ge(s_full, 1 + n * GH)
                    pool.sem_inc(s_held, 1)
                    pool.tensor_copy(KA[0][:, :], KA[1][:, :])
                    pool.tensor_copy(KB[0][0:HD, :], KB[1][0:HD, :]).then_inc(k_copy, 1)
                    pool.wait_ge(s["v_out"], 1 + n + 1)
                    pool.wait_ge(s["u_full"], 1 + n * GH)
                    pool.sem_inc(s_held, 1)
                    pool.tensor_copy(V0[0][:, :, :], V0[1][:, :, :]).then_inc(v_copy, 1)
                with pool.Fori(0, PAIRS // 2) as g:
                    for i in range(2):
                        n = b * PAIRS + g * 2 + i
                        pool.wait_ge(S[1]["v_out"], 1 + n + 1)
                        pool.wait_ge(S[1]["u_full"], 1 + 2 * n)
                        for t in reversed(range(NT - 2)):
                            after = V1[i][:, t + 2, :, :] if t == NT - 3 else Vlater[:, t + 1, :, :]
                            ins = pool.tensor_tensor(Vlater[:, t, :, :], after, V1[i][:, t + 1, :, :], ALU.add)
                            if t:
                                ins.then_inc(xw_ones, 1)
                                pool.wait_ge(xw_ones, n * (NT - 3) + NT - 2 - t)
                        ins.then_inc(later, 1)


def const_array():
    import numpy as np
    c = np.zeros((P, CONST_TOTAL), np.float32)

    def put(name, a):
        c[:, CONST_AT[name]:CONST_AT[name] + CONST_COLS[name]] = a

    p = np.arange(P)[:, None]
    q = np.arange(P)[None, :]
    put("ident", p == q)
    put("neg", np.where(q > p, -1e30, 0.0))
    put("mask", p > q)
    put("first", np.broadcast_to(E1 - np.arange(E1)[None, :], (P, E1)))
    rows = np.full((P, NT), EPS_MASK / QSCALE)
    rows[P - 1, NT - 1] = -3e38
    put("eps_row", rows)
    a = np.arange(4)[None, :, None]
    col = np.arange(32)[None, None, :]
    put("chunk", (col == 2 * a + (np.arange(P) // CHUNK)[:, None, None]).reshape(P, 4 * 32))
    k = np.arange(T)[None, :]
    r = p % CQ
    put("spread", (p % 32 < 2 * CQ) & (4 * (r // 2) + 2 * (p // 32 % 2) + r % 2 == k // CHUNK))
    put("own_chunk", (p - HD) == k // CHUNK)
    sel = np.zeros((E1, E1, P), np.float32)
    for e in range(E1):
        sel[e, e, :] = 1.0
    return c, sel


def host_arrays(inp):
    import numpy as np
    g = lambda n: np.asarray(inp[n])
    c, sel = const_array()
    a = {"consts": c, "sel": sel, "hidden": g("L0_attn_hidden_states")}
    a["c"] = np.stack([g("L0_c"), g("L1_c")], -1)
    a["wmod"] = np.stack([g("L0_wmod"), g("L1_wmod")], 1)
    a["wq0"] = g("L0_attn_w_q").T.reshape(P, HEADS, HD)
    a["wk0"] = g("L0_attn_w_k").T.reshape(P, GROUPS, HD)
    a["wv0"] = g("L0_attn_w_v").T
    a["wo0"] = g("L0_attn_w_o").T.reshape(PAIRS, P, P).transpose(1, 0, 2)
    a["kgen_w"] = g("L0_attn_w_kgen").T
    a["kgen_b"] = g("L0_attn_b_kgen")
    a["conv_w"] = g("L0_attn_w_conv")[:, 0, :]
    a["conv_b"] = g("L0_attn_b_conv")[:, None]
    for n in ("norm_g", "norm_b", "slot_g", "slot_b", "scale"):
        a[n] = g(f"L0_ffn_{n}")
    a["slots"] = g("L0_ffn_slot_embeds").reshape(NT, P, P).transpose(1, 0, 2)
    for n in ("Wg", "Wu", "Wd", "bd"):
        a[n] = g(f"L0_ffn_{n}")
    a["bgu"] = np.stack([g("L0_ffn_bg").reshape(E0, 2, P), g("L0_ffn_bu").reshape(E0, 2, P)], 1).transpose(0, 3, 1, 2)
    a["wq1"] = g("L1_attn_W_query").transpose(1, 0, 2)
    a["wk1"] = g("L1_attn_W_key").transpose(1, 0, 2)
    a["wv1"] = g("L1_attn_W_values").transpose(1, 0, 2).reshape(P, HEADS * HD)
    a["wo1"] = g("L1_attn_W_output").reshape(PAIRS, P, P).transpose(1, 0, 2)
    a["bq1"] = g("L1_attn_Bias_query").T
    a["bk1"] = g("L1_attn_Bias_key").T
    a["bv1"] = g("L1_attn_Bias_values").reshape(1, HEADS * HD)
    a["bo1"] = g("L1_attn_Bias_output")[None]
    a["router"] = g("L1_ffn_router_w").T
    a["gate_up"] = g("L1_ffn_gate_up_proj")
    a["down"] = g("L1_ffn_down_proj")
    a["wsh"] = np.concatenate([g("L1_ffn_shared_gate_w").T, g("L1_ffn_shared_up_w").T,
                               g("L1_ffn_shared_down_w").T.reshape(SF // P, P, P).transpose(1, 0, 2).reshape(P, SF)], 1)
    return {n: np.ascontiguousarray(v) for n, v in a.items()}


def kernel(**inputs):
    import concourse.bacc as _bacc
    from concourse.bass_utils import run_bass_kernel_spmd as _run

    nc = _bacc.Bacc("TRN2", target_bir_lowering=False, num_devices=1)
    arrays = {f"in_{n}": a for n, a in host_arrays(inputs).items()}
    A = {n[3:]: nc.dram_tensor(n, a.shape, mybir.dt.from_np(a.dtype), kind="ExternalInput").ap()
         for n, a in arrays.items()}
    out = nc.dram_tensor("out_0", (NB, T, P), F32, kind="ExternalOutput").ap()
    layer_program(nc, A, out)
    r = _run(nc, [arrays], core_ids=[0])
    return r.results[0]["out_0"]
```

```python
from contextlib import ExitStack

import concourse.bass as bass
from concourse import mybir
from concourse.alu_op_type import AluOpType as ALU

F32 = mybir.dt.float32
FR = mybir.dt.float32r
BF16 = mybir.dt.bfloat16
I32 = mybir.dt.int32
ACT = mybir.ActivationFunctionType
AX = mybir.AxisListType.X
ds = bass.ds

P = 128
NB = 2
T = 1024
NT = T // P
BANK = 512
HALF = T // BANK
HD = 64
HEADS = 16
PAIRS = HEADS // 2
GH = 4
GROUPS = HEADS // GH
CHUNK = 64
NC = T // CHUNK
E0, F0, SLOTS = 16, 256, 64
E1, F1, SF = 16, 128, 512
QSCALE = HD ** -0.5
EPS_LN = 1e-5
EPS_MASK = 1e-10
EPS_TOTAL = 1e-9
CQ = NC // 2

CONST_COLS = {"ident": 128, "neg": 128, "mask": 128, "first": 16,
              "expert": E1, "eps_row": NT, "chunk": 4 * 32}
CONST_AT = {}
_at = 0
for _name, _cols in CONST_COLS.items():
    CONST_AT[_name] = _at
    _at += _cols
CONST_TOTAL = _at

UNITS1 = E1 + SF // F1

LN_STEPS = 4
MOD_STEPS = 9
CONV_STEPS = 7
NORM_STEPS = 8
ROUTE_STEPS = 5


def layer_program(nc, A, out):
    ctx = ExitStack()
    with ctx:
        def sb(name, shape, dt=F32):
            return ctx.enter_context(nc.sbuf_tensor(name, shape, dt))

        def sem(name):
            return ctx.enter_context(nc.semaphore(name))

        consts = sb("consts", [P, CONST_TOTAL])

        def const(name, lo=0, hi=None):
            at = CONST_AT[name]
            return consts[:, at + lo:at + (CONST_COLS[name] if hi is None else hi)]

        ident = const("ident")
        ident_b = sb("ident_b", [P, P], BF16)
        neg_b = sb("neg_b", [P, P], BF16)
        chunk_sum = const("chunk").rearrange("p (a c) -> p a c", a=4)
        ones_row = sb("ones_row", [1, BANK])
        ones_fr = sb("ones_fr", [1, P], FR)
        eps_col = sb("eps_col", [P, 2])

        x = sb("x", [P, NT, P])
        xn = sb("xn", [P, NT, P])
        hT = sb("hT", [P, T + 2])
        att_in = sb("att_in", [P, T])
        stats = sb("stats", [P, NT, 6])
        mv = sb("mv", [P, NT, 2])
        std = sb("std", [P, NT])
        rstd = sb("rstd", [P, NT])
        ccol = sb("ccol", [P, 2])
        scol = sb("scol", [P, 2])
        sc_b = sb("sc_b", [P, 2, P])
        mod = sb("mod", [P, 2, 6 * P])

        conv_w = sb("conv_w", [P, 3])
        conv_b = sb("conv_b", [P, 1])
        kgen_w = sb("kgen_w", [P, 3])
        kgen_b = sb("kgen_b", [P, 3])
        ctx_sum = sb("ctx_sum", [P, 1])
        ctx_b = sb("ctx_b", [P, P])
        dyn = sb("dyn", [P, 3])
        dsig = sb("dsig", [P, 3])
        dsum = sb("dsum", [P, 1])
        gate = sb("gate", [P, 1])

        wq_s = sb("wq_s", [P, 4, P])
        wk_s = sb("wk_s", [P, 4, P])
        wv_s = sb("wv_s", [P, 256])
        bq = sb("bq", [P, HEADS])
        bk = sb("bk", [P, HEADS])
        bv_s = sb("bv_s", [1, 256])
        wo = sb("wo", [P, PAIRS, P])
        bo1 = sb("bo1", [1, P])
        QA = [sb(f"QA{i}", [P, T], FR) for i in range(2)]
        QB = [sb(f"QB{i}", [P, T], FR) for i in range(2)]
        KA = [sb(f"KA{i}", [P, T], FR) for i in range(2)]
        KB = [sb(f"KB{i}", [P, T], FR) for i in range(2)]
        V1 = [sb(f"V1{i}", [P, NT, 2, P]) for i in range(2)]
        Vlater = sb("Vlater", [P, NT - 2, 2, P])
        own0 = Vlater[:, :, :, :].rearrange("p t h d -> p (t h d)")
        V0 = [own0[:, i * BANK:(i + 1) * BANK].rearrange("p (t d) -> p t d", t=NT) for i in range(2)]
        EE = [sb(f"EE{i}", [P, NT, T]) for i in range(2)]
        E = EE[0]
        U = sb("U", [P, PAIRS, T])
        mx = sb("mx", [P, NT, NC])
        mrow1 = sb("mrow1", [P, NT, 2])
        mtop1 = sb("mtop1", [P, NT])
        mx1 = sb("mx1", [P, NT])
        spread = sb("spread", [P, T], FR)
        S_sb = own0[:, 2 * BANK:3 * BANK]
        r0 = sb("r0", [P, 4, 4, CQ])
        sw = sb("sw", [P, 4, 4, CQ])
        r1 = sb("r1", [P, 4, 4, CQ])
        tot = sb("tot", [P, 4, 2])
        rhi = sb("rhi", [P, 4, 4, CQ], FR)
        rp = sb("rp", [P, 4, 4, 32])
        r_parts = sb("r_parts", [P, BANK], FR)
        F = att_in
        lnd = xn[:, :, :].rearrange("p t d -> p (t d)")
        key_rows = U[:, 6:8, :]
        gsign = U[:, 3, 0:4 * P].rearrange("p (l h d) -> p l h d", l=2, h=2)
        gabs = U[:, 3, 4 * P:8 * P].rearrange("p (l h d) -> p l h d", l=2, h=2)

        seT = sb("seT", [P, T])
        slot_aff = U[:, 2, 0:2 * P].rearrange("p (k d) -> p k d", k=2)
        norm_aff = sb("norm_aff", [P, 2, P])
        scale_b = sb("scale_b", [P, 1])
        xf_parts = QA
        se_parts = QB
        slT = U[:, 1, :]
        slot_tok = U[:, 2, :].rearrange("p (t d) -> p t d", t=NT)
        neg_rows = [KA[i][0:1, :] for i in range(2)]
        Uf = U[:, :, :].rearrange("p n t -> p (n t)")
        u_at = [3 * T]

        def in_u(cols, rows=P):
            at = u_at[0]
            u_at[0] += cols
            assert u_at[0] <= PAIRS * T
            return Uf[0:rows, at:at + cols]

        xfa = in_u(NT * (P + 1)).rearrange("p (t d) -> p t d", t=NT)
        eo = in_u(NT * (P + 1)).rearrange("p (t d) -> p t d", t=NT)
        mxs = sb("mxs", [P, 2, NT])
        rsl = sb("rsl", [P, NT])
        wg_s = [in_u(F0) for _ in range(2)]
        wu_s = [in_u(F0) for _ in range(2)]
        wd_s = [in_u(F0).rearrange("p (h d) -> p h d", h=2) for _ in range(2)]
        bgu_s = [sb(f"bgu_s{i}", [P, 2, 2]) for i in range(2)]
        bd_s = [sb(f"bd_s{i}", [1, P]) for i in range(2)]
        gel = [EE[1][:, i, 0:P].rearrange("p (f s) -> p f s", f=2) for i in range(2)]
        act0 = [EE[1][:, i, P:2 * P].rearrange("p (f s) -> p f s", f=2) for i in range(2)]

        router = sb("router", [P, E1])
        lg = U[:, 3, 0 * P:1 * P].rearrange("p (t e) -> p t e", t=NT)
        top = sb("top", [P, NT])
        eq = U[:, 3, 1 * P:2 * P].rearrange("p (t e) -> p t e", t=NT)
        best = sb("best", [P, NT])
        sig = sb("sig", [P, NT])
        sc_tok = U[:, 3, 2 * P:3 * P].rearrange("p (t e) -> p t e", t=NT)
        scT = QA[1][0:2 * E1, :]
        sel1 = [QA[0][0:2 * E1, i * P:(i + 1) * P] for i in range(2)]
        sc_hi = QB[0][:, 0:NT * E1].rearrange("p (t e) -> p t e", t=NT)
        sc_parts = U[:, 3, 4 * P:6 * P].rearrange("p (t e) -> p t e", t=NT)
        wgu1 = [U[:, 1, i * 4 * P:i * 4 * P + 2 * P] for i in range(2)]
        wd1 = [U[:, 1, i * 4 * P + 2 * P:i * 4 * P + 3 * P] for i in range(2)]
        zero_row = U[0:1, 2, 0:BANK]
        xs1 = [E[:, i, :] for i in range(2)]
        sg1 = [E[:, 2 + i, :] for i in range(2)]
        ac1 = [E[:, 4 + i, :] for i in range(2)]
        wmod = U[:, 4:6, :].rearrange("p a b -> p (a b)")[:, 0:12 * P].rearrange("p (l n) -> p l n", l=2)
        wsh = E[:, 6:8, :].rearrange("p a b -> p (a b)")[:, 0:3 * SF]

        PS = ctx.enter_context(nc.psum_tensor("PS", [P, 8 * BANK], F32))

        def banks(first, cols=T, lo=0, rows=P):
            return PS[0:rows, first * BANK + lo:first * BANK + lo + cols]

        s_const = sem("s_const")
        s_prep = sem("s_prep")
        s_x = sem("s_x")
        s_c = sem("s_c")
        s_out = sem("s_out")
        s_held = sem("s_held")
        s_silu = sem("s_silu")
        s_scb = sem("s_scb")
        s_mod_ps = sem("s_mod_ps")
        s_mod = sem("s_mod")
        ln_var = sem("ln_var")
        ln_std = sem("ln_std")
        ln_link = sem("ln_link")
        ln_out = sem("ln_out")
        tr_ps = sem("tr_ps")
        tr_out = sem("tr_out")
        cv_link = sem("cv_link")
        cv_ctx = sem("cv_ctx")
        cv_dyn = sem("cv_dyn")
        cv_pre = sem("cv_pre")
        cv_sig = sem("cv_sig")
        cv_out = sem("cv_out")

        def layer_sems(names):
            return [{n: sem(f"{n}_{L}") for n in ("wo_in " + names).split()} for L in range(2)]

        S = layer_sems("w_in proj_q q_hi q_lo proj_k k_hi k_lo proj_v v_out p1_full p1_max "
                       "m_both m_top mt_ps m_rows p2_full p2_f p2_exp u_full u_out o_full")
        s_full = sem("s_full")
        nr_link = sem("nr_link")
        s_copy = sem("s_copy")
        st_ps = sem("st_ps")
        rp_out = sem("rp_out")
        rb_ps = sem("rb_ps")
        s_rr = sem("s_rr")
        p3_full = sem("p3_full")
        p3_mul = sem("p3_mul")
        k_copy = sem("k_copy")
        v_copy = sem("v_copy")
        later = sem("later")
        f_exp = sem("f_exp")
        diag = sem("diag")
        u_ln = sem("u_ln")
        u_inv = sem("u_inv")
        u_norm = sem("u_norm")
        den_out = sem("den_out")
        res_link = sem("res_link")

        se_high = sem("se_high")
        xf_high = sem("xf_high")
        lg_full = sem("lg_full")
        lg_max = sem("lg_max")
        nm_ps = sem("nm_ps")
        nm_out = sem("nm_out")
        ex_full = sem("ex_full")
        ex_out = sem("ex_out")
        sl_full = sem("sl_full")
        sl_link = sem("sl_link")
        sl_out = sem("sl_out")
        xw = [sem(f"xw{i}") for i in range(2)]
        xf_full = sem("xf_full")
        xf_gel = sem("xf_gel")
        xf_act = sem("xf_act")
        xd_full = sem("xd_full")
        xd_out = sem("xd_out")
        cb_full = sem("cb_full")
        xw_ones = sem("xw_ones")

        rt_full = sem("rt_full")
        rt_link = sem("rt_link")
        rt_sig_in = sem("rt_sig_in")
        rt_sig = sem("rt_sig")
        rt_out = sem("rt_out")
        rt_ps = sem("rt_ps")
        sc_link = sem("sc_link")
        rt_T = sem("rt_T")
        yw = [sem(f"yw{i}") for i in range(2)]
        shw = sem("shw")
        yd = [sem(f"yd{i}") for i in range(2)]
        y_sel = sem("y_sel")
        y_sc = sem("y_sc")
        y_xs = sem("y_xs")
        y_gate = sem("y_gate")
        y_up = sem("y_up")
        y_silu = sem("y_silu")
        y_act = sem("y_act")
        y_dn = sem("y_dn")

        start_at_one = [s_out, s_full, xd_full, y_dn, p3_mul, f_exp, den_out, k_copy, v_copy, xf_act, xd_out, y_up,
                        y_silu, y_act, later]
        start_at_one += [S[L][name] for L in range(2) for name in ("proj_v", "proj_q", "proj_k", "q_hi", "q_lo", "k_hi", "k_lo", "v_out", "p1_max",
                                                               "p2_exp", "o_full", "u_out", "u_full")]

        class Chain:

            def __init__(self, eng, semaphore, base):
                self.eng, self.semaphore, self.base, self.n = eng, semaphore, base, 0

            def done(self, ins):
                ins.then_inc(self.semaphore, 1)
                self.n += 1
                self.eng.wait_ge(self.semaphore, self.base + self.n)

        def place(g, u):
            return (g, u) if u < GH else (g + 1, u - GH)

        def has_prev2(i, u):
            return not (isinstance(i, int) and i < 2)

        def run_heads(eng, head):
            head(0, 0, 0, has_prev=False, has_next=True, has_second=True, last=False)
            head(1, 0, 1, has_prev=True, has_next=True, has_second=True, last=False)
            with eng.Fori(0, GROUPS - 1) as g:
                for u in range(2, GH + 2):
                    head(g * GH + u, *place(g, u), has_prev=True, has_next=True, has_second=True, last=False)
            with eng.Fori(GROUPS - 1, GROUPS) as g:
                for u in range(2, GH):
                    head(g * GH + u, g, u, has_prev=True, has_next=u < GH - 1, has_second=u < GH - 2, last=True)

        block = ctx.enter_context(nc.Block())

        LN_CALLS = 5
        TR_CALLS = 5

        @block.sync
        def _(sp):
            for dst, src in [(consts[:, :], A["consts"]), (conv_w[:, :], A["conv_w"]), (conv_b[:, :], A["conv_b"]),
                             (kgen_w[:, :], A["kgen_w"]), (kgen_b[:, :], A["kgen_b"].partition_broadcast(P)),
                             (bo1[:, :], A["bo1"]),
                             (bq[0:HD, :], A["bq1"]), (bq[HD:P, :], A["bq1"]), (bk[0:HD, :], A["bk1"]), (bk[HD:P, :], A["bk1"]),
                             (slot_aff[:, 0, :], A["slot_g"].partition_broadcast(P)),
                             (slot_aff[:, 1, :], A["slot_b"].partition_broadcast(P)),
                             (scale_b[:, :], A["scale"].partition_broadcast(P)),
                             (norm_aff[:, 0, :], A["norm_g"].partition_broadcast(P)),
                             (norm_aff[:, 1, :], A["norm_b"].partition_broadcast(P)),
                             (router[:, :], A["router"]), (key_rows, A["key_rows"]),
                             (x[:, :, :], A["slots"])]:
                sp.dma_start(dst, src).then_inc(s_const, 16)
            for q in start_at_one:
                sp.sem_inc(q, 1)
            sp.wait_ge(ln_out, 1)
            with sp.Fori(0, NB) as b:
                sp.wait_ge(s_out, 1 + b * 16)
                sp.dma_start(x[:, :, :], A["hidden"][ds(b, 1)].squeeze(0).rearrange("(t p) d -> p t d", p=P)).then_inc(s_x, 16)
                sp.dma_start(ccol[:, :], A["c"][ds(b, 1)].squeeze(0)).then_inc(s_c, 16)
                sp.dma_start(wmod[:, :, :], A["wmod"]).then_inc(s_c, 16)
                for L in range(2):
                    v_used = sp.snap(1 + (b + L) * (GROUPS * (2 if L == 0 else 1)))
                    q_used = sp.snap(1 + (b + L) * (GROUPS * 4))
                    k_used = sp.snap(1 + (b + L) * (GROUPS * (4 if L == 0 else 1)))
                    wo_used = sp.snap(1 + b + L)
                    sp.wait_ge(S[1 - L]["proj_v"], v_used)
                    sp.sem_inc(s_held, 1)
                    sp.wait_ge(S[1 - L]["proj_q"], q_used)
                    sp.sem_inc(s_held, 1)
                    sp.wait_ge(S[1 - L]["proj_k"], k_used)
                    sp.sem_inc(s_held, 1)
                    sp.wait_ge(S[1 - L]["o_full"], wo_used)
                    sp.sem_inc(s_held, 1)
                    sp.dma_start(wo[:, :, :], A[f"wo{L}"]).then_inc(S[L]["wo_in"], 16)
                    with sp.Fori(0, GROUPS) as g:
                        v_used = sp.snap(1 + (b * GROUPS + g) * (1 if L == 0 else 4))
                        q_used = sp.snap(1 + (b * GROUPS + g) * 4)
                        sp.wait_ge(S[L]["proj_v" if L == 0 else "proj_k"], v_used)
                        sp.wait_ge(S[L]["proj_q"], q_used)
                        sp.sem_inc(s_held, 1)
                        w_in = S[L]["w_in"]
                        for half in range(2):
                            cols = slice(half * HD, half * HD + HD)
                            sp.dma_start(wq_s[:, :, cols], A[f"wq{L}"][:, ds(g * 4, 4), :]).then_inc(w_in, 16)
                            if L == 0:
                                sp.dma_start(wk_s[:, 0, cols], A["wk0"][:, ds(g, 1), :].squeeze(1)).then_inc(w_in, 16)
                            else:
                                sp.dma_start(wk_s[:, :, cols], A["wk1"][:, ds(g * 4, 4), :]).then_inc(w_in, 16)
                        if L == 0:
                            sp.dma_start(wv_s[:, 0:HD], A["wv0"][:, ds(g * HD, HD)]).then_inc(w_in, 16)
                        else:
                            sp.dma_start(wv_s[:, :], A["wv1"][:, ds(g * 256, 256)]).then_inc(w_in, 16)
                            sp.dma_start(bv_s[:, :], A["bv1"][:, ds(g * 256, 256)]).then_inc(w_in, 16)
                    if L == 0:
                        with sp.Fori(0, E0 // 2) as j:
                            for i in range(2):
                                sp.wait_ge(S[0]["o_full"], 1 + b + 1)
                                sp.sem_inc(s_held, 1)
                                sp.wait_ge(xd_full, 1 + b * (E0 // 2) + j)
                                e = j * 2 + i
                                sp.dma_start(wg_s[i], A["Wg"][ds(e, 1)].squeeze(0)).then_inc(xw[i], 16)
                                sp.dma_start(wu_s[i], A["Wu"][ds(e, 1)].squeeze(0)).then_inc(xw[i], 16)
                                sp.dma_start(wd_s[i], A["Wd"][ds(e, 1)].squeeze(0).rearrange("(h p) d -> p h d", p=P)).then_inc(xw[i], 16)
                                sp.dma_start(bgu_s[i][:, :, :], A["bgu"][ds(e, 1)].squeeze(0)).then_inc(xw[i], 16)
                                sp.dma_start(bd_s[i][:, :], A["bd"][ds(e, 1)]).then_inc(xw[i], 16)
                    else:
                        sp.wait_ge(S[1]["o_full"], 1 + b + 1)
                        sp.dma_start(wsh, A["wsh"]).then_inc(shw, 16)

                        def expert_weights(j, first):
                            for i in range(2):
                                e = j * 2 + i
                                if not first:
                                    sp.wait_ge(y_up, b * UNITS1 + e)
                                    sp.sem_inc(s_held, 1)
                                sp.dma_start(wgu1[i], A["gate_up"][ds(e, 1)].squeeze(0)).then_inc(yw[i], 16)
                                if not first:
                                    sp.wait_ge(y_dn, b * UNITS1 + e)
                                    sp.sem_inc(s_held, 1)
                                sp.dma_start(wd1[i], A["down"][ds(e, 1)].squeeze(0)).then_inc(yd[i], 16)

                        expert_weights(0, True)
                        with sp.Fori(1, E1 // 2) as j:
                            expert_weights(j, False)
                sp.wait_ge(res_link, (b + 1) * 8)
                sp.dma_start(out[ds(b, 1)].squeeze(0).rearrange("(t p) d -> p t d", p=P), x[:, :, :]).then_inc(s_out, 16)
            sp.wait_ge(s_out, 1 + NB * 16)

        @block.tensor
        def _(pe):
            def transposed(src, m):
                for t in range(NT):
                    mm = pe.transpose(banks(0, P, t * P), src(t), ident)
                mm.then_inc(tr_ps, 1)

            def attention(L, b):
                s = S[L]
                x_in = att_in if L == 0 else hT[:, 1:T + 1]
                m_rows_n = NC if L == 0 else 1
                krows = HD + m_rows_n
                b1 = (5, 6) if L == 0 else (4, 5)
                b1_units = 2 * NT if L == 0 else NT + NT // 2
                q_bank, k_bank = (0, 2) if L == 0 else (2, 4)
                h0 = b * HEADS
                g0 = b * GROUPS

                def pair_of(g, u):
                    return b * PAIRS + g * 2 + u // 2

                def inputs_ready(g):
                    if L == 0:
                        pe.wait_ge(cv_out, b + 1)
                    else:
                        pe.wait_ge(tr_out, 1 + b * TR_CALLS + 4)
                    pe.wait_ge(s["w_in"], (g0 + g + 1) * (80 if L == 0 else 96))

                def project_q(u):
                    for half in range(2):
                        mm = pe.matmul(banks(q_bank + half, BANK), wq_s[:, u, :], x_in[:, half * BANK:(half + 1) * BANK],
                                       start=True, stop=True)
                    mm.then_inc(s["proj_q"], 1)

                def project_k(u):
                    for half in range(2):
                        mm = pe.matmul(banks(k_bank + half, BANK), wk_s[:, u * L, :],
                                       x_in[:, half * BANK:(half + 1) * BANK], start=True, stop=True)
                    mm.then_inc(s["proj_k"], 1)

                def project_v(u):
                    for t in range(NT):
                        if L == 0:
                            mm = pe.matmul(banks(7, HD, t * HD), x_in[:, t * P:(t + 1) * P], wv_s[:, 0:HD],
                                           start=True, stop=True)
                        else:
                            pe.matmul(banks(2, P, t * P), x_in[:, t * P:(t + 1) * P],
                                      wv_s[:, u * HD:u * HD + P], start=True, stop=False)
                            mm = pe.matmul(banks(2, P, t * P), ones_row[:, 0:P], bv_s[:, u * HD:u * HD + P],
                                           start=False, stop=True)
                    mm.then_inc(s["proj_v"], 1)

                def parts_ready(n, group):
                    n_k = group + 1 if L == 0 else n + 1
                    pe.wait_ge(s["q_hi"], 1 + n + 1)
                    pe.wait_ge(s["q_lo"], 1 + n + 1)
                    pe.wait_ge(s["k_hi"], 1 + n_k)
                    pe.wait_ge(s["k_lo"], 1 + n_k)

                def maxima(i, g, u, units):
                    n = h0 + i
                    q = QB[u % 2]
                    k = KA[1 if u < 2 else 0] if L == 0 else KA[u % 2]
                    for x in units:
                        if L == 0:
                            t, half = divmod(x, 2)
                        else:
                            t, half = (x, 0) if x < NT // 2 else divmod(x + NT // 2, 2)
                        lo, hi = half * BANK, (half + 1) * BANK
                        if L == 1:
                            hi = min(hi, (t + 1) * P)
                        if x >= 2:
                            pe.wait_ge(s["p1_max"], 1 + n * b1_units + x - 1)
                        own = L == 1 and hi == (t + 1) * P
                        mm = pe.matmul(banks(b1[x % 2], hi - lo), q[0:HD, t * P:(t + 1) * P], k[0:HD, lo:hi],
                                       start=True, stop=not own)
                        if own:
                            mm = pe.matmul(banks(b1[x % 2], P, hi - lo - P), ident_b[:, :], neg_b[:, :],
                                           start=False, stop=True)
                        mm.then_inc(s["p1_full"], 1)

                def turn_maxima(n):
                    if L == 0:
                        pe.wait_ge(s["p1_max"], 1 + (n + 1) * b1_units)
                    else:
                        pe.wait_ge(s["m_top"], n + 1)
                    for t in range(NT):
                        src = mx[:, t, :] if L == 0 else mx1[:, t:t + 1]
                        mm = pe.transpose(banks(b1[0], P, t * P, rows=m_rows_n), src, ident)
                    mm.then_inc(s["mt_ps"], 1)

                def scores(n, u, t):
                    par = u % 2
                    kk = (1 if u == 0 else 0) if L == 0 else par
                    if t >= 1:
                        pe.wait_ge(s["p2_exp"], 1 + n * NT + t)
                    spans = []
                    for half in range(2):
                        lo, hi = max(half * BANK, 0 if L == 0 else t * P), (half + 1) * BANK
                        if lo < hi:
                            spans.append((lo, hi))
                    for lo, hi in spans:
                        pe.matmul(banks(0, hi - lo, lo), KA[kk][:, t * P:(t + 1) * P], QA[par][:, lo:hi],
                                  start=True, stop=False)
                    for lo, hi in spans:
                        mm = pe.matmul(banks(0, hi - lo, lo), KB[kk][0:krows, t * P:(t + 1) * P],
                                       QB[par][0:krows, lo:hi], start=False, stop=True)
                    mm.then_inc(s["p2_full"], 1)

                def chunk_sums(n, u, a):
                    pe.wait_ge(s["p2_exp"], 1 + n * NT + 2 * a + 2)
                    for half in range(2):
                        for odd in range(2):
                            j = 2 * half + odd
                            mm = pe.matmul(PS[32 * j:32 * j + 32, 4 * BANK:5 * BANK], chunk_sum[:, a, :],
                                           EE[u % 2][:, 2 * a + odd, half * BANK:(half + 1) * BANK],
                                           start=(a == 0), stop=(a == 3))
                    return mm

                def turn_sums(n):
                    pe.wait_ge(s_copy, n + 1)
                    for k in range(4):
                        mm = pe.transpose(banks(4, P, k * P), S_sb[:, k * P:(k + 1) * P], ident)
                    mm.then_inc(st_ps, 1)

                def turn_normalisers(n):
                    pe.wait_ge(rp_out, n + 1)
                    for k in range(4):
                        mm = pe.transpose(banks(4, P, k * P), rp[:, k, :, :].rearrange("p j c -> p (j c)"), ident)
                    mm.then_inc(rb_ps, 1)

                def chunk_weights(n, g, u, t, k_followed):
                    if t == 0:
                        pe.wait_ge(s_rr, n + 1)
                        if k_followed:
                            pe.wait_ge(s["k_hi"], 1 + g0 + g + 2)
                            pe.wait_ge(s["k_lo"], 1 + g0 + g + 2)
                    else:
                        pe.wait_ge(p3_mul, 1 + n * NT + t)
                    for half in range(2):
                        q = 32 * (2 * half + t % 2)
                        mm = pe.matmul(banks(2 + half, BANK), spread[q:q + 2 * CQ, t * P:(t + 1) * P],
                                       r_parts[q:q + 2 * CQ, :], start=True, stop=True,
                                       tile_position=(q, 0))
                    mm.then_inc(p3_full, 1)

                def values0(n, g, u, t, k_followed):
                    if t == 0:
                        pe.wait_ge(s["u_out"], 1 + n)
                        if u == 1:
                            pe.wait_ge(v_copy, 1 + g0 + g + 1)
                        if k_followed:
                            pe.wait_ge(s["v_out"], 1 + g0 + g + 2)
                    pe.wait_ge(p3_mul, 1 + n * NT + t + 1)
                    for half in range(2):
                        mm = pe.matmul(PS[HD * half:HD * half + HD, 7 * BANK:8 * BANK], V0[1 if u == 0 else 0][:, t, :],
                                       EE[u % 2][:, t, half * BANK:(half + 1) * BANK],
                                       start=(t == 0), stop=(t == NT - 1))
                    if t == NT - 1:
                        mm.then_inc(s["u_full"], 1)

                def head0(i, g, u, has_prev, has_next, has_second, last):
                    n = h0 + i
                    gp, up = (g, u - 1) if u else (g - 1, GH - 1)
                    g1, u1 = place(g, u + 1)
                    g2, u2 = place(g, u + 2)
                    kf = u == GH - 1 and not last
                    pe.wait_ge(s["m_rows"], n + 1)
                    if has_next:
                        pe.wait_ge(s["q_hi"], 1 + n + 2)
                        pe.wait_ge(s["q_lo"], 1 + n + 2)
                    if u == 1:
                        pe.wait_ge(k_copy, 1 + g0 + g + 1)
                    for t in range(NT):
                        scores(n, u, t)
                        if has_next:
                            if t == 0:
                                parts_ready(n + 1, g0 + g1)
                            maxima(i + 1, g1, u1, [2 * t])
                        if has_prev and t == 1:
                            turn_normalisers(n - 1)
                        if has_prev and t >= 2:
                            chunk_weights(n - 1, gp, up, t - 2, kf)
                        if has_next:
                            maxima(i + 1, g1, u1, [2 * t + 1])
                        if has_prev and t >= 3:
                            values0(n - 1, gp, up, t - 3, kf)
                        if t >= 3 and t % 2 == 1:
                            if t == 3 and has_prev:
                                pe.wait_ge(s_rr, n)
                            chunk_sums(n, u, (t - 3) // 2)
                    if has_prev:
                        chunk_weights(n - 1, gp, up, NT - 2, kf)
                        values0(n - 1, gp, up, NT - 3, kf)
                    if has_second:
                        if u2 == 0:
                            inputs_ready(g2)
                        pe.wait_ge(s["p2_exp"], 1 + (n + 1) * NT)
                        project_q(u2)
                    chunk_sums(n, u, 3).then_inc(s_full, 1)
                    if has_next:
                        turn_maxima(n + 1)
                    if has_prev:
                        chunk_weights(n - 1, gp, up, NT - 1, kf)
                        values0(n - 1, gp, up, NT - 2, kf)
                    turn_sums(n)
                    if has_prev:
                        values0(n - 1, gp, up, NT - 1, kf)
                    if has_second:
                        if u2 == 0:
                            pe.wait_ge(k_copy, 1 + g0 + g2)
                            pe.wait_ge(p3_mul, 1 + n * NT)
                            project_k(u2)
                            pe.wait_ge(v_copy, 1 + g0 + g2)
                            pe.wait_ge(s["u_out"], 1 + n)
                            project_v(u2)

                def values1(n, u, t):
                    if t == 0:
                        pe.wait_ge(diag, n + 1)
                        pe.wait_ge(s["u_out"], 1 + n)
                        pe.wait_ge(den_out, 1 + n)
                    for half in range(2):
                        lo, hi = max(half * BANK, t * P), (half + 1) * BANK
                        if lo < hi:
                            pe.matmul(banks(6, hi - lo, lo), V1[u // 2][:, t, u % 2, :], EE[u % 2][:, t, lo:hi],
                                      start=(t == 0), stop=False, skip_group_check=True)

                def values_masked(n, g, u):
                    pe.wait_ge(later, 1 + pair_of(g, u) + 1)
                    for t in range(NT - 1):
                        v = V1[u // 2][:, t + 1, u % 2, :] if t == NT - 2 else Vlater[:, t, u % 2, :]
                        mm = pe.matmul(banks(6, P, t * P), v, F[:, t * P:(t + 1) * P], start=False,
                                       stop=(t in (3, NT - 2)), skip_group_check=True)
                    mm.then_inc(s["u_full"], 1)

                def head1(i, g, u, has_prev, has_next, has_second, last):
                    n = h0 + i
                    gp, up = (g, u - 1) if u else (g - 1, GH - 1)
                    g1, u1 = place(g, u + 1)
                    g2, u2 = place(g, u + 2)
                    new_v = u % 2 == 1 and not (last and u == GH - 1)
                    pe.wait_ge(s["m_rows"], n + 1)
                    if has_prev:
                        pe.wait_ge(f_exp, 1 + n)
                    done = 0
                    for t in range(NT):
                        scores(n, u, t)
                        if has_next:
                            if t == 1:
                                parts_ready(n + 1, None)
                            todo = range(done, min(b1_units, done + 2 * (t > 0)))
                            maxima(i + 1, g1, u1, todo)
                            done += len(todo)
                        if t == 3 and new_v:
                            project_v(u1 if u1 else 0)
                        if has_prev:
                            values1(n - 1, up, t)
                        if t == NT - 2 and has_second:
                            if u2 == 0:
                                inputs_ready(g2)
                            if new_v:
                                pe.wait_ge(s["v_out"], 1 + pair_of(g, u) + 2)
                            project_q(u2)
                    if has_prev:
                        values_masked(n - 1, gp, up)
                    if has_next:
                        turn_maxima(n + 1)
                    pe.wait_ge(s["p2_exp"], 1 + (n + 1) * NT)
                    for half in range(2):
                        mm = pe.matmul(banks(half, BANK), KB[u % 2][HD:HD + 1, 0:P],
                                       QB[u % 2][HD:HD + 1, half * BANK:(half + 1) * BANK], start=True, stop=True)
                    mm.then_inc(s["p2_f"], 1)
                    if has_second:
                        pe.wait_ge(s["m_rows"], n + 2)
                        project_k(u2)

                inputs_ready(0)
                project_q(0)
                project_k(0)
                if L == 0:
                    project_v(0)
                parts_ready(h0, g0)
                if L == 1:
                    project_v(0)
                    pe.wait_ge(s["v_out"], 1 + pair_of(0, 0) + 1)
                else:
                    pe.wait_ge(s["v_out"], 1 + g0 + 1)
                project_q(1)
                maxima(0, 0, 0, range(b1_units))
                turn_maxima(h0)
                if L == 1:
                    pe.wait_ge(s["m_rows"], h0 + 1)
                    project_k(1)
                run_heads(pe, head0 if L == 0 else head1)
                n = h0 + HEADS - 1
                if L == 0:
                    turn_normalisers(n)
                    for t in range(NT):
                        chunk_weights(n, GROUPS - 1, GH - 1, t, False)
                        values0(n, GROUPS - 1, GH - 1, t, False)
                else:
                    for t in range(NT):
                        values1(n, GH - 1, t)
                    values_masked(n, GROUPS - 1, GH - 1)
                if L == 0:
                    pe.wait_ge(s["u_out"], 1 + (b + 1) * HEADS)
                else:
                    pe.wait_ge(u_norm, (b + 1) * HEADS)
                pe.wait_ge(s["wo_in"], (b + 1) * 16)
                for t in range(NT):
                    for p in range(PAIRS):
                        mm = pe.matmul(banks(0, P, t * P), U[:, p, t * P:(t + 1) * P], wo[:, p, :],
                                       start=(p == 0), stop=(p == PAIRS - 1 and L == 0))
                    if L == 1:
                        mm = pe.matmul(banks(0, P, t * P), ones_row[:, 0:P], bo1[:, :], start=False, stop=True)
                mm.then_inc(s["o_full"], 1)

            def mixture(b):
                pe.wait_ge(tr_out, 1 + b * TR_CALLS + 2)
                for i in range(2 * NT):
                    kind, t = divmod(i, NT)
                    a, c = (xf_parts, se_parts) if kind == 0 else (se_parts, xf_parts)
                    first = 2 * (i % 2)
                    if i >= 2:
                        pe.wait_ge(lg_max, b * 2 * NT + i - 1)
                    for half in range(2):
                        mm = pe.matmul(banks(first + half, BANK), a[0][:, t * P:(t + 1) * P],
                                       c[0][:, half * BANK:(half + 1) * BANK], start=True, stop=True)
                    mm.then_inc(lg_full, 1)
                pe.wait_ge(lg_max, (b + 1) * 2 * NT)
                for kind in range(2):
                    for t in range(NT):
                        mm = pe.transpose(banks(4 + 2 * kind, P, t * P, rows=1), mxs[:, kind, t:t + 1], ident)
                mm.then_inc(nm_ps, 1)
                pe.wait_ge(nm_out, b + 1)

                def exponents(kind):
                    for t in range(NT):
                        i = kind * NT + t
                        a, c = (xf_parts, se_parts) if kind == 0 else (se_parts, xf_parts)
                        first = 2 * (i % 2)
                        tile = slice(t * P, (t + 1) * P)
                        if i >= 2:
                            pe.wait_ge(ex_out, b * 2 * NT + i - 1)
                        terms = ((a[0][:, tile], c[0]), (a[0][:, tile], c[1]), (a[1][:, tile], c[0]),
                                 (ones_fr[:, :], neg_rows[1 - kind]))
                        for m, (lhs, rhs) in enumerate(terms):
                            for half in range(2):
                                mm = pe.matmul(banks(first + half, BANK), lhs, rhs[:, half * BANK:(half + 1) * BANK],
                                               start=(m == 0), stop=(m == len(terms) - 1))
                        mm.then_inc(ex_full, 1)

                exponents(0)
                pe.wait_ge(ex_out, b * 2 * NT + NT)
                for st in range(NT):
                    for t in range(NT):
                        mm = pe.matmul(banks(4, P + 1, st * 256), E[:, t, st * P:(st + 1) * P], xfa[:, t, :],
                                       start=(t == 0), stop=(t == NT - 1))
                mm.then_inc(sl_full, 1)
                exponents(1)
                pe.wait_ge(sl_out, b + 1)
                pe.wait_ge(ex_out, (b + 1) * 2 * NT)
                transposed(lambda t: slot_tok[:, t, :], None)
                with pe.Fori(0, E0 // 2) as j:
                    pe.wait_ge(tr_out, 1 + b * TR_CALLS + 3)
                    for i in range(2):
                        ex = (b * (E0 // 2) + j) * 2 + i
                        pe.wait_ge(xw[i], (b * (E0 // 2) + j + 1) * 80)
                        pe.wait_ge(xf_act, 1 + ex - i)
                        rhs = slT[:, ds((j * 2 + i) * SLOTS, SLOTS)]
                        for k in range(4):
                            w = (wg_s if k < 2 else wu_s)[i]
                            mm = pe.matmul(banks(i, SLOTS, k * SLOTS), w[:, (k % 2) * P:(k % 2 + 1) * P], rhs,
                                           start=True, stop=True)
                        mm.then_inc(xf_full, 1)
                    pe.wait_ge(xd_out, 1 + b * (E0 // 2) + j)
                    for i in range(2):
                        pe.wait_ge(xf_act, 1 + (b * (E0 // 2) + j) * 2 + i + 1)
                        o = PS[HD * i:HD * i + HD, 2 * BANK:2 * BANK + P]
                        pe.matmul(o, act0[i][:, 0, :], wd_s[i][:, 0, :], start=True, stop=False)
                        pe.matmul(o, act0[i][:, 1, :], wd_s[i][:, 1, :], start=False, stop=False)
                        mm = pe.matmul(o, ones_row[:, 0:SLOTS], bd_s[i][:, :], start=False, stop=True)
                    mm.then_inc(xd_full, 1)
                pe.wait_ge(xd_out, 1 + (b + 1) * (E0 // 2))
                for t in range(NT):
                    for st in range(NT):
                        mm = pe.matmul(banks(4, P + 1, t * 256), E[:, st, t * P:(t + 1) * P], eo[:, st, :],
                                       start=(st == 0), stop=(st == NT - 1))
                mm.then_inc(cb_full, 1)

            def experts(b):
                pe.wait_ge(tr_out, 1 + b * TR_CALLS + 5)
                for t in range(NT):
                    mm = pe.matmul(banks(2, E1, t * E1), hT[:, 1 + t * P:1 + (t + 1) * P], router[:, :],
                                   start=True, stop=True)
                mm.then_inc(rt_full, 1)
                pe.wait_ge(rt_out, b + 1)
                for t in range(NT):
                    mm = pe.transpose(banks(4, P, t * P, rows=2 * E1), sc_parts[:, t, :], ident)
                mm.then_inc(rt_ps, 1)
                pe.wait_ge(rt_T, b + 1)
                for half in range(2):
                    pe.matmul(banks(6 + half, BANK), ones_row[:, 0:P], zero_row, start=True, stop=False,
                              skip_group_check=True)

                def gate_up(y, wg, wu, src):
                    pe.wait_ge(y_silu, 1 + y)
                    for half in range(2):
                        mm = pe.matmul(banks(2 + half, BANK), wg, src[:, half * BANK:(half + 1) * BANK],
                                       start=True, stop=True)
                    mm.then_inc(y_gate, 1)
                    pe.wait_ge(y_act, 1 + y)
                    for half in range(2):
                        mm = pe.matmul(banks(4 + half, BANK), wu, src[:, half * BANK:(half + 1) * BANK],
                                       start=True, stop=True)
                    mm.then_inc(y_up, 1)

                def down(y, a, w):
                    pe.wait_ge(y_act, 1 + y + 1)
                    for t in range(NT):
                        mm = pe.matmul(banks(6, P, t * P), a[:, t * P:(t + 1) * P], w, start=False, stop=False,
                                       skip_group_check=True)
                    mm.then_inc(y_dn, 1)

                def spread_score(e, i):
                    pe.wait_ge(y_sel, b * E1 + e + 1)
                    for half in range(2):
                        mm = pe.matmul(banks(half, BANK), sel1[i], scT[:, half * BANK:(half + 1) * BANK],
                                       start=True, stop=True)
                    mm.then_inc(y_sc, 1)

                def routed(j, first=False, last=False):
                    for i in range(2):
                        e = j * 2 + i
                        y = b * UNITS1 + e
                        pe.wait_ge(y_xs, b * E1 + e + 1)
                        if not (last and i == 1):
                            spread_score(e + 1, 1 - i)
                        pe.wait_ge(yw[i], (b * (E1 // 2) + j + 1) * 16)
                        gate_up(y, wgu1[i][:, 0:F1], wgu1[i][:, F1:2 * F1], xs1[i])
                        if not (first and i == 0):
                            pe.wait_ge(yd[1 - i], (b * (E1 // 2) + j + i) * 16)
                            down(y - 1, ac1[1 - i], wd1[1 - i])

                spread_score(0, 0)
                routed(0, first=True)
                with pe.Fori(1, E1 // 2 - 1) as j:
                    routed(j)
                routed(E1 // 2 - 1, last=True)
                pe.wait_ge(shw, (b + 1) * 16)
                for k in range(SF // F1):
                    y = b * UNITS1 + E1 + k
                    gate_up(y, wsh[:, k * P:(k + 1) * P], wsh[:, SF + k * P:SF + (k + 1) * P], hT[:, 1:T + 1])
                    if k == 0:
                        pe.wait_ge(yd[1], (b + 1) * (E1 // 2) * 16)
                        down(y - 1, ac1[1], wd1[1])
                    else:
                        down(y - 1, ac1[(k - 1) % 2], wsh[:, 2 * SF + (k - 1) * P:2 * SF + k * P])
                k = SF // F1 - 1
                down(y, ac1[k % 2], wsh[:, 2 * SF + k * P:2 * SF + (k + 1) * P])

            pe.wait_ge(s_const, 18 * 16)
            pe.wait_ge(s_prep, 3)
            pe.wait_ge(ln_out, 1)
            transposed(lambda t: xn[:, t, :], 0)
            with pe.Fori(0, NB) as b:
                pe.wait_ge(s_c, (b + 1) * 32)
                pe.wait_ge(s_scb, b + 1)
                for L in range(2):
                    for half in range(2):
                        mm = pe.matmul(banks(2 * L + half, 3 * P), sc_b[:, L, :],
                                       wmod[:, L, half * 3 * P:(half + 1) * 3 * P], start=True, stop=True)
                mm.then_inc(s_mod_ps, 1)
                pe.wait_ge(ln_out, 1 + b * LN_CALLS + 1)
                transposed(lambda t: xn[:, t, :], 0)
                pe.wait_ge(cv_ctx, b + 1)
                pe.matmul(banks(2, 3), ctx_b[:, :], kgen_w[:, :], start=True, stop=True).then_inc(cv_dyn, 1)
                attention(0, b)
                pe.wait_ge(ln_out, 1 + b * LN_CALLS + 3)
                transposed(lambda t: xfa[:, t, 0:P], 1)
                mixture(b)
                pe.wait_ge(ln_out, 1 + b * LN_CALLS + 4)
                transposed(lambda t: xn[:, t, :], 3)
                attention(1, b)
                pe.wait_ge(ln_out, 1 + b * LN_CALLS + 5)
                transposed(lambda t: xn[:, t, :], 4)
                experts(b)

        @block.scalar
        def _(act):
            def std_of(m):
                act.wait_ge(ln_var, m + 1)
                act.activation(std[:, :], mv[:, :, 1], ACT.Sqrt, bias=eps_col[:, 0:1]).then_inc(ln_std, 1)

            def attention(L, b):
                s = S[L]
                h0 = b * HEADS
                g0 = b * GROUPS

                def high_q(i, u):
                    n = h0 + i
                    act.wait_ge(s["proj_q"], 1 + n + 1)
                    if L == 0:
                        act.activation(QA[u % 2][:, :], banks(0), ACT.Copy)
                        act.activation(QB[u % 2][0:HD, :], banks(0, rows=HD), ACT.Copy).then_inc(s["q_hi"], 1)
                    else:
                        act.activation(QA[u % 2][:, :], banks(2), ACT.Identity, bias=bq[:, ds(i, 1)])
                        act.activation(QB[u % 2][0:HD, :], banks(2, rows=HD), ACT.Identity,
                                       bias=bq[0:HD, ds(i, 1)]).then_inc(s["q_hi"], 1)

                def high_k(i, g, u):
                    if L == 0:
                        act.wait_ge(s["proj_k"], 1 + g0 + g + 1)
                        act.activation(KA[1][:, :], banks(2), ACT.Copy).then_inc(s["k_hi"], 1)
                    else:
                        act.wait_ge(s["proj_k"], 1 + h0 + i + 1)
                        act.activation(KA[u % 2][:, :], banks(4), ACT.Identity, bias=bk[:, ds(i, 1)]).then_inc(s["k_hi"], 1)

                def values_out(g, buffer):
                    if L == 0:
                        act.wait_ge(s["proj_v"], 1 + g0 + g + 1)
                        act.activation(own0[:, BANK:2 * BANK], banks(7, BANK),
                                       ACT.Copy).then_inc(s["v_out"], 1)
                    else:
                        act.wait_ge(s["proj_v"], 1 + b * PAIRS + g + 1)
                        act.activation(V1[buffer][:, :, :, 0:HD], banks(2).rearrange("p (t h d) -> p t h d", t=NT, h=2),
                                       ACT.Copy).then_inc(s["v_out"], 1)

                def output(n, g, u):
                    act.wait_ge(s["u_full"], 1 + n + 1)
                    rows = slice(HD * (u % 2), HD * (u % 2) + HD)
                    if L == 0:
                        for half in range(2):
                            ins = act.activation(U[rows, ds(g * 2 + u // 2, 1), half * BANK:(half + 1) * BANK].squeeze(1),
                                                 PS[HD * half:HD * half + HD, 7 * BANK:8 * BANK], ACT.Copy)
                        ins.then_inc(s["u_out"], 1)
                    else:
                        act.activation(lnd[rows, :], PS[HD:P, 6 * BANK:8 * BANK], ACT.Copy).then_inc(den_out, 1)

                def inverse(n, u):
                    rows = slice(HD * (u % 2), HD * (u % 2) + HD)
                    act.wait_ge(den_out, 1 + n + 1)
                    act.activation(lnd[rows, :], lnd[rows, :], ACT.Ln).then_inc(u_ln, 1)
                    act.wait_ge(u_ln, n + 1)
                    act.activation(lnd[rows, :], lnd[rows, :], ACT.Exp, scale=-1.0).then_inc(u_inv, 1)

                def normalisers(n):
                    act.wait_ge(rb_ps, n + 1)
                    act.activation(r_parts[:, :], banks(4, BANK), ACT.Copy).then_inc(s_rr, 1)

                def head(i, g, u, has_prev, has_next, has_second, last):
                    n = h0 + i
                    gp, up = (g, u - 1) if u else (g - 1, GH - 1)
                    g2, u2 = place(g, u + 2)
                    for t in range(NT):
                        lo = 0 if L == 0 else t * P
                        act.wait_ge(s["p2_full"], n * NT + t + 1)
                        act.activation(EE[u % 2][:, t, lo:T], banks(0, T - lo, lo), ACT.Exp,
                                       scale=QSCALE).then_inc(s["p2_exp"], 1)
                        if L == 0 and has_prev and t == 1:
                            normalisers(n - 1)
                        if L == 1 and t == 0 and has_prev2(i, u):
                            inverse(n - 2, u)
                        if L == 1 and t == 3 and u % 2 == 1 and not (last and u == GH - 1):
                            values_out(g * 2 + u // 2 + 1, 1 - u // 2)
                    if L == 0:
                        if has_second:
                            high_q(i + 2, u2)
                        act.wait_ge(s_full, 1 + n + 1)
                        act.activation(S_sb[:, :], banks(4, BANK), ACT.Copy).then_inc(s_copy, 1)
                        if has_prev:
                            output(n - 1, gp, up)
                        if has_second and u2 == 0:
                            high_k(i + 2, g2, u2)
                            values_out(g2, 1)
                    else:
                        act.wait_ge(s["p2_f"], n + 1)
                        act.activation(F[:, :], banks(0), ACT.Exp, bias=eps_col[:, 1:2], scale=QSCALE).then_inc(f_exp, 1)
                        if has_second:
                            high_q(i + 2, u2)
                        if has_prev:
                            output(n - 1, gp, up)
                        if has_second:
                            high_k(i + 2, g2, u2)

                high_q(0, 0)
                high_k(0, 0, 0)
                values_out(0, 0)
                high_q(1, 1)
                if L == 1:
                    high_k(1, 0, 1)
                run_heads(act, head)
                n = h0 + HEADS - 1
                if L == 0:
                    normalisers(n)
                output(n, GROUPS - 1, GH - 1)
                if L == 1:
                    inverse(n - 1, GH - 2)
                    inverse(n, GH - 1)

            act.wait_ge(s_prep, 3)
            std_of(0)
            with act.Fori(0, NB) as b:
                m = 1 + b * LN_CALLS
                act.wait_ge(s_c, (b + 1) * 32)
                act.activation(scol[:, :], ccol[:, :], ACT.Silu).then_inc(s_silu, 1)
                std_of(m)
                act.wait_ge(cv_pre, b + 1)
                act.activation(dsig[:, :], dyn[:, :], ACT.Sigmoid).then_inc(cv_sig, 1)
                attention(0, b)
                act.wait_ge(S[0]["o_full"], 1 + b + 1)
                act.activation(se_parts[0][:, :], seT[:, :], ACT.Copy).then_inc(se_high, 1)
                std_of(m + 1)
                std_of(m + 2)
                for i in range(2 * NT):
                    kind, t = divmod(i, NT)
                    act.wait_ge(ex_full, b * 2 * NT + i + 1)
                    act.activation(E[:, t, :], banks(2 * (i % 2)), ACT.Exp).then_inc(ex_out, 1)
                with act.Fori(0, E0 // 2) as j:
                    for i in range(2):
                        act.wait_ge(xf_full, (b * (E0 // 2) + j) * 2 + i + 1)
                        act.activation(gel[i][:, 0, :], banks(i, SLOTS), ACT.Gelu, bias=bgu_s[i][:, 0, 0:1])
                        act.activation(gel[i][:, 1, :], banks(i, SLOTS, SLOTS), ACT.Gelu,
                                       bias=bgu_s[i][:, 0, 1:2]).then_inc(xf_gel, 1)
                    act.wait_ge(xd_full, 1 + b * (E0 // 2) + j + 1)
                    act.activation(eo[:, ds(j, 1), 0:P].squeeze(1), banks(2, P), ACT.Copy).then_inc(xd_out, 1)
                std_of(m + 3)
                attention(1, b)
                std_of(m + 4)
                act.wait_ge(rt_sig_in, b + 1)
                act.activation(sig[:, :], top[:, :], ACT.Sigmoid).then_inc(rt_sig, 1)

                def silu(y, i):
                    act.wait_ge(y_gate, y + 1)
                    act.activation(sg1[i], banks(2), ACT.Silu).then_inc(y_silu, 1)

                with act.Fori(0, E1 // 2) as j:
                    for i in range(2):
                        silu(b * UNITS1 + j * 2 + i, i)
                for k in range(SF // F1):
                    silu(b * UNITS1 + E1 + k, k % 2)

        @block.vector
        def _(dve):
            def layernorm(src, dst, scale, shift, m):
                step = Chain(dve, ln_link, m * LN_STEPS)
                for t in range(NT):
                    ins = dve.bn_stats(stats[:, t, :], src[:, t, :])
                step.done(ins)
                dve.sem_inc(s_held, 1)
                for t in range(NT):
                    ins = dve.bn_aggr(mv[:, t, :], stats[:, t, :])
                ins.then_inc(ln_var, 1)
                dve.wait_ge(ln_std, m + 1)
                step.done(dve.reciprocal(rstd[:, :], std[:, :]))
                for t in range(NT):
                    ins = dve.tensor_scalar(xn[:, t, :], src[:, t, :], mv[:, t, 0:1], rstd[:, t:t + 1],
                                            ALU.subtract, ALU.mult)
                step.done(ins)
                step.done(dve.tensor_tensor(xn[:, :, :], xn[:, :, :],
                                            scale.unsqueeze(1).to_broadcast([P, NT, P]), ALU.mult))
                dve.tensor_tensor(dst, xn[:, :, :], shift.unsqueeze(1).to_broadcast([P, NT, P]),
                                  ALU.add).then_inc(ln_out, 1)
                dve.wait_ge(ln_out, m + 1)
                assert step.n == LN_STEPS

            def evacuate(dst, m):
                dve.wait_ge(tr_ps, m + 1)
                dve.tensor_copy(dst, banks(0)).then_inc(tr_out, 1)

            def residual(b, k, y, g):
                step = Chain(dve, res_link, b * 8 + 2 * k)
                step.done(dve.tensor_tensor(xn[:, :, :], y, g.unsqueeze(1).to_broadcast([P, NT, P]), ALU.mult))
                step.done(dve.tensor_tensor(x[:, :, :], x[:, :, :], xn[:, :, :], ALU.add))

            def tiles(ap):
                return ap.rearrange("p (t d) -> p t d", t=NT)

            def row_under_k(h, lo, hi, value):
                dve.tensor_scalar(KB[h][HD:HD + 1, lo:hi], consts[HD:HD + 1, 0:hi - lo], 0.0, value,
                                  ALU.mult, ALU.add)

            def modulation(b):
                dve.wait_ge(s_silu, b + 1)
                dve.tensor_copy(sc_b[:, :, :], scol[:, :].unsqueeze(2).to_broadcast([P, 2, P])).then_inc(s_scb, 1)
                step = Chain(dve, s_mod, b * MOD_STEPS)
                dve.wait_ge(s_mod_ps, b + 1)
                for L in range(2):
                    for half in range(2):
                        ins = dve.tensor_copy(mod[:, L, half * 3 * P:(half + 1) * 3 * P], banks(2 * L + half, 3 * P))
                step.done(ins)
                parts = mod[:, :, :].rearrange("p l (h k d) -> p l h k d", h=2, k=3)
                step.done(dve.tensor_scalar(parts[:, 0, :, 1, :], parts[:, 0, :, 1, :], 1.0, None, ALU.add))
                step.done(dve.tensor_scalar(parts[:, 1, :, 1, :], parts[:, 1, :, 1, :], 1.0, None, ALU.add))
                for L in range(2):
                    dve.tensor_scalar(gsign[:, L, :, :], parts[:, L, :, 2, :], 0.0, 2.0, ALU.is_ge, ALU.mult)
                    step.done(dve.scalar_tensor_tensor(out=gabs[:, L, :, :], in0=parts[:, L, :, 2, :], scalar=-1.0,
                                                       in1=parts[:, L, :, 2, :], op0=ALU.mult, op1=ALU.max))
                step.done(dve.tensor_scalar(gabs, gabs, 0.25, None, ALU.max))
                for L in range(2):
                    ins = dve.scalar_tensor_tensor(out=parts[:, L, :, 2, :], in0=gsign[:, L, :, :], scalar=-1.0,
                                                   in1=gabs[:, L, :, :], op0=ALU.add, op1=ALU.mult)
                step.done(ins)
                for h in range(2):
                    row_under_k(h, 0, CHUNK, 1.0)
                    row_under_k(h, CHUNK, BANK, 0.0)
                    row_under_k(h, BANK, T, 0.0)
                step.done(dve.memset(hT[:, 0:1], 0.0))
                step.done(dve.memset(hT[:, T + 1:T + 2], 0.0))
                assert step.n == MOD_STEPS, step.n

            def convolution(b):
                step = Chain(dve, cv_link, b * CONV_STEPS)
                dve.wait_ge(tr_out, 1 + b * TR_CALLS + 1)
                step.done(dve.tensor_reduce(ctx_sum[:, :], hT[:, 1:T + 1], AX, ALU.add))
                step.done(dve.tensor_scalar(ctx_sum[:, :], ctx_sum[:, :], 1.0 / T, None, ALU.mult))
                dve.tensor_copy(ctx_b[:, :], ctx_sum[:, :].to_broadcast([P, P])).then_inc(cv_ctx, 1)
                step.done(dve.tensor_scalar(att_in[:, :], hT[:, 0:T], conv_w[:, 0:1], None, ALU.mult))
                for k in range(1, 3):
                    step.done(dve.scalar_tensor_tensor(out=att_in[:, :], in0=hT[:, k:k + T], scalar=conv_w[:, k:k + 1],
                                                       in1=att_in[:, :], op0=ALU.mult, op1=ALU.add))
                dve.wait_ge(cv_dyn, b + 1)
                dve.tensor_tensor(dyn[:, :], banks(2, 3), kgen_b[:, :], ALU.add).then_inc(cv_pre, 1)
                dve.wait_ge(cv_sig, b + 1)
                step.done(dve.tensor_reduce(dsum[:, :], dsig[:, :], AX, ALU.add))
                step.done(dve.tensor_scalar(gate[:, :], dsum[:, :], 1.0 / 3.0, None, ALU.mult))
                dve.tensor_scalar(att_in[:, :], att_in[:, :], conv_b[:, 0:1], gate[:, 0:1],
                                  ALU.add, ALU.mult).then_inc(cv_out, 1)
                assert step.n == CONV_STEPS, step.n

            def attention(L, b):
                s = S[L]
                h0 = b * HEADS
                g0 = b * GROUPS
                b1 = (5, 6) if L == 0 else (4, 5)
                b1_units = 2 * NT if L == 0 else NT + NT // 2

                def low_q(i, u):
                    n = h0 + i
                    dve.wait_ge(s["q_hi"], 1 + n + 1)
                    if L == 0:
                        dve.tensor_tensor(QA[u % 2][HD:P, :], PS[HD:P, 0:T], QA[u % 2][HD:P, :],
                                          ALU.subtract).then_inc(s["q_lo"], 1)
                    else:
                        dve.scalar_tensor_tensor(out=QA[u % 2][HD:P, :], in0=PS[HD:P, 2 * BANK:4 * BANK],
                                                 scalar=bq[HD:P, ds(i, 1)], in1=QA[u % 2][HD:P, :], op0=ALU.add,
                                                 op1=ALU.subtract).then_inc(s["q_lo"], 1)

                def low_k(i, g, u):
                    if L == 0:
                        dve.wait_ge(s["k_hi"], 1 + g0 + g + 1)
                        dve.tensor_tensor(KB[1][0:HD, :], banks(2, rows=HD), KA[1][0:HD, :],
                                          ALU.subtract).then_inc(s["k_lo"], 1)
                    else:
                        dve.wait_ge(s["k_hi"], 1 + h0 + i + 1)
                        dve.scalar_tensor_tensor(out=KB[u % 2][0:HD, :], in0=banks(4, rows=HD), scalar=bk[0:HD, ds(i, 1)],
                                                 in1=KA[u % 2][0:HD, :], op0=ALU.add,
                                                 op1=ALU.subtract).then_inc(s["k_lo"], 1)

                def maxima(n, units):
                    for x in units:
                        dve.wait_ge(s["p1_full"], n * b1_units + x + 1)
                        if L == 0:
                            t, half = divmod(x, 2)
                            dve.tensor_reduce(mx[:, t, half * 8:half * 8 + 8],
                                              banks(b1[x % 2], BANK).rearrange("p (c k) -> p c k", c=8),
                                              AX, ALU.max).then_inc(s["p1_max"], 1)
                        else:
                            t, half = (x, 0) if x < NT // 2 else divmod(x + NT // 2, 2)
                            width = min(BANK, (t + 1) * P - half * BANK)
                            dve.tensor_reduce(mrow1[:, t, half:half + 1], banks(b1[x % 2], width),
                                              AX, ALU.max).then_inc(s["p1_max"], 1)

                def maxima_rows(n, u):
                    if L == 1:
                        dve.wait_ge(s["p1_max"], 1 + (n + 1) * b1_units)
                        dve.tensor_reduce(mtop1[:, :], mrow1[:, :, :], AX, ALU.max).then_inc(s["m_both"], 1)
                        dve.wait_ge(s["m_both"], n + 1)
                        dve.tensor_tensor(mx1[:, :], mtop1[:, :], const("eps_row"), ALU.max).then_inc(s["m_top"], 1)
                    rows = NC if L == 0 else 1
                    dve.wait_ge(s["mt_ps"], n + 1)
                    dve.tensor_scalar(QB[u % 2][HD:HD + rows, :], banks(b1[0], rows=rows), -1.0, None,
                                      ALU.mult).then_inc(s["m_rows"], 1)

                def normaliser(n):
                    step = Chain(dve, nr_link, n * NORM_STEPS)
                    sums = banks(4, BANK).rearrange("p (k j c) -> p k j c", k=4, j=4)[:, :, :, 0:CQ]
                    dve.wait_ge(st_ps, n + 1)
                    step.done(dve.reciprocal(r0[:, :, :, :], sums))
                    step.done(dve.tensor_tensor(sw[:, :, :, :], sums, r0[:, :, :, :], ALU.mult))
                    dve.tensor_reduce(tot[:, :, :], sw[:, :, :, :].rearrange("p k (h o) c -> p k h (o c)", h=2), AX, ALU.add)
                    step.done(dve.tensor_tensor(r1[:, :, :, :], sw[:, :, :, :], r0[:, :, :, :], ALU.mult))
                    step.done(dve.tensor_scalar(tot[:, :, :], tot[:, :, :], EPS_TOTAL, None, ALU.add))
                    step.done(dve.reciprocal(tot[:, :, :], tot[:, :, :]))
                    flat = r1[:, :, :, :].rearrange("p k (h o) c -> p (k h) (o c)", h=2)
                    step.done(dve.tensor_tensor(flat, flat, tot[:, :, :].rearrange("p k h -> p (k h)").unsqueeze(2).to_broadcast([P, 8, 2 * CQ]),
                                                ALU.mult))
                    step.done(dve.tensor_copy(rhi[:, :, :, :], r1[:, :, :, :]))
                    step.done(dve.tensor_copy(rp[:, :, :, 0:CQ], rhi[:, :, :, :]))
                    dve.tensor_tensor(rp[:, :, :, CQ:2 * CQ], r1[:, :, :, :], rhi[:, :, :, :],
                                      ALU.subtract).then_inc(rp_out, 1)
                    assert step.n == NORM_STEPS, step.n

                def weigh(n, u, t):
                    dve.wait_ge(p3_full, n * NT + t + 1)
                    dve.tensor_tensor(EE[u % 2][:, t, :], EE[u % 2][:, t, :], banks(2), ALU.mult).then_inc(p3_mul, 1)

                def head0(i, g, u, has_prev, has_next, has_second, last):
                    n = h0 + i
                    up = (u - 1) % GH
                    g2, u2 = place(g, u + 2)
                    for t in range(NT):
                        if has_next:
                            maxima(n + 1, [2 * t, 2 * t + 1])
                        if has_prev and t >= 2:
                            weigh(n - 1, up, t - 2)
                    if has_prev:
                        weigh(n - 1, up, NT - 2)
                    if has_next:
                        maxima_rows(n + 1, u + 1)
                    if has_prev:
                        weigh(n - 1, up, NT - 1)
                    if has_second:
                        low_q(i + 2, u2)
                        if u2 == 0:
                            low_k(i + 2, g2, u2)
                    normaliser(n)

                def output(n, g, u):
                    dve.wait_ge(s["u_full"], 1 + n + 1)
                    rows = slice(HD * (u % 2), HD * (u % 2) + HD)
                    dve.tensor_copy(U[rows, ds(g * 2 + u // 2, 1), :].squeeze(1), PS[0:HD, 6 * BANK:8 * BANK]
                                    ).then_inc(s["u_out"], 1)

                def normalise(n, g, u):
                    dve.wait_ge(s["u_out"], 1 + n + 1)
                    dve.sem_inc(s_held, 1)
                    dve.wait_ge(u_inv, n + 1)
                    rows = slice(HD * (u % 2), HD * (u % 2) + HD)
                    place_u = U[rows, ds(g * 2 + u // 2, 1), :].squeeze(1)
                    dve.tensor_tensor(place_u, place_u, lnd[rows, :], ALU.mult).then_inc(u_norm, 1)

                def head1(i, g, u, has_prev, has_next, has_second, last):
                    n = h0 + i
                    gp, up = (g, u - 1) if u else (g - 1, GH - 1)
                    g2, u2 = place(g, u + 2)
                    if has_next:
                        maxima(n + 1, range(4))
                    if has_prev2(i, u):
                        normalise(n - 2, *((g, u - 2) if u > 1 else (g - 1, u + GH - 2)))
                    if has_next:
                        maxima(n + 1, range(4, b1_units))
                        maxima_rows(n + 1, u + 1)
                    dve.wait_ge(f_exp, 1 + n + 1)
                    dve.sem_inc(s_held, 1)
                    flat = EE[u % 2][:, :, :].rearrange("p t q -> p (t q)")
                    for t in range(NT):
                        at = t * (T + P)
                        ins = dve.copy_predicated(flat[:, at:at + P], const("mask").bitcast(I32),
                                                  F[:, t * P:(t + 1) * P])
                    ins.then_inc(diag, 1)
                    if has_prev:
                        output(n - 1, gp, up)
                    if has_second:
                        low_q(i + 2, u2)
                        low_k(i + 2, g2, u2)

                low_q(0, 0)
                low_k(0, 0, 0)
                low_q(1, 1)
                maxima(h0, range(b1_units))
                maxima_rows(h0, 0)
                if L == 1:
                    low_k(1, 0, 1)
                run_heads(dve, head0 if L == 0 else head1)
                n = h0 + HEADS - 1
                if L == 0:
                    for t in range(NT):
                        weigh(n, GH - 1, t)
                else:
                    output(n, GROUPS - 1, GH - 1)
                    normalise(n - 1, GROUPS - 1, GH - 2)
                    normalise(n, GROUPS - 1, GH - 1)
                dve.wait_ge(s["o_full"], 1 + b + 1)
                residual(b, 2 * L, tiles(banks(0)), mod[:, L, 2 * P:3 * P])

            def mixture(b):
                for i in range(2 * NT):
                    kind, t = divmod(i, NT)
                    dve.wait_ge(lg_full, b * 2 * NT + i + 1)
                    dve.tensor_reduce(mxs[:, kind, t:t + 1], banks(2 * (i % 2)), AX, ALU.max).then_inc(lg_max, 1)
                dve.wait_ge(nm_ps, b + 1)
                dve.tensor_scalar(neg_rows[0], banks(4, rows=1), -1.0, None, ALU.mult)
                dve.tensor_scalar(neg_rows[1], banks(6, rows=1), -1.0, None, ALU.mult).then_inc(nm_out, 1)
                dve.wait_ge(sl_full, b + 1)
                wide = banks(4, 4 * BANK).rearrange("p (t d) -> p t d", t=NT)
                dve.reciprocal(rsl[:, :], wide[:, :, P]).then_inc(sl_link, 1)
                dve.wait_ge(sl_link, b * 3 + 1)
                dve.tensor_tensor(slot_tok[:, :, :], wide[:, :, 0:P], rsl[:, :].unsqueeze(2).to_broadcast([P, NT, P]),
                                  ALU.mult).then_inc(sl_out, 1)
                evacuate(slT, 1 + b * TR_CALLS + 2)
                with dve.Fori(0, E0 // 2) as j:
                    for i in range(2):
                        dve.wait_ge(xf_gel, (b * (E0 // 2) + j) * 2 + i + 1)
                        for f in range(2):
                            ins = dve.scalar_tensor_tensor(out=act0[i][:, f, :], in0=banks(i, SLOTS, (2 + f) * SLOTS),
                                                           scalar=bgu_s[i][:, 1, f:f + 1], in1=gel[i][:, f, :],
                                                           op0=ALU.add, op1=ALU.mult)
                        ins.then_inc(xf_act, 1)
                dve.wait_ge(cb_full, b + 1)
                dve.reciprocal(rsl[:, :], wide[:, :, P]).then_inc(sl_link, 1)
                dve.wait_ge(sl_link, b * 3 + 2)
                dve.tensor_tensor(xn[:, :, :], wide[:, :, 0:P], rsl[:, :].unsqueeze(2).to_broadcast([P, NT, P]),
                                  ALU.mult).then_inc(sl_link, 1)
                dve.wait_ge(sl_link, b * 3 + 3)
                residual(b, 1, xn[:, :, :], mod[:, 0, 5 * P:6 * P])

            def experts(b):
                step = Chain(dve, rt_link, b * ROUTE_STEPS)
                wide = [P, NT, E1]
                dve.wait_ge(rt_full, b + 1)
                step.done(dve.tensor_copy(lg[:, :, :], banks(2, NT * E1).rearrange("p (t e) -> p t e", t=NT)))
                dve.tensor_reduce(top[:, :], lg[:, :, :], AX, ALU.max).then_inc(rt_sig_in, 1)
                dve.wait_ge(rt_sig_in, b + 1)
                step.done(dve.tensor_tensor(eq[:, :, :], lg[:, :, :], top[:, :].unsqueeze(2).to_broadcast(wide),
                                            ALU.is_equal))
                step.done(dve.tensor_tensor(eq[:, :, :], eq[:, :, :],
                                            const("first").unsqueeze(1).to_broadcast(wide), ALU.mult))
                step.done(dve.tensor_reduce(best[:, :], eq[:, :, :], AX, ALU.max))
                step.done(dve.tensor_tensor(eq[:, :, :], eq[:, :, :], best[:, :].unsqueeze(2).to_broadcast(wide),
                                            ALU.is_equal))
                assert step.n == ROUTE_STEPS
                dve.wait_ge(rt_sig, b + 1)
                dve.tensor_tensor(sc_tok[:, :, :], eq[:, :, :], sig[:, :].unsqueeze(2).to_broadcast(wide),
                                  ALU.mult).then_inc(sc_link, 1)
                dve.wait_ge(sc_link, b * 2 + 1)
                dve.tensor_copy(sc_hi, sc_tok[:, :, :]).then_inc(sc_link, 1)
                dve.wait_ge(sc_link, b * 2 + 2)
                dve.tensor_copy(sc_parts[:, :, 0:E1], sc_hi)
                dve.tensor_tensor(sc_parts[:, :, E1:2 * E1], sc_tok[:, :, :], sc_hi, ALU.subtract).then_inc(rt_out, 1)

                def selector(e, i):
                    dve.tensor_copy(sel1[i], const("expert")[0:2 * E1, ds(e, 1)].to_broadcast([2 * E1, P])
                                    ).then_inc(y_sel, 1)

                selector(0, 0)
                selector(1, 1)
                dve.wait_ge(rt_ps, b + 1)
                dve.memset(zero_row, 0.0)
                dve.tensor_copy(scT[:, :], banks(4, rows=2 * E1)).then_inc(rt_T, 1)

                def product(y, i):
                    dve.wait_ge(y_up, 1 + y + 1)
                    dve.wait_ge(y_silu, 1 + y + 1)
                    dve.tensor_tensor(ac1[i], banks(4), sg1[i], ALU.mult).then_inc(y_act, 1)

                def scale_input(e, i):
                    dve.wait_ge(y_sc, b * E1 + e + 1)
                    dve.tensor_tensor(xs1[i], hT[:, 1:T + 1], banks(0), ALU.mult).then_inc(y_xs, 1)

                def routed(j, last=False):
                    for i in range(2):
                        e = j * 2 + i
                        if not (last and i == 1):
                            scale_input(e + 1, 1 - i)
                        if not last:
                            selector(e + 2, i)
                        product(b * UNITS1 + e, i)

                scale_input(0, 0)
                with dve.Fori(0, E1 // 2 - 1) as j:
                    routed(j)
                routed(E1 // 2 - 1, last=True)
                for k in range(SF // F1):
                    product(b * UNITS1 + E1 + k, k % 2)
                dve.wait_ge(y_dn, 1 + (b + 1) * UNITS1)
                residual(b, 3, tiles(banks(6)), mod[:, 1, 5 * P:6 * P])

            dve.memset(ones_row[:, :], 1.0)
            dve.memset(eps_col[:, 0:1], EPS_LN)
            dve.memset(eps_col[:, 1:2], EPS_MASK)
            dve.memset(V1[0][:, :, :, HD:P], 1.0)
            dve.memset(V1[1][:, :, :, HD:P], 1.0)
            dve.memset(rp[:, :, :, :], 0.0)
            dve.memset(mrow1[:, :, :], -3e38).then_inc(s_prep, 1)
            dve.wait_ge(s_const, 18 * 16)
            dve.tensor_copy(ident_b[:, :], ident)
            dve.tensor_scalar(ones_fr[:, :], consts[0:1, 0:P], 0.0, 1.0, ALU.mult, ALU.add)
            dve.tensor_copy(spread[:, :], key_rows[:, 0, :])
            for h in range(2):
                dve.tensor_copy(KB[h][HD:HD + NC, :], key_rows[HD:HD + NC, 1, :])
            dve.tensor_copy(neg_b[:, :], const("neg")).then_inc(s_prep, 1)
            dve.tensor_scalar(slot_aff[:, 0:2, :], slot_aff[:, 0:2, :], scale_b[:, 0:1], None,
                              ALU.mult).then_inc(s_prep, 1)
            dve.wait_ge(s_prep, 3)
            layernorm(x, xn[:, :, :], slot_aff[:, 0, :], slot_aff[:, 1, :], 0)
            evacuate(seT[:, :], 0)
            with dve.Fori(0, NB) as b:
                m = 1 + b * LN_CALLS
                r = 1 + b * TR_CALLS
                modulation(b)
                dve.wait_ge(s_x, (b + 1) * 16)
                layernorm(x, xn[:, :, :], mod[:, 0, P:2 * P], mod[:, 0, 0:P], m)
                evacuate(hT[:, 1:T + 1], r)
                convolution(b)
                attention(0, b)
                layernorm(x, xn[:, :, :], mod[:, 0, 4 * P:5 * P], mod[:, 0, 3 * P:4 * P], m + 1)
                dve.memset(xfa[:, :, P:P + 1], 1.0)
                dve.memset(eo[:, :, P:P + 1], 1.0)
                layernorm(xn, xfa[:, :, 0:P], norm_aff[:, 0, :], norm_aff[:, 1, :], m + 2)
                dve.wait_ge(se_high, b + 1)
                dve.tensor_tensor(se_parts[1][:, :], seT[:, :], se_parts[0][:, :], ALU.subtract)
                dve.wait_ge(tr_ps, r + 2)
                dve.tensor_copy(xf_parts[0][:, :], banks(0)).then_inc(xf_high, 1)
                dve.wait_ge(xf_high, b + 1)
                dve.tensor_tensor(xf_parts[1][:, :], banks(0), xf_parts[0][:, :], ALU.subtract).then_inc(tr_out, 1)
                mixture(b)
                for h in range(2):
                    row_under_k(h, 0, BANK, 1.0)
                    row_under_k(h, BANK, T, 1.0)
                layernorm(x, xn[:, :, :], mod[:, 1, P:2 * P], mod[:, 1, 0:P], m + 3)
                evacuate(hT[:, 1:T + 1], r + 3)
                attention(1, b)
                layernorm(x, xn[:, :, :], mod[:, 1, 4 * P:5 * P], mod[:, 1, 3 * P:4 * P], m + 4)
                evacuate(hT[:, 1:T + 1], r + 4)
                experts(b)

        @block.gpsimd
        def _(pool):
            with pool.Fori(0, NB) as b:
                with pool.Fori(0, GROUPS) as g:
                    n = b * GROUPS + g
                    s = S[0]
                    pool.wait_ge(s["k_hi"], 1 + n + 1)
                    pool.wait_ge(s["k_lo"], 1 + n + 1)
                    pool.wait_ge(s_full, 1 + n * GH)
                    pool.sem_inc(s_held, 1)
                    pool.tensor_copy(KA[0][:, :], KA[1][:, :])
                    pool.tensor_copy(KB[0][0:HD, :], KB[1][0:HD, :]).then_inc(k_copy, 1)
                    pool.wait_ge(s["v_out"], 1 + n + 1)
                    pool.wait_ge(s["u_full"], 1 + n * GH)
                    pool.sem_inc(s_held, 1)
                    pool.tensor_copy(V0[0][:, :, :], V0[1][:, :, :]).then_inc(v_copy, 1)
                with pool.Fori(0, PAIRS // 2) as g:
                    for i in range(2):
                        n = b * PAIRS + g * 2 + i
                        pool.wait_ge(S[1]["v_out"], 1 + n + 1)
                        pool.wait_ge(S[1]["u_full"], 1 + 2 * n)
                        for t in reversed(range(NT - 2)):
                            after = V1[i][:, t + 2, :, :] if t == NT - 3 else Vlater[:, t + 1, :, :]
                            ins = pool.tensor_tensor(Vlater[:, t, :, :], after, V1[i][:, t + 1, :, :], ALU.add)
                            if t:
                                ins.then_inc(xw_ones, 1)
                                pool.wait_ge(xw_ones, n * (NT - 3) + NT - 2 - t)
                        ins.then_inc(later, 1)


def const_array():
    import numpy as np
    c = np.zeros((P, CONST_TOTAL), np.float32)

    def put(name, a):
        c[:, CONST_AT[name]:CONST_AT[name] + CONST_COLS[name]] = a

    p = np.arange(P)[:, None]
    q = np.arange(P)[None, :]
    put("ident", p == q)
    put("neg", np.where(q > p, -1e30, 0.0))
    put("mask", p > q)
    put("expert", (p % E1 == np.arange(E1)[None, :]) & (p < 2 * E1))
    put("first", np.broadcast_to(E1 - np.arange(E1)[None, :], (P, E1)))
    rows = np.full((P, NT), EPS_MASK / QSCALE)
    rows[P - 1, NT - 1] = -3e38
    put("eps_row", rows)
    a = np.arange(4)[None, :, None]
    col = np.arange(32)[None, None, :]
    put("chunk", (col == 2 * a + (np.arange(P) // CHUNK)[:, None, None]).reshape(P, 4 * 32))
    k = np.arange(T)[None, :]
    r = p % CQ
    spread = ((p % 32 < 2 * CQ) & (4 * (r // 2) + 2 * (p // 32 % 2) + r % 2 == k // CHUNK)).astype(np.float32)
    own_chunk = ((p - HD) == k // CHUNK).astype(np.float32)
    return c, np.stack([spread, own_chunk], 1)


def host_arrays(inp):
    import numpy as np
    g = lambda n: np.asarray(inp[n])
    c, key_rows = const_array()
    a = {"consts": c, "key_rows": key_rows, "hidden": g("L0_attn_hidden_states")}
    a["c"] = np.stack([g("L0_c"), g("L1_c")], -1)
    a["wmod"] = np.stack([g("L0_wmod"), g("L1_wmod")], 1)
    a["wq0"] = g("L0_attn_w_q").T.reshape(P, HEADS, HD)
    a["wk0"] = g("L0_attn_w_k").T.reshape(P, GROUPS, HD)
    a["wv0"] = g("L0_attn_w_v").T
    a["wo0"] = g("L0_attn_w_o").T.reshape(PAIRS, P, P).transpose(1, 0, 2)
    a["kgen_w"] = g("L0_attn_w_kgen").T
    a["kgen_b"] = g("L0_attn_b_kgen")
    a["conv_w"] = g("L0_attn_w_conv")[:, 0, :]
    a["conv_b"] = g("L0_attn_b_conv")[:, None]
    for n in ("norm_g", "norm_b", "slot_g", "slot_b", "scale"):
        a[n] = g(f"L0_ffn_{n}")
    a["slots"] = g("L0_ffn_slot_embeds").reshape(NT, P, P).transpose(1, 0, 2)
    for n in ("Wg", "Wu", "Wd", "bd"):
        a[n] = g(f"L0_ffn_{n}")
    a["bgu"] = np.stack([g("L0_ffn_bg").reshape(E0, 2, P), g("L0_ffn_bu").reshape(E0, 2, P)], 1).transpose(0, 3, 1, 2)
    a["wq1"] = g("L1_attn_W_query").transpose(1, 0, 2)
    a["wk1"] = g("L1_attn_W_key").transpose(1, 0, 2)
    a["wv1"] = g("L1_attn_W_values").transpose(1, 0, 2).reshape(P, HEADS * HD)
    a["wo1"] = g("L1_attn_W_output").reshape(PAIRS, P, P).transpose(1, 0, 2)
    a["bq1"] = g("L1_attn_Bias_query").T
    a["bk1"] = g("L1_attn_Bias_key").T
    a["bv1"] = g("L1_attn_Bias_values").reshape(1, HEADS * HD)
    a["bo1"] = g("L1_attn_Bias_output")[None]
    a["router"] = g("L1_ffn_router_w").T
    a["gate_up"] = g("L1_ffn_gate_up_proj")
    a["down"] = g("L1_ffn_down_proj")
    a["wsh"] = np.concatenate([g("L1_ffn_shared_gate_w").T, g("L1_ffn_shared_up_w").T,
                               g("L1_ffn_shared_down_w").T.reshape(SF // P, P, P).transpose(1, 0, 2).reshape(P, SF)], 1)
    return {n: np.ascontiguousarray(v) for n, v in a.items()}


def kernel(**inputs):
    import concourse.bacc as _bacc
    from concourse.bass_utils import run_bass_kernel_spmd as _run

    nc = _bacc.Bacc("TRN2", target_bir_lowering=False, num_devices=1)
    arrays = {f"in_{n}": a for n, a in host_arrays(inputs).items()}
    A = {n[3:]: nc.dram_tensor(n, a.shape, mybir.dt.from_np(a.dtype), kind="ExternalInput").ap()
         for n, a in arrays.items()}
    out = nc.dram_tensor("out_0", (NB, T, P), F32, kind="ExternalOutput").ap()
    layer_program(nc, A, out)
    r = _run(nc, [arrays], core_ids=[0])
    return r.results[0]["out_0"]
```
